# Optimizing a Trainium2 kernel written in Bass

```python
import numpy as np
import jax
import jax.numpy as jnp

def _softmax(x, axis=-1):
    return jax.nn.softmax(x, axis=axis)

def _gelu(x):
    return jax.nn.gelu(x, approximate=True)

def _silu(x):
    return jax.nn.silu(x)

def _sigmoid(x):
    return jax.nn.sigmoid(x)

def _layernorm(x, axis=-1, eps=1e-05):
    m = jnp.mean(x, axis=axis, keepdims=True)
    v = jnp.var(x, axis=axis, keepdims=True)
    return (x - m) / jnp.sqrt(v + eps)

def _scatter_add(tgt, idx, src, axis=0):
    return tgt.at[idx].add(src)

def _segment_sum(src, seg, n):
    return jax.ops.segment_sum(src, seg, n)
kernel_name = 'mk_audio_tower_d2_tok_audfeat768_r4_bfa199'

def setup_inputs(seed: int=0):
    np.random.seed(seed)
    _w = jnp.asarray

    def _rec_inputs():
        import jax
        import jax.numpy as jnp
        _rk = jax.random.key(seed)
        x = -4.65018e-05 + 0.999886 * jax.random.normal(jax.random.fold_in(_rk, 1), (16, 256, 192), jnp.float32)
        return x
    x = _rec_inputs()

    def _L0_tok_setup():
        import jax, jax.numpy as jnp
        import numpy as np
        B, N, DIM = (8, 2048, 192)
        DIM_OUT, HEADS, Q_STRIDE, WINDOW = (192, 12, 2, 64)
        HEAD_DIM = DIM_OUT // HEADS
        key = jax.random.key(seed)
        k1, k2, k3, k4, k5 = jax.random.split(key, 5)
        s_in = 1.0 / np.sqrt(DIM)
        s_out = 1.0 / np.sqrt(DIM_OUT)
        return {'x': jax.random.normal(k1, (B, N, DIM), jnp.float32), 'Wqkv': jax.random.normal(k2, (DIM, 3 * DIM_OUT), jnp.float32) * s_in, 'bqkv': jax.random.normal(k3, (3 * DIM_OUT,), jnp.float32) * 0.01, 'Wproj': jax.random.normal(k4, (DIM_OUT, DIM_OUT), jnp.float32) * s_out, 'bproj': jax.random.normal(k5, (DIM_OUT,), jnp.float32) * 0.01}
    _L0_tok_all = _L0_tok_setup()
    _L0_tok_in = {k: v for k, v in _L0_tok_all.items() if k in ('Wqkv', 'bqkv', 'Wproj', 'bproj')}
    del _L0_tok_all

    def _L0_attn_setup():
        import jax, jax.numpy as jnp
        import numpy as np
        import math
        B, N, C = (8, 1024, 192)
        H = 12
        DH = C // H
        M = 64
        LN_EPS = 1e-05

        def _phi(t, random_features):
            norm_sq = 0.5 * jnp.sum(t * t, axis=-1, keepdims=True)
            proj = jnp.einsum('bhnd,md->bhnm', t, random_features)
            return jnp.exp(proj - norm_sq) * (1.0 / math.sqrt(M))
        key = jax.random.key(seed)
        ks = jax.random.split(key, 7)
        x = jax.random.normal(ks[0], (B, N, C), dtype=jnp.float32)
        W_qkv = jax.random.normal(ks[1], (C, 3 * C), dtype=jnp.float32) * (1.0 / math.sqrt(C))
        W_proj = jax.random.normal(ks[2], (C, C), dtype=jnp.float32) * (1.0 / math.sqrt(C))
        b_proj = jnp.zeros((C,), dtype=jnp.float32)
        gamma = jnp.ones((C,), dtype=jnp.float32)
        beta = jnp.zeros((C,), dtype=jnp.float32)
        random_features = jax.random.normal(ks[3], (M, DH), dtype=jnp.float32) / math.sqrt(DH)
        return {'x': x, 'W_qkv': W_qkv, 'W_proj': W_proj, 'b_proj': b_proj, 'gamma': gamma, 'beta': beta, 'random_features': random_features}
    _L0_attn_all = _L0_attn_setup()
    _L0_attn_in = {k: v for k, v in _L0_attn_all.items() if k in ('W_qkv', 'W_proj', 'b_proj', 'gamma', 'beta', 'random_features')}
    del _L0_attn_all

    def _L0_ffn_setup():
        import jax, jax.numpy as jnp
        import numpy as np
        B, T, H, F, E = (128, 32, 192, 768, 3)
        key = jax.random.key(seed)
        ks = jax.random.split(key, 4)
        s = 0.02
        return {'x': jax.random.normal(ks[0], (B, T, H), jnp.float32), 'Wg': jax.random.normal(ks[1], (E, H), jnp.float32) * s, 'W1': jax.random.normal(ks[2], (E, H, F), jnp.float32) * s, 'b1': jnp.zeros((E, F), jnp.float32), 'W2': jax.random.normal(ks[3], (E, F, H), jnp.float32) * s, 'b2': jnp.zeros((E, H), jnp.float32)}
    _L0_ffn_all = _L0_ffn_setup()
    _L0_ffn_in = {k: v for k, v in _L0_ffn_all.items() if k in ('Wg', 'W1', 'b1', 'W2', 'b2')}
    del _L0_ffn_all

    def _L1_attn_setup():
        import jax, jax.numpy as jnp
        import numpy as np
        Bsz, L, D, N = (2, 512, 192, 16)

        def _forward(x, A, W_delta, delta_bias, W_B, W_C):
            B, Lx, Dx = x.shape
            Nx = A.shape[1]
            delta = jax.nn.softplus(x @ W_delta.T + delta_bias)
            B_sel = (x @ W_B.T).reshape(B, Lx, Dx, Nx)
            C_sel = (x @ W_C.T).reshape(B, Lx, Dx, Nx)
            dA = delta[..., None] * A
            A_bar = jnp.exp(dA)
            B_bar = (A_bar - 1.0) / dA * delta[..., None] * B_sel
            Bx = B_bar * x[..., None]

            def step(h, inp):
                a_t, bx_t, c_t = inp
                h = a_t * h + bx_t
                y_t = jnp.sum(h * c_t, axis=-1)
                return (h, y_t)
            h0 = jnp.zeros((B, Dx, Nx), dtype=x.dtype)
            scan_in = (jnp.moveaxis(A_bar, 1, 0), jnp.moveaxis(Bx, 1, 0), jnp.moveaxis(C_sel, 1, 0))
            _, ys = jax.lax.scan(step, h0, scan_in)
            return jnp.moveaxis(ys, 0, 1)
        key = jax.random.key(seed)
        ks = jax.random.split(key, 6)
        x = jax.random.normal(ks[0], (Bsz, L, D), dtype=jnp.float32)
        A = -0.5 - 0.5 * jax.random.uniform(ks[1], (D, N), dtype=jnp.float32)
        s = 1.0 / np.sqrt(D).astype(np.float32)
        W_delta = jax.random.normal(ks[2], (D, D), dtype=jnp.float32) * s
        dt = jax.random.uniform(ks[3], (D,), dtype=jnp.float32) * 0.099 + 0.001
        delta_bias = jnp.log(jnp.expm1(dt))
        W_B = jax.random.normal(ks[4], (D * N, D), dtype=jnp.float32) * s
        W_C = jax.random.normal(ks[5], (D * N, D), dtype=jnp.float32) * s
        return {'x': x, 'A': A, 'W_delta': W_delta, 'delta_bias': delta_bias, 'W_B': W_B, 'W_C': W_C}
    _L1_attn_all = _L1_attn_setup()
    _L1_attn_in = {k: v for k, v in _L1_attn_all.items() if k in ('A', 'W_delta', 'delta_bias', 'W_B', 'W_C')}
    del _L1_attn_all

    def _L1_ffn_setup():
        import jax, jax.numpy as jnp
        import numpy as np
        HIDDEN = 192
        INNER = 128
        EPS = 1e-05
        key = jax.random.key(seed)
        ks = jax.random.split(key, 6)
        B, S = (8, 1024)
        x = jax.random.normal(ks[0], (B, S, HIDDEN), dtype=jnp.float32)
        W1 = jax.random.normal(ks[1], (INNER, HIDDEN), dtype=jnp.float32) * 0.02
        b1 = jnp.zeros((INNER,), dtype=jnp.float32)
        W2 = jax.random.normal(ks[2], (HIDDEN, INNER), dtype=jnp.float32) * 0.02
        b2 = jnp.zeros((HIDDEN,), dtype=jnp.float32)
        bound = 1.0 / np.sqrt(HIDDEN)
        Wo = jax.random.uniform(ks[3], (HIDDEN, HIDDEN), minval=-bound, maxval=bound, dtype=jnp.float32)
        bo = jax.random.uniform(ks[4], (HIDDEN,), minval=-bound, maxval=bound, dtype=jnp.float32)
        gamma = jnp.ones((HIDDEN,), dtype=jnp.float32)
        beta = jnp.zeros((HIDDEN,), dtype=jnp.float32)
        return {'x': x, 'W1': W1, 'b1': b1, 'W2': W2, 'b2': b2, 'Wo': Wo, 'bo': bo, 'gamma': gamma, 'beta': beta}
    _L1_ffn_all = _L1_ffn_setup()
    _L1_ffn_in = {k: v for k, v in _L1_ffn_all.items() if k in ('W1', 'b1', 'W2', 'b2', 'Wo', 'bo', 'gamma', 'beta')}
    del _L1_ffn_all
    return {'x': x, 'L0_tok_Wqkv': _L0_tok_in['Wqkv'], 'L0_tok_bqkv': _L0_tok_in['bqkv'], 'L0_tok_Wproj': _L0_tok_in['Wproj'], 'L0_tok_bproj': _L0_tok_in['bproj'], 'L0_attn_W_qkv': _L0_attn_in['W_qkv'], 'L0_attn_W_proj': _L0_attn_in['W_proj'], 'L0_attn_b_proj': _L0_attn_in['b_proj'], 'L0_attn_gamma': _L0_attn_in['gamma'], 'L0_attn_beta': _L0_attn_in['beta'], 'L0_attn_random_features': _L0_attn_in['random_features'], 'L0_ffn_Wg': _L0_ffn_in['Wg'], 'L0_ffn_W1': _L0_ffn_in['W1'], 'L0_ffn_b1': _L0_ffn_in['b1'], 'L0_ffn_W2': _L0_ffn_in['W2'], 'L0_ffn_b2': _L0_ffn_in['b2'], 'L1_attn_A': _L1_attn_in['A'], 'L1_attn_W_delta': _L1_attn_in['W_delta'], 'L1_attn_delta_bias': _L1_attn_in['delta_bias'], 'L1_attn_W_B': _L1_attn_in['W_B'], 'L1_attn_W_C': _L1_attn_in['W_C'], 'L1_ffn_W1': _L1_ffn_in['W1'], 'L1_ffn_b1': _L1_ffn_in['b1'], 'L1_ffn_W2': _L1_ffn_in['W2'], 'L1_ffn_b2': _L1_ffn_in['b2'], 'L1_ffn_Wo': _L1_ffn_in['Wo'], 'L1_ffn_bo': _L1_ffn_in['bo'], 'L1_ffn_gamma': _L1_ffn_in['gamma'], 'L1_ffn_beta': _L1_ffn_in['beta']}

def reference(x, L0_tok_Wqkv, L0_tok_bqkv, L0_tok_Wproj, L0_tok_bproj, L0_attn_W_qkv, L0_attn_W_proj, L0_attn_b_proj, L0_attn_gamma, L0_attn_beta, L0_attn_random_features, L0_ffn_Wg, L0_ffn_W1, L0_ffn_b1, L0_ffn_W2, L0_ffn_b2, L1_attn_A, L1_attn_W_delta, L1_attn_delta_bias, L1_attn_W_B, L1_attn_W_C, L1_ffn_W1, L1_ffn_b1, L1_ffn_W2, L1_ffn_b2, L1_ffn_Wo, L1_ffn_bo, L1_ffn_gamma, L1_ffn_beta):
    import jax
    import jax.numpy as jnp

    def _L0_tok_ref(x, Wqkv, bqkv, Wproj, bproj):
        import jax, jax.numpy as jnp
        import numpy as np
        B, N, DIM = (8, 2048, 192)
        DIM_OUT, HEADS, Q_STRIDE, WINDOW = (192, 12, 2, 64)
        HEAD_DIM = DIM_OUT // HEADS
        b, n, _ = x.shape
        nw = n // (Q_STRIDE * WINDOW)
        n1 = n // nw
        qkv = x @ Wqkv + bqkv
        qkv = qkv.reshape(b, n1, nw, 3, HEADS, HEAD_DIM).transpose(3, 0, 4, 2, 1, 5)
        q, k, v = (qkv[0], qkv[1], qkv[2])
        q = jnp.max(q.reshape(b, HEADS, nw, Q_STRIDE, n1 // Q_STRIDE, HEAD_DIM), axis=3)
        scale = HEAD_DIM ** (-0.5)
        attn = jax.nn.softmax(jnp.einsum('bhwqd,bhwkd->bhwqk', q * scale, k), axis=-1)
        o = jnp.einsum('bhwqk,bhwkd->bhwqd', attn, v)
        nq = o.shape[3]
        o = o.transpose(0, 2, 3, 1, 4).reshape(b, nw * nq, DIM_OUT)
        return o @ Wproj + bproj

    def _L0_attn_ref(x, W_qkv, W_proj, b_proj, gamma, beta, random_features):
        import jax, jax.numpy as jnp
        import numpy as np
        import math
        B, N, C = (8, 1024, 192)
        H = 12
        DH = C // H
        M = 64
        LN_EPS = 1e-05

        def _phi(t, random_features):
            norm_sq = 0.5 * jnp.sum(t * t, axis=-1, keepdims=True)
            proj = jnp.einsum('bhnd,md->bhnm', t, random_features)
            return jnp.exp(proj - norm_sq) * (1.0 / math.sqrt(M))
        b, n, c = x.shape
        qkv = (x @ W_qkv).reshape(b, n, 3, H, DH)
        qkv = jnp.transpose(qkv, (2, 0, 3, 1, 4))
        q, k, v = (qkv[0], qkv[1], qkv[2])
        q_p = _phi(q, random_features)
        k_p = _phi(k, random_features)
        kv = jnp.einsum('bhnm,bhnd->bhmd', k_p, v)
        out = jnp.einsum('bhnm,bhmd->bhnd', q_p, kv)
        k_sum = jnp.sum(k_p, axis=2)
        normalizer = jnp.einsum('bhnm,bhm->bhn', q_p, k_sum)[..., None]
        out = out / (normalizer + 1e-06)
        x_attn = jnp.transpose(out, (0, 2, 1, 3)).reshape(b, n, c)
        x_attn = x_attn @ W_proj + b_proj
        y = x + x_attn
        mu = jnp.mean(y, axis=-1, keepdims=True)
        var = jnp.mean(jnp.square(y - mu), axis=-1, keepdims=True)
        return (y - mu) * jax.lax.rsqrt(var + LN_EPS) * gamma + beta

    def _L0_ffn_ref(x, Wg, W1, b1, W2, b2):
        import jax, jax.numpy as jnp
        import numpy as np
        B, T, H, F, E = (128, 32, 192, 768, 3)
        scores = jax.nn.softmax(jnp.mean(x, axis=1) @ Wg.T, axis=-1)
        _, idx = jax.lax.top_k(scores, 1)
        sel = idx[:, 0]
        h = jax.nn.gelu(jnp.einsum('bth,ehf->betf', x, W1) + b1[None, :, None, :], approximate=False)
        y = jnp.einsum('betf,efh->beth', h, W2) + b2[None, :, None, :]
        w = scores * jax.nn.one_hot(sel, E, dtype=scores.dtype)
        out = jnp.einsum('beth,be->bth', y, w)
        return out

    def _L1_attn_ref(x, A, W_delta, delta_bias, W_B, W_C):
        import jax, jax.numpy as jnp
        import numpy as np
        Bsz, L, D, N = (2, 512, 192, 16)

        def _forward(x, A, W_delta, delta_bias, W_B, W_C):
            B, Lx, Dx = x.shape
            Nx = A.shape[1]
            delta = jax.nn.softplus(x @ W_delta.T + delta_bias)
            B_sel = (x @ W_B.T).reshape(B, Lx, Dx, Nx)
            C_sel = (x @ W_C.T).reshape(B, Lx, Dx, Nx)
            dA = delta[..., None] * A
            A_bar = jnp.exp(dA)
            B_bar = (A_bar - 1.0) / dA * delta[..., None] * B_sel
            Bx = B_bar * x[..., None]

            def step(h, inp):
                a_t, bx_t, c_t = inp
                h = a_t * h + bx_t
                y_t = jnp.sum(h * c_t, axis=-1)
                return (h, y_t)
            h0 = jnp.zeros((B, Dx, Nx), dtype=x.dtype)
            scan_in = (jnp.moveaxis(A_bar, 1, 0), jnp.moveaxis(Bx, 1, 0), jnp.moveaxis(C_sel, 1, 0))
            _, ys = jax.lax.scan(step, h0, scan_in)
            return jnp.moveaxis(ys, 0, 1)
        return _forward(x, A, W_delta, delta_bias, W_B, W_C)

    def _L1_ffn_ref(x, W1, b1, W2, b2, Wo, bo, gamma, beta):
        import jax, jax.numpy as jnp
        import numpy as np
        HIDDEN = 192
        INNER = 128
        EPS = 1e-05
        h = jax.nn.relu(jnp.einsum('bsd,id->bsi', x, W1) + b1)
        pred = jnp.einsum('bsi,di->bsd', h, W2) + b2
        out = jnp.einsum('bsd,ed->bse', pred, Wo) + bo
        mu = jnp.mean(out, axis=-1, keepdims=True)
        var = jnp.mean(jnp.square(out - mu), axis=-1, keepdims=True)
        out = (out - mu) * jax.lax.rsqrt(var + EPS) * gamma + beta
        return out
    h = _L0_tok_ref(x, L0_tok_Wqkv, L0_tok_bqkv, L0_tok_Wproj, L0_tok_bproj)
    h = h + _L0_attn_ref(_layernorm(h, axis=-1), L0_attn_W_qkv, L0_attn_W_proj, L0_attn_b_proj, L0_attn_gamma, L0_attn_beta, L0_attn_random_features)
    h = h + _L0_ffn_ref(_layernorm(h, axis=-1), L0_ffn_Wg, L0_ffn_W1, L0_ffn_b1, L0_ffn_W2, L0_ffn_b2)
    h = h + _L1_attn_ref(_layernorm(h, axis=-1), L1_attn_A, L1_attn_W_delta, L1_attn_delta_bias, L1_attn_W_B, L1_attn_W_C)
    h = h + _L1_ffn_ref(_layernorm(h, axis=-1), L1_ffn_W1, L1_ffn_b1, L1_ffn_W2, L1_ffn_b2, L1_ffn_Wo, L1_ffn_bo, L1_ffn_gamma, L1_ffn_beta)
    return h

_drawn_inputs = setup_inputs


def setup_inputs(seed=0):
    import zlib

    import numpy as np

    out = dict(_drawn_inputs(seed))
    spreads = {'L0_attn_b_proj': (0.0, 0.1),
     'L0_attn_gamma': (1.0, 0.2),
     'L0_attn_beta': (0.0, 0.1),
     'L0_ffn_b1': (0.0, 0.475),
     'L0_ffn_b2': (0.0, 0.1),
     'L1_ffn_b1': (0.0, 0.1),
     'L1_ffn_b2': (0.0, 0.1),
     'L1_ffn_gamma': (1.0, 0.2),
     'L1_ffn_beta': (0.0, 0.1)}
    factors = {}
    for name, (base, spread) in spreads.items():
        noise = np.random.default_rng([zlib.crc32(name.encode()), seed]).standard_normal(out[name].shape)
        drawn = base * np.exp(spread * noise) if base else spread * noise
        out[name] = jnp.asarray(drawn.astype(out[name].dtype))
    for name, factor in factors.items():
        out[name] = (out[name] * factor).astype(out[name].dtype)
    return out
```

```python
from contextlib import ExitStack

import concourse.bass as bass
from concourse import mybir

fp32 = mybir.dt.float32
fp16 = mybir.dt.float16
i32 = mybir.dt.int32
ALU = mybir.AluOpType
ACT = mybir.ActivationFunctionType
AX = mybir.AxisListType

NB, NRAW, C = 16, 256, 192
P = 128
CR = C - P
W, NQ = 2, 64
T = W * NQ
H, D = 12, 16
HP = H // 2
M = 64
E, F = 3, 768
FT = F // P
N = 16
I = 128
GB = 4
G = NB // GB
GT = GB * T
N1, N2 = N, N // 2
NT = N1 + N2
EPS = 1e-5
WS = 32.0
ES = 64.0
LNS = 6


class Signal:

    def __init__(self, sem, per):
        self.sem, self.per = sem, per


def passes(e):
    return range(G)


def wait(e, signal, it, k):
    assert 1 <= k <= signal.per
    e.wait_ge(signal.sem, it * signal.per + k)


def again(e, signal, it, k):
    assert 1 <= k <= signal.per
    if it > 0:
        e.wait_ge(signal.sem, (it - 1) * signal.per + k)


def tower(nc, x, Wqkv, bqkv, Wproj, bproj, aWqkv, aWproj, abproj, agamma, abeta, rfeat, Wg, W1, b1, W2, b2,
          sA, sWd, sdb, sWB, sWC, fW1, fb1, fW2, fb2, fWo, fbo, fgamma, fbeta, out):
    ctx = ExitStack()
    with ctx:
        def sb(name, shape, dt=fp32):
            return ctx.enter_context(nc.sbuf_tensor(name, shape, dt))

        def once(name):
            return ctx.enter_context(nc.semaphore(name))

        def signal(name, per, engine):
            return Signal(ctx.enter_context(nc.semaphore(name)), per)

        ident = sb("ident", [P, P])
        ones = sb("ones", [P, P])
        headmask = sb("headmask", [P, 8])
        negmask = sb("negmask", [P, 8])
        pairmask = sb("pairmask", [P, 2, D + 1])
        rf_rep = sb("rf_rep", [P, M])
        rf_blk = sb("rf_blk", [P, 8, M])
        norm_blk = sb("norm_blk", [P, 8, M])
        tw_a, tw_r = sb("tw_a", [P, 3 * C]), sb("tw_r", [CR, 3 * C])
        tbq_a, tbq_r = sb("tbq_a", [P, 2]), sb("tbq_r", [CR, 2])
        tbv = sb("tbv", [HP * D, 2])
        tbv_b = sb("tbv_b", [HP * D, 2, P])
        tproj = sb("tproj", [HP * D, 2, C])
        tbias = sb("tbias", [P, C])
        pw_a, pw_r = sb("pw_a", [P, 3 * C]), sb("pw_r", [CR, 3 * C])
        pproj_a, pproj_r = sb("pproj_a", [P, C]), sb("pproj_r", [CR, C])
        ROWS = 7
        rows = sb("rows", [1, ROWS, C])
        bc = sb("bc", [P, ROWS, C])
        R_TPROJ, R_AB, R_AG, R_ABETA, R_FBO, R_FG, R_FBETA = range(ROWS)
        wg_a, wg_r = sb("wg_a", [P, E]), sb("wg_r", [CR, E])
        w1_h, w1_l = sb("w1_h", [P, E * F], fp16), sb("w1_l", [P, E * F], fp16)
        w1_d = sb("w1_d", [P, E * F], fp16)
        b1_hl = sb("b1_hl", [CR, E * F], fp16)
        b2_row = sb("b2_row", [1, E * C])
        w2 = sb("w2", [P, E, FT, C])
        NS = 2 * NT + 2
        sw_h, sw_l = sb("sw_h", [P, NS, P], fp16), sb("sw_l", [P, NS, P], fp16)
        sw_d = sb("sw_d", [P, NS, P], fp16)
        a_all, ra_all = sb("a_all", [P, NT]), sb("ra_all", [P, NT])
        dbias = sb("dbias", [P, 2])
        CH = 8
        fold = sb("fold", [P, CR])
        fw1_n = sb("fw1_n", [P, C])
        fw1_a, fw1_r = sb("fw1_a", [P, I]), sb("fw1_r", [CR, I])
        fw2_a, fw2_r = sb("fw2_a", [P, I]), sb("fw2_r", [CR, I])
        fwo_a, fwo_r = sb("fwo_a", [P, C]), sb("fwo_r", [CR, C])
        fwoT_a, fwoT_r = sb("fwoT_a", [P, C]), sb("fwoT_r", [CR, C])
        fw21 = sb("fw21", [I, C])
        fb1_c, fb2_a, fb2_r = sb("fb1_c", [I, 1]), sb("fb2_a", [P, 1]), sb("fb2_r", [CR, 1])
        fb2_ab, fb2_rb = sb("fb2_ab", [P, P]), sb("fb2_rb", [CR, P])

        h = sb("h", [P, GB, C])
        xn = sb("xn", [P, GB, C + CR])
        yres = sb("yres", [P, GB, C])
        outb = sb("outb", [P, GB, C])
        ln_st, ln_mv = sb("ln_st", [P, GB, 6]), sb("ln_mv", [P, GB, 2])
        ln_ve, ln_rs, minus_half = sb("ln_ve", [P, GB]), sb("ln_rs", [P, GB]), sb("minus_half", [P, GB])
        gx_a, gx_r = sb("gx_a", [P, GT]), sb("gx_r", [CR, GT])
        xa_h, xa_l = sb("xa_h", [P, GT], fp16), sb("xa_l", [P, GT], fp16)
        xd_h, xe_l = sb("xd_h", [P, GT], fp16), sb("xe_l", [CR, GT], fp16)
        t_v = sb("t_v", [P, 2, W, HP, 2 * D + 1])
        p_v = sb("p_v", [P, GB, H, D + 1])
        ones16 = sb("ones16", [CR, P], fp16)

        AR = 13824
        arena = sb("arena", [P, AR])

        def carve(layout):
            at, views = 0, []
            for rows_, *dims in layout:
                n = 1
                for d in dims:
                    n *= d
                assert at + n <= AR
                v = arena[0:rows_, at:at + n]
                if len(dims) == 2:
                    v = v.rearrange("p (a b) -> p a b", b=dims[1])
                elif len(dims) == 3:
                    v = v.rearrange("p (a b c) -> p a b c", b=dims[1], c=dims[2])
                views.append(v)
                at += n
            return views

        CH = 8
        raw, w1_sa, w1_sd, b1_row = carve([(P, 2, CH, C + CR), (P, E, F), (P, E, F), (CR, E * F)])
        (t_x, t_xa, t_xr, t_qa, t_qr, t_ka, t_kr, t_qx, t_qxr, t_qm, t_qmr, t_mx, t_p, t_e, t_pt, t_rd, t_o,
         t_ot) = carve([(P, 2, W, C), (P, W * P), (CR, W * P), (P, W, P), (CR, W, P), (P, W, P), (CR, W, P),
                        (P, W, NQ), (CR, W, NQ), (P, W, 8, NQ), (CR, W, 4, NQ), (P, W * HP), (P, W * HP, P),
                        (P, W * HP, P), (P, W * HP, P), (P, W * HP), (P, W * HP, D), (HP * D, 2, W, NQ)])
        (p_t, p_sq, p_qp, p_kp, p_kv, p_n, p_r, p_xa, p_y0) = carve([
            (P, 4, GT), (P, 4, GT), (P, HP, GT), (P, 2, H * M), (P, 2, HP, 2 * (D + 1)), (P, 2, H), (P, 2, H),
            (P, GB, C), (P, GB, C)])
        m_h, = carve([(P, 2, F)])
        AB = 3
        (s_x, s_z, s_u, s_l, s_dt, s_a, s_w, s_wx, s_h, s_p, s_ya, s_yr) = carve([
            (P, 2, GT), (P, 2, GT), (P, 2, GT), (P, 2, GT), (P, 2, GT), (P, AB, GT), (P, AB, GT), (P, AB, GT),
            (P, AB, GT), (P, AB, GT), (P, GT), (CR, GT)])
        m_ma, m_mr = sb("m_ma", [P, GB]), sb("m_mr", [CR, GB])
        m_pa, m_pr = sb("m_pa", [P, GB, E]), sb("m_pr", [CR, GB, E])
        m_l, m_ls, m_e, m_eq = (sb(f"m_{n}", [P, GB, E]) for n in ("l", "ls", "e", "eq"))
        m_mx, m_sum, m_w = sb("m_mx", [P, GB]), sb("m_sum", [P, GB]), sb("m_w", [P, GB])
        m_t = sb("m_t", [P, 2, GB])
        m_idx = sb("m_idx", [P, GB], i32)
        f_h = sb("f_h", [I, GT])

        ps = ctx.enter_context(nc.psum_tensor("ps", [P, 8, 512], fp32))

        def bank(n, rows=P, a=0, b=512):
            return ps[0:rows, n, a:b]

        d_small, d_tok, d_attn, d_moe, d_ffn = (once(n) for n in ("d_small", "d_tok", "d_attn", "d_moe", "d_ffn"))
        d_raw = [once("d_raw0"), once("d_raw1")]
        c_ident, c_ones, c_mask, c_half = (once(n) for n in ("c_ident", "c_ones", "c_mask", "c_half"))
        c_v1, c_blk, c_bzero = once("c_v1"), once("c_blk"), once("c_bzero")
        c_w1hi, c_w1lo = once("c_w1hi"), once("c_w1lo")
        c_bcast, c_bcast_used, c_ra = once("c_bcast"), once("c_bcast_used"), once("c_ra")
        c_swT, c_swhi, c_swlo, c_cols = once("c_swT"), once("c_swhi"), once("c_swlo"), once("c_cols")
        c_fT, c_fTs, c_fw, c_fws = once("c_fT"), once("c_fTs"), once("c_fw"), once("c_fws")
        d_out = once("d_out")

        ln_stats = signal("ln_stats", LNS * GB, "dve")
        ln_aggr = signal("ln_aggr", LNS * GB, "dve")
        ln_eps = signal("ln_eps", LNS, "pool")
        ln_rstd = signal("ln_rstd", LNS, "pool")
        ln_norm = signal("ln_norm", LNS * GB, "dve")
        ln_dup = signal("ln_dup", 2, "pool")
        x_in = [signal(f"x_in{n}", 16 * GB // 2, "sp") for n in range(2)]
        t_xT = signal("t_xT", GB, "pe")
        t_xTa = signal("t_xTa", GB, "act")
        t_xTr = signal("t_xTr", GB, "dve")
        t_qk = signal("t_qk", GB, "pe")
        t_vps = signal("t_vps", GB, "pe")
        t_q = signal("t_q", 2 * GB, "act")
        t_k = signal("t_k", 2 * GB, "act")
        t_vs = signal("t_vs", GB, "dve")
        t_qmax = signal("t_qmax", 2 * GB, "dve")
        t_qmask = signal("t_qmask", 2 * GB, "dve")
        t_s = signal("t_s", GB, "pe")
        t_max = signal("t_max", GB, "dve")
        t_sub = signal("t_sub", GB, "dve")
        t_exp = signal("t_exp", GB, "act")
        t_pT = signal("t_pT", 3 * GB, "pe")
        t_pTa = signal("t_pTa", 2 * GB, "act")
        t_pTd = signal("t_pTd", GB, "dve")
        t_ops = signal("t_ops", GB, "pe")
        t_rden = signal("t_rden", GB, "dve")
        t_on = signal("t_on", 2 * GB, "dve")
        t_oT = signal("t_oT", GB, "pe")
        t_oTs = signal("t_oTs", GB, "dve")
        t_y = signal("t_y", GB, "pe")
        t_h = signal("t_h", GB, "dve")
        gxT = signal("gxT", 4, "pe")
        gxTa = signal("gxTa", 2, "act")
        gxTr = signal("gxTr", 2, "dve")
        xhi = signal("xhi", 4, "act")
        xlo = signal("xlo", 4, "dve")
        p_qk = signal("p_qk", 4, "pe")
        p_vps = signal("p_vps", 2, "pe")
        p_sqd = signal("p_sqd", 4, "act")
        p_cp = signal("p_cp", 4, "dve")
        p_vs = signal("p_vs", 2, "dve")
        p_fq = signal("p_fq", HP, "pe")
        p_eq = signal("p_eq", HP, "act")
        p_fk = signal("p_fk", GB, "pe")
        p_ek = signal("p_ek", GB, "act")
        p_kvp = signal("p_kvp", GB, "pe")
        p_kvs = signal("p_kvs", GB, "dve")
        p_num = signal("p_num", GB, "pe")
        p_den = signal("p_den", GB, "dve")
        p_rec = signal("p_rec", GB, "dve")
        p_att = signal("p_att", GB, "dve")
        p_aT = signal("p_aT", 1, "pe")
        p_aTa = signal("p_aTa", 1, "act")
        p_aTr = signal("p_aTr", 1, "dve")
        p_pr = signal("p_pr", 2, "pe")
        p_b = signal("p_b", 2, "dve")
        p_y = signal("p_y", 2, "dve")
        p_g = signal("p_g", 1, "dve")
        p_be = signal("p_be", 1, "dve")
        p_h = signal("p_h", 1, "dve")
        m_mean = signal("m_mean", 2, "dve")
        m_prod = signal("m_prod", 2, "dve")
        m_log = signal("m_log", 1, "pe")
        m_st = signal("m_st", 9, "dve")
        m_ex = signal("m_ex", 1, "act")
        m_up = signal("m_up", GB, "pe")
        m_act = signal("m_act", 2 * GB, "act")
        m_dn = signal("m_dn", GB, "pe")
        m_res = signal("m_res", GB, "dve")
        s_xc = signal("s_xc", 2, "dve")
        s_dps = signal("s_dps", 2, "pe")
        s_zs = signal("s_zs", 2, "dve")
        s_abs = signal("s_abs", 1, "act")
        s_exp = signal("s_exp", 1, "act")
        s_ln = signal("s_ln", 1, "act")
        s_dlt = signal("s_dlt", 1, "dve")
        s_as = signal("s_as", NT, "act")
        s_ws = signal("s_ws", NT, "act")
        s_wxs = signal("s_wxs", NT, "pool")
        s_a0 = signal("s_a0", NT, "pool")
        s_bps = signal("s_bps", NT, "pe")
        s_cps = signal("s_cps", NT, "pe")
        s_bx = signal("s_bx", NT, "dve")
        s_hs = signal("s_hs", NT, "dve")
        s_pr = signal("s_pr", NT, "dve")
        s_acc = signal("s_acc", NT, "pe")
        s_yc = signal("s_yc", 2, "act")
        s_yT = signal("s_yT", 2, "pe")
        s_res = signal("s_res", 2, "dve")
        f_up = signal("f_up", 1, "pe")
        f_rl = signal("f_rl", 1, "act")
        f_dn = signal("f_dn", 2, "pe")
        f_b = signal("f_b", 2, "dve")
        f_g = signal("f_g", 1, "dve")
        f_be = signal("f_be", 1, "dve")
        f_out = signal("f_out", 1, "dve")
        o_out = signal("o_out", 16, "sp")

        CHUNKS = [(sWB, 0, 0), (sWB, 1, 8), (sWB, 2, 16), (sWC, 0, 24), (sWC, 1, 32), (sWC, 2, 40)]

        ctx.enter_context(nc.allow_non_contiguous_dma(reason="a few small weight vectors"))
        block = ctx.enter_context(nc.Block())

        @block.sync
        def _(e):
            def raw_chunk(c):
                src, part, _ = CHUNKS[c]
                if c >= 2:
                    e.wait_ge(c_swT, 4 * (c - 1))
                for p0, p1, v in raw_parts(src, part):
                    e.dma_start(raw[p0:p1, c % 2, :, 0:C], v[:, :, :]).then_inc(d_raw[c % 2], 16)
                    e.dma_start(raw[p0:p1, c % 2, :, C:C + CR], v[:, :, P:C]).then_inc(d_raw[c % 2], 16)

            def raw_parts(src, part):
                v = src.rearrange("(d n) k -> d n k", n=N)
                if part < 2:
                    return [(0, P, v[0:P, 8 * part:8 * part + 8, :])]
                u = src.rearrange("(d j s) k -> s d j k", j=N2, s=2)
                return [(0, 64, u[0, P:C, :, :]), (64, P, u[1, P:C, :, :])]

            e.dma_start(tw_a[:, :], Wqkv[0:P, :]).then_inc(d_tok, 16)
            e.dma_start(tw_r[:, :], Wqkv[P:C, :]).then_inc(d_tok, 16)
            for j in range(2):
                col = bqkv[j * C:(j + 1) * C].rearrange("(p o) -> p o", o=1)
                e.dma_start(tbq_a[:, j:j + 1], col[0:P, :]).then_inc(d_tok, 16)
                e.dma_start(tbq_r[:, j:j + 1], col[P:C, :]).then_inc(d_tok, 16)
            for j in range(HP):
                e.dma_start(tproj[D * j:D * j + D, :, :],
                            Wproj[2 * D * j:2 * D * j + 2 * D, :].rearrange("(s d) c -> d s c", s=2)).then_inc(d_tok, 16)
                e.dma_start(tbv[D * j:D * j + D, :],
                            bqkv[2 * C + 2 * D * j:2 * C + 2 * D * j + 2 * D].rearrange("(s d) -> d s", s=2)).then_inc(d_tok, 16)
            for n, v in enumerate((bproj, abproj, agamma, abeta, fbo, fgamma, fbeta)):
                e.dma_start(rows[0:1, n, :], v.rearrange("(o c) -> o c", o=1)).then_inc(d_small, 16)
            for j in range(8):
                e.dma_start(rf_rep[D * j:D * j + D, :], rfeat.rearrange("m d -> d m")).then_inc(d_small, 16)
            e.dma_start(a_all[:, 0:N1], sA[0:P, :]).then_inc(d_small, 16)
            for s in range(2):
                e.dma_start(a_all[64 * s:64 * s + 64, N1:NT],
                            sA[P:C, :].rearrange("d (j s) -> s d j", s=2)[s, :, :]).then_inc(d_small, 16)
            dcol = sdb.rearrange("(p o) -> p o", o=1)
            e.dma_start(dbias[:, 0:1], dcol[0:P, :]).then_inc(d_small, 16)
            e.dma_start(dbias[0:64, 1:2], dcol[P:C, :]).then_inc(d_small, 16)
            e.dma_start(dbias[64:P, 1:2], dcol[P:C, :]).then_inc(d_small, 16)
            raw_chunk(0)
            raw_chunk(1)
            e.dma_start(pw_a[:, :], aWqkv[0:P, :]).then_inc(d_attn, 16)
            e.dma_start(pw_r[:, :], aWqkv[P:C, :]).then_inc(d_attn, 16)
            e.dma_start(pproj_a[:, :], aWproj[0:P, :]).then_inc(d_attn, 16)
            e.dma_start(pproj_r[:, :], aWproj[P:C, :]).then_inc(d_attn, 16)
            e.dma_start(w1_sa[:, :, :], W1[:, 0:P, :].rearrange("e k f -> k e f")).then_inc(d_moe, 16)
            e.dma_start(w1_sd[0:64, :, :], W1[:, P:C, :].rearrange("e k f -> k e f")).then_inc(d_moe, 16)
            e.dma_start(w1_sd[64:P, :, :], W1[:, P:C, :].rearrange("e k f -> k e f")).then_inc(d_moe, 16)
            for r in (0, 32):
                e.dma_start(b1_row[r:r + 1, :], b1.rearrange("(o e) f -> o (e f)", o=1)).then_inc(d_moe, 16)
            for n in range(E):
                e.dma_start(w2[:, n, :, :], W2[n, :, :].rearrange("(t p) c -> p t c", p=P)).then_inc(d_moe, 16)
            e.dma_start(b2_row[:, :], b2.rearrange("(o e) c -> o (e c)", o=1)).then_inc(d_moe, 16)
            e.dma_start(wg_a[:, :], Wg[:, 0:P].rearrange("e k -> k e")).then_inc(d_moe, 16)
            e.dma_start(wg_r[:, :], Wg[:, P:C].rearrange("e k -> k e")).then_inc(d_moe, 16)
            e.dma_start(fw1_n[:, :], fW1[:, :]).then_inc(d_ffn, 16)
            e.dma_start(fw2_a[:, :], fW2[0:P, :]).then_inc(d_ffn, 16)
            e.dma_start(fw2_r[:, :], fW2[P:C, :]).then_inc(d_ffn, 16)
            e.dma_start(fwo_a[:, :], fWo[0:P, :]).then_inc(d_ffn, 16)
            e.dma_start(fwo_r[:, :], fWo[P:C, :]).then_inc(d_ffn, 16)
            e.dma_start(fb1_c[:, :], fb1.rearrange("(p o) -> p o", o=1)).then_inc(d_ffn, 16)
            e.dma_start(fb2_a[:, :], fb2.rearrange("(p o) -> p o", o=1)[0:P, :]).then_inc(d_ffn, 16)
            e.dma_start(fb2_r[:, :], fb2.rearrange("(p o) -> p o", o=1)[P:C, :]).then_inc(d_ffn, 16)
            for c in range(2, 6):
                raw_chunk(c)
            e.wait_ge(c_swT, 20)
            for p0, p1, j, v in ((0, P, 0, sWd[0:P, :]), (0, 64, 1, sWd[P:C, :]), (64, P, 1, sWd[P:C, :])):
                e.dma_start(raw[p0:p1, 0, j, 0:C], v[:, :]).then_inc(d_raw[0], 16)
                e.dma_start(raw[p0:p1, 0, j, C:C + CR], v[:, P:C]).then_inc(d_raw[0], 16)

            e.wait_ge(c_swT, NS // 2)
            e.wait_ge(c_w1lo, 3)
            e.wait_ge(c_w1hi, 4)
            for it in passes(e):
                for b in range(GB):
                    if b >= 2:
                        wait(e, t_xT, it, b - 1)
                    else:
                        again(e, t_xT, it, GB - 1 + b)
                        if b == 0:
                            again(e, s_yc, it, 2)
                            again(e, s_acc, it, NT)
                    e.dma_start(t_x[:, b % 2, :, :],
                                x[it * GB + b, :, :].rearrange("(p w) c -> p w c", w=W)).then_inc(x_in[b % 2].sem, 16)
                wait(e, f_out, it, 1)
                e.dma_start(out[it * GB:it * GB + GB, :, :].rearrange("b p c -> p b c"), outb[:, :, :]).then_inc(o_out.sem, 16)
            e.wait_ge(o_out.sem, 16 * G)

        @block.gpsimd
        def _(e):
            e.memset(ident[:, :], 0.0).then_inc(c_ident, 1)
            e.memset(ones[:, :], 1.0).then_inc(c_ones, 1)
            e.memset(ones16[:, :], 1.0).then_inc(c_ones, 1)
            e.memset(minus_half[:, :], -0.5).then_inc(c_half, 1)
            e.memset(headmask[:, :], 1.0).then_inc(c_mask, 1)
            e.memset(pairmask[:, :, :], 1.0).then_inc(c_mask, 1)
            e.memset(t_v[:, :, :, :, 2 * D:2 * D + 1], 1.0).then_inc(c_v1, 1)
            e.memset(p_v[:, :, :, D:D + 1], 1.0).then_inc(c_v1, 1)
            e.wait_ge(c_ident, 1)
            e.affine_select(out=ident[:, :], in_=ident[:, :], compare_op=ALU.not_equal, fill=1.0, base=0,
                            pattern=[[-1, P]], channel_multiplier=1).then_inc(c_ident, 1)
            e.wait_ge(c_mask, 2)
            e.affine_select(out=headmask[:, :], in_=headmask[:, :], compare_op=ALU.is_ge, fill=0.0, base=0,
                            pattern=[[-D, 8]], channel_multiplier=1).then_inc(c_mask, 1)
            e.affine_select(out=pairmask[:, :, :], in_=pairmask[:, :, :], compare_op=ALU.is_ge, fill=0.0, base=0,
                            pattern=[[-M, 2], [0, D + 1]], channel_multiplier=1).then_inc(c_mask, 1)
            e.wait_ge(c_mask, 4)
            e.affine_select(out=headmask[:, :], in_=headmask[:, :], compare_op=ALU.is_ge, fill=0.0, base=D - 1,
                            pattern=[[D, 8]], channel_multiplier=-1).then_inc(c_mask, 1)
            e.affine_select(out=pairmask[:, :, :], in_=pairmask[:, :, :], compare_op=ALU.is_ge, fill=0.0, base=M - 1,
                            pattern=[[M, 2], [0, D + 1]], channel_multiplier=-1).then_inc(c_mask, 1)

            def rstd(it, k):
                wait(e, ln_aggr, it, GB * (k + 1))
                e.tensor_scalar(ln_ve[:, :], ln_mv[:, :, 1], EPS, None, ALU.add).then_inc(ln_eps.sem, 1)
                wait(e, ln_eps, it, k + 1)
                e.tensor_tensor(ln_rs[:, :], ln_ve[:, :], minus_half[:, :], ALU.pow).then_inc(ln_rstd.sem, 1)

            def duplicate(it, k, n):
                wait(e, ln_norm, it, GB * (k + 1))
                e.tensor_copy(xn[:, :, C:C + CR], xn[:, :, P:C]).then_inc(ln_dup.sem, 1)

            for it in passes(e):
                rstd(it, 0)
                rstd(it, 1)
                rstd(it, 2)
                duplicate(it, 2, 0)
                rstd(it, 3)
                duplicate(it, 3, 1)
                for i in range(NT):
                    wait(e, s_ws, it, i + 1)
                    if i == 0:
                        wait(e, s_xc, it, 2)
                    if i >= AB:
                        wait(e, s_bx, it, i - AB + 1)
                    e.tensor_tensor(s_wx[:, i % AB, :], s_w[:, i % AB, :], s_x[:, i // N1, :], ALU.mult).then_inc(s_wxs.sem, 1)
                    e.memset(s_a[:, i % AB, :].rearrange("p (b t) -> p b t", t=T)[:, :, 0:1], 0.0).then_inc(s_a0.sem, 1)
                rstd(it, 4)
                rstd(it, 5)

        @block.scalar
        def _(e):
            act = e.activation
            e.wait_ge(d_moe, 16 * 11)
            e.wait_ge(c_bzero, 1)
            act(w1_h[:, :].rearrange("p (e f) -> p e f", e=E), w1_sa[:, :, :], ACT.Copy, scale=ES).then_inc(c_w1hi, 1)
            act(w1_d[:, :].rearrange("p (e f) -> p e f", e=E), w1_sd[:, :, :], ACT.Copy, scale=ES).then_inc(c_w1hi, 1)
            act(b1_hl[0:1, :], b1_row[0:1, :], ACT.Copy, scale=ES).then_inc(c_w1hi, 1)
            act(b1_hl[32:33, :], b1_row[32:33, :], ACT.Copy, scale=ES).then_inc(c_w1hi, 1)
            for q in range(NS // 2):
                e.wait_ge(c_swT, q + 1)
                v = bank(q % 4).rearrange("p (a b) -> p a b", b=P)
                act(sw_h[:, 2 * q:2 * q + 2, :], v[:, 0:2, :], ACT.Copy, scale=WS).then_inc(c_swhi, 1)
                act(sw_d[:, 2 * q:2 * q + 2, :], v[:, 2:4, :], ACT.Copy, scale=WS).then_inc(c_swhi, 1)

            def t_front(it, b):
                wait(e, t_xT, it, b + 1)
                if b == 0 and it == 0:
                    e.wait_ge(d_tok, 16 * (6 + 2 * HP))
                act(t_xa[:, :], bank(0, P, 0, 256), ACT.Copy).then_inc(t_xTa.sem, 1)
                wait(e, t_qk, it, b + 1)
                if b >= 1:
                    wait(e, t_qmax, it, 2 * b)
                act(t_qa[:, :, :].rearrange("p w t -> p (w t)"), bank(1, P, 0, 256), ACT.Identity,
                    bias=tbq_a[:, 0:1]).then_inc(t_q.sem, 1)
                act(t_qr[:, :, :].rearrange("p w t -> p (w t)"), bank(2, CR, 0, 256), ACT.Identity,
                    bias=tbq_r[:, 0:1]).then_inc(t_q.sem, 1)
                if b >= 1:
                    wait(e, t_s, it, b)
                act(t_ka[:, :, :].rearrange("p w t -> p (w t)"), bank(1, P, 256, 512), ACT.Identity,
                    bias=tbq_a[:, 1:2]).then_inc(t_k.sem, 1)
                act(t_kr[:, :, :].rearrange("p w t -> p (w t)"), bank(2, CR, 256, 512), ACT.Identity,
                    bias=tbq_r[:, 1:2]).then_inc(t_k.sem, 1)

            for it in passes(e):
                t_front(it, 0)
                for b in range(GB):
                    wait(e, t_sub, it, b + 1)
                    if b >= 1:
                        wait(e, t_pT, it, 3 * b)
                    act(t_e[:, :, :], t_p[:, :, :], ACT.Exp, scale=D ** -0.5).then_inc(t_exp.sem, 1)
                    if b + 1 < GB:
                        t_front(it, b + 1)
                    for j in range(2):
                        wait(e, t_pT, it, 3 * b + j + 1)
                        if b >= 1 and j == 0:
                            wait(e, t_ops, it, b)
                        act(t_pt[:, 4 * j:4 * j + 4, :].rearrange("p a b -> p (a b)"), bank(4 + j), ACT.Copy).then_inc(t_pTa.sem, 1)
                wait(e, gxT, it, 1)
                act(gx_a[:, :], bank(0), ACT.Copy).then_inc(gxTa.sem, 1)
                for j in range(4):
                    r = P if j < 2 else CR
                    wait(e, p_qk, it, j + 1)
                    act(p_sq[0:r, j, :], bank(2 + j, r), ACT.Square).then_inc(p_sqd.sem, 1)
                for j in range(HP):
                    wait(e, p_fq, it, j + 1)
                    act(p_qp[:, j, :], bank(j % 2), ACT.Exp).then_inc(p_eq.sem, 1)
                for b in range(GB):
                    wait(e, p_fk, it, b + 1)
                    if b >= 2:
                        wait(e, p_kvp, it, b - 1)
                    q = 2 + 2 * (b % 2)
                    act(p_kp[:, b % 2, :], ps[:, q:q + 2, :].rearrange("p a b -> p (a b)")[:, 0:H * M], ACT.Exp).then_inc(p_ek.sem, 1)
                wait(e, p_aT, it, 1)
                act(gx_a[:, :], bank(0), ACT.Copy).then_inc(p_aTa.sem, 1)
                wait(e, gxT, it, 2)
                act(xa_h[:, :], bank(0), ACT.Copy).then_inc(xhi.sem, 1)
                act(xd_h[:, :], bank(1), ACT.Copy).then_inc(xhi.sem, 1)
                wait(e, m_st, it, 3)
                act(m_e[:, :, :], m_ls[:, :, :], ACT.Exp).then_inc(m_ex.sem, 1)
                for b in range(GB):
                    wait(e, m_up, it, b + 1)
                    if b >= 2:
                        wait(e, m_dn, it, b - 1)
                    q = 2 + 2 * (b % 2)
                    act(m_h[:, b % 2, 0:512], bank(q), ACT.Gelu, scale=1 / ES).then_inc(m_act.sem, 1)
                    act(m_h[:, b % 2, 512:F], bank(q + 1, P, 0, F - 512), ACT.Gelu, scale=1 / ES).then_inc(m_act.sem, 1)
                wait(e, gxT, it, 3)
                act(xa_h[:, :], bank(0), ACT.Copy).then_inc(xhi.sem, 1)
                act(xd_h[:, :], bank(1), ACT.Copy).then_inc(xhi.sem, 1)
                wait(e, s_zs, it, 2)
                act(s_u[:, :, :], s_z[:, :, :], ACT.Abs).then_inc(s_abs.sem, 1)
                wait(e, s_abs, it, 1)
                act(s_l[:, :, :], s_u[:, :, :], ACT.Exp, scale=-1.0).then_inc(s_exp.sem, 1)
                wait(e, s_exp, it, 1)
                act(s_u[:, :, :], s_l[:, :, :], ACT.Ln, bias=1.0).then_inc(s_ln.sem, 1)
                wait(e, s_dlt, it, 1)
                for i in range(NT + 1):
                    if i < NT:
                        if i >= AB:
                            wait(e, s_hs, it, i - AB + 1)
                        act(s_a[:, i % AB, :], s_dt[:, i // N1, :], ACT.Exp, scale=a_all[:, i:i + 1]).then_inc(s_as.sem, 1)
                    if i >= 1:
                        wait(e, s_as, it, i)
                        if i > AB:
                            wait(e, s_wxs, it, i - AB)
                        act(s_w[:, (i - 1) % AB, :], s_a[:, (i - 1) % AB, :], ACT.Copy, bias=-1.0).then_inc(s_ws.sem, 1)
                wait(e, s_acc, it, NT)
                act(s_ya[:, :], bank(6), ACT.Copy).then_inc(s_yc.sem, 1)
                act(s_yr[:, :], bank(7, CR), ACT.Copy).then_inc(s_yc.sem, 1)
                wait(e, gxT, it, 4)
                act(gx_a[:, :], bank(0), ACT.Copy).then_inc(gxTa.sem, 1)
                wait(e, f_up, it, 1)
                act(f_h[:, :], bank(2), ACT.Relu, bias=fb1_c[:, 0:1]).then_inc(f_rl.sem, 1)

        @block.tensor
        def _(e):
            mm = nc.tensor.matmul
            tr = nc.tensor.transpose
            e.wait_ge(c_ident, 2)
            for q in range(NS // 2):
                c, j = q // 4, 2 * (q % 4)
                if q % 4 == 0:
                    e.wait_ge(d_raw[c % 2], (32, 32, 96, 64, 128, 128, 224)[c])
                if q >= 4:
                    e.wait_ge(c_swhi, 2 * (q - 3))
                    e.wait_ge(c_swlo, 2 * (q - 3))
                for s in range(2):
                    tr(bank(q % 4, P, P * s, P * s + P), raw[:, c % 2, j + s, 0:P], ident[:, :])
                for s in range(2):
                    last = tr(bank(q % 4, P, P * (2 + s), P * (3 + s)), raw[:, c % 2, j + s, P:C + CR], ident[:, :])
                last.then_inc(c_swT, 1)
            e.wait_ge(d_small, 16 * (ROWS + 8 + 3 + 3))
            e.wait_ge(d_tok, 16 * (6 + 2 * HP))
            e.wait_ge(c_ones, 2)
            e.wait_ge(c_cols, 4)
            mm(bank(4, P, 0, C), ones[0:1, :], rows[0:1, R_TPROJ, :], start=True, stop=False)
            for s in range(2):
                mm(bank(4, P, 0, C), tbv_b[:, s, :], tproj[:, s, :], start=False, stop=s == 1)
            for n in range(1, ROWS):
                if n != R_FBO:
                    last = mm(bank(4 + n // 2, P, C * (n % 2), C * (n % 2) + C), ones[0:1, :], rows[0:1, n, :], start=True, stop=True)
            last.then_inc(c_bcast, 1)
            e.wait_ge(d_ffn, 16 * 8)
            e.wait_ge(c_bcast_used, 5)
            e.wait_ge(c_swhi, NS)
            e.wait_ge(c_swlo, NS)
            tr(bank(0, P, 0, I), fw1_n[:, 0:P], ident[:, :])
            tr(bank(1, CR, 0, I), fw1_n[:, P:C], ident[:, :])
            tr(bank(0, P, I, I + P), fwo_a[:, 0:P], ident[:, :])
            tr(bank(1, CR, I, I + P), fwo_a[:, P:C], ident[:, :])
            tr(bank(0, P, I + P, I + C), fwo_r[:, 0:P], ident[0:CR, 0:CR])
            tr(bank(1, CR, I + P, I + C), fwo_r[:, P:C], ident[0:CR, 0:CR]).then_inc(c_fT, 1)
            e.wait_ge(c_fTs, 4)
            mm(bank(2, P, 0, C), fw2_a[:, :], fwoT_a[:, :], start=True, stop=False)
            mm(bank(2, P, 0, C), fw2_r[:, :], fwoT_r[:, :], start=False, stop=True)
            mm(bank(3, P, 0, C), ones[0:1, :], rows[0:1, R_FBO, :], start=True, stop=False)
            mm(bank(3, P, 0, C), fb2_ab[:, :], fwoT_a[:, :], start=False, stop=False)
            mm(bank(3, P, 0, C), fb2_rb[:, :], fwoT_r[:, :], start=False, stop=True).then_inc(c_fw, 1)
            e.wait_ge(c_fws, 2)
            e.wait_ge(c_blk, 3)

            def t_front(it, b):
                wait(e, x_in[b % 2], it, 16 * (b // 2 + 1))
                if b == 0:
                    again(e, f_b, it, 2)
                if b >= 2:
                    wait(e, t_h, it, b - 1)
                for w in range(W):
                    tr(bank(0, P, P * w, P * w + P), t_x[:, b % 2, w, 0:P], ident[:, :])
                for w in range(W):
                    last = tr(bank(3, CR, P * w, P * w + P), t_x[:, b % 2, w, P:C], ident[:, :])
                last.then_inc(t_xT.sem, 1)
                wait(e, t_xTa, it, b + 1)
                wait(e, t_xTr, it, b + 1)
                for out_, c0, n in ((bank(1, P, 0, 256), 0, P), (bank(1, P, 256, 512), C, P),
                                    (bank(2, CR, 0, 256), P, CR), (bank(2, CR, 256, 512), C + P, CR)):
                    mm(out_, tw_a[:, c0:c0 + n], t_xa[:, :], start=True, stop=False)
                    last = mm(out_, tw_r[:, c0:c0 + n], t_xr[:, :], start=False, stop=True)
                last.then_inc(t_qk.sem, 1)
                for w in range(W):
                    mm(bank(3, P, C * w, C * w + C), t_xa[:, P * w:P * w + P], tw_a[:, 2 * C:3 * C], start=True, stop=False)
                    last = mm(bank(3, P, C * w, C * w + C), t_xr[:, P * w:P * w + P], tw_r[:, 2 * C:3 * C], start=False, stop=True)
                last.then_inc(t_vps.sem, 1)

            def to_channels(it, k, src, split=False):
                for b in range(GB):
                    tr(bank(0, P, T * b, T * b + T), src[:, b, 0:P], ident[:, :])
                for b in range(GB):
                    last = tr(bank(1, P if split else CR, T * b, T * b + T), src[:, b, P:C + CR if split else C], ident[:, :])
                return last

            def cols(b):
                return slice(T * b, T * b + T)

            def split_mm(out_, w_hi, w_lo, w_d, w_d0, c, last_stop=True):
                mm(out_, w_hi, xa_h[:, c], start=True, stop=False)
                mm(out_, w_hi, xa_l[:, c], start=False, stop=False)
                mm(out_, w_lo, xa_h[:, c], start=False, stop=False)
                mm(out_, w_d, xd_h[:, c], start=False, stop=False)
                return mm(out_, w_d0, xe_l[:, c], start=False, stop=last_stop)

            for it in passes(e):
                t_front(it, 0)
                for b in range(GB):
                    wait(e, t_qmask, it, 2 * b + 2)
                    wait(e, t_k, it, 2 * b + 2)
                    if b >= 1:
                        wait(e, t_pTa, it, 2 * b)
                        wait(e, t_pTd, it, b)
                    for w in range(W):
                        for j in range(HP):
                            n = w * HP + j
                            o = ps[:, 4 + n // 4, P * (n % 4):P * (n % 4) + P]
                            if j < 4:
                                last = mm(o, t_qm[:, w, 2 * j:2 * j + 2, :], t_ka[:, w, :], start=True, stop=True)
                            else:
                                last = mm(o, t_qmr[:, w, 2 * j - 8:2 * j - 6, :], t_kr[:, w, :], start=True, stop=True)
                    last.then_inc(t_s.sem, 1)
                    if b + 1 < GB:
                        t_front(it, b + 1)
                    wait(e, t_exp, it, b + 1)
                    for n in range(W * HP):
                        last = tr(ps[:, 4 + n // 4, P * (n % 4):P * (n % 4) + P], t_e[:, n, :], ident[:, :])
                        if n % 4 == 3:
                            last.then_inc(t_pT.sem, 1)
                    wait(e, t_vs, it, b + 1)
                    if b >= 1:
                        wait(e, t_on, it, 2 * b)
                    for n in range(W * HP):
                        if n == 0:
                            wait(e, t_pTa, it, 2 * b + 1)
                        if n == 4:
                            wait(e, t_pTa, it, 2 * b + 2)
                        if n == 8:
                            wait(e, t_pTd, it, b + 1)
                        last = mm(bank(7, P, 33 * n, 33 * n + 33), t_pt[:, n, :], t_v[:, b % 2, n // HP, n % HP, :], start=True, stop=True)
                    last.then_inc(t_ops.sem, 1)
                    wait(e, t_on, it, 2 * b + 2)
                    if b >= 1:
                        wait(e, t_h, it, b)
                    for w in range(W):
                        last = tr(bank(3, HP * D, P * w, P * w + P), t_o[:, HP * w:HP * w + HP, :].rearrange("p a b -> p (a b)"), ident[:, :])
                    last.then_inc(t_oT.sem, 1)
                    wait(e, t_oTs, it, b + 1)
                    for s in range(2):
                        last = mm(bank(3, P, 256, 256 + C),
                                  t_ot[:, s, :, :],
                                  tproj[:, s, :], start=s == 0, stop=s == 1)
                    last.then_inc(t_y.sem, 1)
                wait(e, ln_norm, it, GB)
                to_channels(it, 0, xn).then_inc(gxT.sem, 1)
                wait(e, gxTa, it, 1)
                wait(e, gxTr, it, 1)
                wait(e, t_h, it, GB)
                for j, c0 in enumerate((0, C, P, C + P)):
                    n = P if j < 2 else CR
                    mm(bank(2 + j, n), pw_a[:, c0:c0 + n], gx_a[:, :], start=True, stop=False)
                    mm(bank(2 + j, n), pw_r[:, c0:c0 + n], gx_r[:, :], start=False, stop=True).then_inc(p_qk.sem, 1)
                for b in range(GB):
                    o = bank(6 + b // 2, P, C * (b % 2), C * (b % 2) + C)
                    mm(o, gx_a[:, cols(b)], pw_a[:, 2 * C:3 * C], start=True, stop=False)
                    last = mm(o, gx_r[:, cols(b)], pw_r[:, 2 * C:3 * C], start=False, stop=True)
                    if b % 2:
                        last.then_inc(p_vps.sem, 1)
                for j in range(HP):
                    r, k, i = (P, 0, j) if j < 4 else (CR, 2, j - 4)
                    wait(e, p_cp, it, k + 1)
                    wait(e, p_sqd, it, k + 1)
                    if j >= 2:
                        wait(e, p_eq, it, j - 1)
                    mm(bank(j % 2), rf_blk[0:r, 2 * i:2 * i + 2, :], p_t[0:r, k, :], start=True, stop=False)
                    mm(bank(j % 2), norm_blk[0:r, 2 * i:2 * i + 2, :], p_sq[0:r, k, :], start=False, stop=True).then_inc(p_fq.sem, 1)

                def features_k(b):
                    if b == 0:
                        wait(e, p_cp, it, 4)
                        wait(e, p_sqd, it, 4)
                    if b >= 2:
                        wait(e, p_ek, it, b - 1)
                    q = 2 + 2 * (b % 2)
                    mm(bank(q), p_t[:, 1, cols(b)], rf_blk[:, :, :], start=True, stop=False)
                    mm(bank(q), p_sq[:, 1, cols(b)], norm_blk[:, :, :], start=False, stop=True)
                    mm(bank(q + 1, P, 0, 256), p_t[0:CR, 3, cols(b)], rf_blk[0:CR, 0:4, :], start=True, stop=False)
                    mm(bank(q + 1, P, 0, 256), p_sq[0:CR, 3, cols(b)], norm_blk[0:CR, 0:4, :], start=False, stop=True).then_inc(p_fk.sem, 1)

                features_k(0)
                features_k(1)
                for b in range(GB):
                    wait(e, p_ek, it, b + 1)
                    wait(e, p_vs, it, 2 if b == 0 else b // 2 + 1)
                    if b >= 1:
                        wait(e, p_kvs, it, b)
                    for j in range(HP):
                        last = mm(bank(6, P, 34 * j, 34 * j + 34), p_kp[:, b % 2, P * j:P * j + P],
                                  p_v[:, b, 2 * j:2 * j + 2, :], start=True, stop=True)
                    last.then_inc(p_kvp.sem, 1)
                    if b + 2 < GB:
                        features_k(b + 2)
                    wait(e, p_kvs, it, b + 1)
                    wait(e, p_eq, it, HP)
                    if b >= 1:
                        wait(e, p_att, it, b)
                    for j in range(HP):
                        last = mm(bank(7, P, 34 * j, 34 * j + 34), p_qp[:, j, cols(b)], p_kv[:, b % 2, j, :], start=True, stop=True)
                    last.then_inc(p_num.sem, 1)
                wait(e, p_att, it, GB)
                to_channels(it, 0, p_xa).then_inc(p_aT.sem, 1)
                wait(e, p_aTa, it, 1)
                wait(e, p_aTr, it, 1)
                for b in range(GB):
                    o = bank(2 + b // 2, P, C * (b % 2), C * (b % 2) + C)
                    mm(o, gx_a[:, cols(b)], pproj_a[:, :], start=True, stop=False)
                    last = mm(o, gx_r[:, cols(b)], pproj_r[:, :], start=False, stop=True)
                    if b % 2:
                        last.then_inc(p_pr.sem, 1)
                wait(e, ln_norm, it, GB * 3)
                wait(e, ln_dup, it, 1)
                to_channels(it, 2, xn, split=True).then_inc(gxT.sem, 1)
                wait(e, m_prod, it, 2)
                mm(bank(2, P, 0, GB * E), ones[:, :], m_pa[:, :, :], start=True, stop=False)
                mm(bank(2, P, 0, GB * E), ones[0:CR, :], m_pr[:, :, :], start=False, stop=True).then_inc(m_log.sem, 1)
                wait(e, m_st, it, 7)
                chosen = [e.value_load(m_idx[0:1, b:b + 1], min_val=0, max_val=E - 1) for b in range(GB)]
                wait(e, xhi, it, 2)
                wait(e, xlo, it, 2)
                w2_flat = w2[:, :, :, :].rearrange("p e t c -> p (e t c)")

                def up(b):
                    if b >= 2:
                        wait(e, m_act, it, 2 * (b - 1))
                    for f in range(FT):
                        o = bank(2 + 2 * (b % 2) + f // 4, P, P * (f % 4), P * (f % 4) + P)
                        at = bass.ds(chosen[b] * F + P * f, P)
                        split_mm(o, w1_h[:, at], w1_l[:, at], w1_d[:, at], w1_d[0:CR, at], cols(b), last_stop=False)
                        last = mm(o, b1_hl[:, at], ones16[:, :], start=False, stop=True)
                    last.then_inc(m_up.sem, 1)

                def down(b):
                    wait(e, m_act, it, 2 * (b + 1))
                    if b >= 2:
                        wait(e, m_res, it, b - 1)
                    o = bank(6 + b % 2, P, 0, C)
                    for f in range(FT):
                        mm(o, m_h[:, b % 2, P * f:P * f + P], w2_flat[:, bass.ds(chosen[b] * (FT * C) + C * f, C)],
                           start=f == 0, stop=False)
                    mm(o, ones[0:1, :], b2_row[0:1, bass.ds(chosen[b] * C, C)], start=False, stop=True).then_inc(m_dn.sem, 1)

                up(0)
                for b in range(GB):
                    if b + 1 < GB:
                        up(b + 1)
                    down(b)
                wait(e, ln_norm, it, GB * 4)
                wait(e, ln_dup, it, 2)
                to_channels(it, 3, xn, split=True).then_inc(gxT.sem, 1)
                wait(e, xhi, it, 4)
                wait(e, xlo, it, 4)
                every = slice(0, GT)

                def scan_weights(o, n):
                    return split_mm(o, sw_h[:, n, :], sw_l[:, n, :], sw_d[:, n, :], sw_d[0:CR, n, :], every)

                for s in range(2):
                    scan_weights(bank(4 + s), 2 * NT + s).then_inc(s_dps.sem, 1)
                LAG = 2
                for i in range(NT + LAG):
                    if i < NT:
                        if i >= 2:
                            wait(e, s_hs, it, i - 1)
                        scan_weights(bank(2 + i % 2), i).then_inc(s_bps.sem, 1)
                        if i >= 2:
                            wait(e, s_pr, it, i - 1)
                        else:
                            wait(e, s_zs, it, 2)
                        scan_weights(bank(4 + i % 2), NT + i).then_inc(s_cps.sem, 1)
                    if i >= LAG:
                        k = i - LAG
                        wait(e, s_pr, it, k + 1)
                        if k < N1:
                            mm(bank(6), ident[:, :], s_p[:, k % AB, :], start=k == 0, stop=k == N1 - 1).then_inc(s_acc.sem, 1)
                        else:
                            mm(bank(7, CR), fold[:, :], s_p[:, k % AB, :], start=k == N1, stop=k == NT - 1).then_inc(s_acc.sem, 1)
                wait(e, s_yc, it, 2)
                for b in range(GB):
                    o = C * (b % 2)
                    tr(bank(b // 2, P, o, o + P), s_ya[:, cols(b)], ident[:, :])
                    last = tr(bank(b // 2, P, o + P, o + C), s_yr[:, cols(b)], ident[0:CR, 0:CR])
                    if b % 2:
                        last.then_inc(s_yT.sem, 1)
                wait(e, ln_norm, it, GB * 5)
                to_channels(it, 4, xn).then_inc(gxT.sem, 1)
                wait(e, gxTa, it, 2)
                wait(e, gxTr, it, 2)
                mm(bank(2), fw1_a[:, :], gx_a[:, :], start=True, stop=False)
                mm(bank(2), fw1_r[:, :], gx_r[:, :], start=False, stop=True).then_inc(f_up.sem, 1)
                wait(e, f_rl, it, 1)
                for b in range(GB):
                    last = mm(bank(3 + b // 2, P, C * (b % 2), C * (b % 2) + C), f_h[:, cols(b)], fw21[:, :], start=True, stop=True)
                    if b % 2:
                        last.then_inc(f_dn.sem, 1)

        @block.vector
        def _(e):
            tt, ts, stt = e.tensor_tensor, e.tensor_scalar, e.scalar_tensor_tensor

            def bcast(row, n):
                return bc[:, row, :].unsqueeze(1).to_broadcast([P, n, C])

            e.memset(b1_hl[:, :], 0.0).then_inc(c_bzero, 1)
            e.wait_ge(c_w1hi, 4)
            e.wait_ge(d_moe, 16 * 11)
            stt(out=w1_l[:, :].rearrange("p (e f) -> p e f", e=E), in0=w1_sa[:, :, :], scalar=ES,
                in1=w1_h[:, :].rearrange("p (e f) -> p e f", e=E), op0=ALU.mult, op1=ALU.subtract).then_inc(c_w1lo, 1)
            wd = w1_d[64:P, :].rearrange("p (e f) -> p e f", e=E)
            stt(out=wd, in0=w1_sd[64:P, :, :], scalar=ES, in1=wd, op0=ALU.mult, op1=ALU.subtract).then_inc(c_w1lo, 1)
            stt(out=b1_hl[32:33, :], in0=b1_row[32:33, :], scalar=ES, in1=b1_hl[32:33, :],
                op0=ALU.mult, op1=ALU.subtract).then_inc(c_w1lo, 1)
            for q in range(NS // 2):
                e.wait_ge(c_swhi, 2 * (q + 1))
                v = bank(q % 4).rearrange("p (a b) -> p a b", b=P)
                w_hi, w_d = sw_h[:, 2 * q:2 * q + 2, :], sw_d[64:P, 2 * q:2 * q + 2, :]
                stt(out=sw_l[:, 2 * q:2 * q + 2, :], in0=v[:, 0:2, :], scalar=WS, in1=w_hi, op0=ALU.mult,
                    op1=ALU.subtract).then_inc(c_swlo, 1)
                stt(out=w_d, in0=v[64:P, 2:4, :], scalar=WS, in1=w_d, op0=ALU.mult, op1=ALU.subtract).then_inc(c_swlo, 1)
            e.wait_ge(d_small, 16 * (ROWS + 8 + 3 + 3))
            e.wait_ge(d_tok, 16 * (6 + 2 * HP))
            e.wait_ge(d_ffn, 16 * 8)
            e.wait_ge(c_mask, 6)
            e.wait_ge(c_ones, 2)
            e.wait_ge(c_ident, 2)
            ts(ra_all[:, :], a_all[:, :], WS, None, ALU.mult).then_inc(c_ra, 1)
            ts(negmask[:, :], headmask[:, :], -0.5, None, ALU.mult).then_inc(c_ra, 1)
            tt(tbv_b[:, :, :], tbv[:, :].unsqueeze(2).to_broadcast([HP * D, 2, P]),
               ones[0:HP * D, :].unsqueeze(1).to_broadcast([HP * D, 2, P]), ALU.mult).then_inc(c_cols, 1)
            ts(fb2_ab[:, :], ones[:, :], fb2_a[:, 0:1], None, ALU.mult).then_inc(c_cols, 1)
            ts(fb2_rb[:, :], ones[0:CR, :], fb2_r[:, 0:1], None, ALU.mult).then_inc(c_cols, 1)
            tt(fold[:, :], ident[:, 0:CR], ident[:, CR:P], ALU.add).then_inc(c_cols, 1)
            e.wait_ge(c_ra, 2)
            e.reciprocal(ra_all[:, :], ra_all[:, :]).then_inc(c_ra, 1)
            tt(rf_blk[:, :, :], rf_rep[:, :].unsqueeze(1).to_broadcast([P, 8, M]),
               headmask[:, :].unsqueeze(2).to_broadcast([P, 8, M]), ALU.mult).then_inc(c_blk, 1)
            tt(norm_blk[:, :, :], ones[:, 0:M].unsqueeze(1).to_broadcast([P, 8, M]),
               negmask[:, :].unsqueeze(2).to_broadcast([P, 8, M]), ALU.mult).then_inc(c_blk, 1)
            e.wait_ge(c_bcast, 1)
            e.tensor_copy(bc[:, 0:2, :], bank(4, P, 0, 2 * C)).then_inc(c_bcast_used, 1)
            e.tensor_copy(bc[:, 2:4, :], bank(5, P, 0, 2 * C)).then_inc(c_bcast_used, 1)
            e.tensor_copy(bc[:, 5, :], bank(6, P, C, 2 * C)).then_inc(c_bcast_used, 1)
            e.tensor_copy(bc[:, 6, :], bank(7, P, 0, C)).then_inc(c_bcast_used, 1)
            e.wait_ge(c_ra, 3)
            e.tensor_copy(m_t[:, 0, :], minus_half[:, :]).then_inc(c_bcast_used, 1)
            e.wait_ge(c_fT, 1)
            e.tensor_copy(fw1_a[:, :], bank(0, P, 0, I)).then_inc(c_fTs, 1)
            e.tensor_copy(fw1_r[:, :], bank(1, CR, 0, I)).then_inc(c_fTs, 1)
            e.tensor_copy(fwoT_a[:, :], bank(0, P, I, I + C)).then_inc(c_fTs, 1)
            e.tensor_copy(fwoT_r[:, :], bank(1, CR, I, I + C)).then_inc(c_fTs, 1)
            e.wait_ge(c_fw, 1)
            e.tensor_copy(fw21[:, :], bank(2, P, 0, C)).then_inc(c_fws, 1)
            e.tensor_copy(bc[:, R_FBO, :], bank(3, P, 0, C)).then_inc(c_fws, 1)
            e.wait_ge(c_blk, 2)
            e.wait_ge(c_fws, 2)
            e.wait_ge(c_bcast_used, 5)
            e.wait_ge(c_v1, 2)
            e.memset(m_mx[:, :], 0.0).then_inc(c_blk, 1)

            def layernorm(it, k, src, ready):
                for b in range(GB):
                    ready(b)
                    e.bn_stats(ln_st[:, b, :], src[:, b, :]).then_inc(ln_stats.sem, 1)
                for b in range(GB):
                    wait(e, ln_stats, it, GB * k + b + 1)
                    e.bn_aggr(ln_mv[:, b, :], ln_st[:, b, :]).then_inc(ln_aggr.sem, 1)
                wait(e, ln_aggr, it, GB * (k + 1))
                wait(e, ln_rstd, it, k + 1)
                for b in range(GB):
                    ts(xn[:, b, 0:C], src[:, b, :], ln_mv[:, b, 0:1], ln_rs[:, b:b + 1], ALU.subtract, ALU.mult).then_inc(ln_norm.sem, 1)

            def t_front(it, b):
                wait(e, t_xT, it, b + 1)
                e.tensor_copy(t_xr[:, :], bank(3, CR, 0, 256)).then_inc(t_xTr.sem, 1)
                wait(e, t_vps, it, b + 1)
                e.tensor_copy(t_v[:, b % 2, :, :, 0:2 * D],
                              bank(3, P, 0, W * C).rearrange("p (w j d) -> p w j d", w=W, j=HP)).then_inc(t_vs.sem, 1)
                wait(e, t_q, it, 2 * b + 2)
                tt(t_qx[:, :, :], t_qa[:, :, 0:NQ], t_qa[:, :, NQ:P], ALU.max).then_inc(t_qmax.sem, 1)
                tt(t_qxr[:, :, :], t_qr[:, :, 0:NQ], t_qr[:, :, NQ:P], ALU.max).then_inc(t_qmax.sem, 1)
                wait(e, t_qmax, it, 2 * b + 1)
                tt(t_qm[:, :, :, :], t_qx[:, :, :].unsqueeze(2).to_broadcast([P, W, 8, NQ]),
                   headmask[:, :].unsqueeze(1).unsqueeze(3).to_broadcast([P, W, 8, NQ]), ALU.mult).then_inc(t_qmask.sem, 1)
                wait(e, t_qmax, it, 2 * b + 2)
                tt(t_qmr[:, :, :, :], t_qxr[:, :, :].unsqueeze(2).to_broadcast([CR, W, 4, NQ]),
                   headmask[0:CR, 0:4].unsqueeze(1).unsqueeze(3).to_broadcast([CR, W, 4, NQ]), ALU.mult).then_inc(t_qmask.sem, 1)

            for it in passes(e):
                t_front(it, 0)
                for b in range(GB):
                    wait(e, t_s, it, b + 1)
                    scores = ps[:, 4:7, :].rearrange("p a (b c) -> p (a b) c", c=P)
                    e.reduce_max(t_mx[:, :], scores, AX.X).then_inc(t_max.sem, 1)
                    wait(e, t_max, it, b + 1)
                    if b >= 1:
                        wait(e, t_exp, it, b)
                    tt(t_p[:, :, :], scores, t_mx[:, :].unsqueeze(2).to_broadcast([P, W * HP, P]), ALU.subtract).then_inc(t_sub.sem, 1)
                    if b + 1 < GB:
                        t_front(it, b + 1)
                    wait(e, t_pT, it, 3 * b + 3)
                    if b >= 1:
                        wait(e, t_ops, it, b)
                    e.tensor_copy(t_pt[:, 8:12, :].rearrange("p a b -> p (a b)"), bank(6)).then_inc(t_pTd.sem, 1)
                    wait(e, t_ops, it, b + 1)
                    o = bank(7, P, 0, W * HP * 33).rearrange("p (n c) -> p n c", c=33)
                    e.reciprocal(t_rd[:, :], o[:, :, 32]).then_inc(t_rden.sem, 1)
                    wait(e, t_rden, it, b + 1)
                    if b >= 1:
                        wait(e, t_oT, it, b)
                    for s in range(2):
                        r = slice(64 * s, 64 * s + 64)
                        tt(t_o[r, :, :], o[r, :, D * s:D * s + D], t_rd[r, :].unsqueeze(2).to_broadcast([64, W * HP, D]),
                           ALU.mult).then_inc(t_on.sem, 1)
                    wait(e, t_oT, it, b + 1)
                    if b >= 1:
                        wait(e, t_y, it, b)
                    e.tensor_copy(t_ot[:, :, :, :].rearrange("p s w q -> p w s q"),
                                  bank(3, HP * D, 0, W * P).rearrange("p (w s q) -> p w s q", w=W, s=2)).then_inc(t_oTs.sem, 1)
                    wait(e, t_y, it, b + 1)
                    tt(h[:, b, :], bank(3, P, 256, 256 + C), bc[:, R_TPROJ, :], ALU.add).then_inc(t_h.sem, 1)
                layernorm(it, 0, h, lambda b: wait(e, t_h, it, b + 1))
                wait(e, gxT, it, 1)
                e.tensor_copy(gx_r[:, :], bank(1, CR)).then_inc(gxTr.sem, 1)
                for j in range(4):
                    r = P if j < 2 else CR
                    wait(e, p_qk, it, j + 1)
                    wait(e, p_sqd, it, j + 1)
                    e.tensor_copy(p_t[0:r, j, :], bank(2 + j, r)).then_inc(p_cp.sem, 1)
                for j in range(2):
                    wait(e, p_vps, it, j + 1)
                    e.tensor_copy(p_v[:, 2 * j:2 * j + 2, :, 0:D],
                                  bank(6 + j, P, 0, 2 * C).rearrange("p (b n d) -> p b n d", b=2, n=H)).then_inc(p_vs.sem, 1)
                for b in range(GB):
                    wait(e, p_kvp, it, b + 1)
                    if b >= 2:
                        wait(e, p_num, it, b - 1)
                    tt(p_kv[:, b % 2, :, :], bank(6, P, 0, 204).rearrange("p (j c) -> p j c", c=34),
                       pairmask[:, :, :].rearrange("p a b -> p (a b)").unsqueeze(1).to_broadcast([P, HP, 34]),
                       ALU.mult).then_inc(p_kvs.sem, 1)
                    wait(e, p_num, it, b + 1)
                    num = bank(7, P, 0, 204).rearrange("p (n c) -> p n c", c=D + 1)
                    ts(p_n[:, b % 2, :], num[:, :, D], M * 1e-6, None, ALU.add).then_inc(p_den.sem, 1)
                    wait(e, p_den, it, b + 1)
                    e.reciprocal(p_r[:, b % 2, :], p_n[:, b % 2, :]).then_inc(p_rec.sem, 1)
                    wait(e, p_rec, it, b + 1)
                    tt(p_xa[:, b, :].rearrange("p (n d) -> p n d", n=H), num[:, :, 0:D],
                       p_r[:, b % 2, :].unsqueeze(2).to_broadcast([P, H, D]), ALU.mult).then_inc(p_att.sem, 1)
                wait(e, p_aT, it, 1)
                e.tensor_copy(gx_r[:, :], bank(1, CR)).then_inc(p_aTr.sem, 1)
                for j in range(2):
                    y = yres[:, 2 * j:2 * j + 2, :]
                    wait(e, p_pr, it, j + 1)
                    tt(y, bank(2 + j, P, 0, 2 * C).rearrange("p (b c) -> p b c", b=2), bcast(R_AB, 2), ALU.add).then_inc(p_b.sem, 1)
                    wait(e, p_b, it, j + 1)
                    tt(y, y, xn[:, 2 * j:2 * j + 2, 0:C], ALU.add).then_inc(p_y.sem, 1)
                layernorm(it, 1, yres, lambda b: wait(e, p_y, it, b // 2 + 1))
                wait(e, ln_norm, it, 2 * GB)
                tt(yres[:, :, :], xn[:, :, 0:C], bcast(R_AG, GB), ALU.mult).then_inc(p_g.sem, 1)
                wait(e, p_g, it, 1)
                tt(yres[:, :, :], yres[:, :, :], bcast(R_ABETA, GB), ALU.add).then_inc(p_be.sem, 1)
                wait(e, p_be, it, 1)
                tt(h[:, :, :], h[:, :, :], yres[:, :, :], ALU.add).then_inc(p_h.sem, 1)
                layernorm(it, 2, h, lambda b: wait(e, p_h, it, 1))
                wait(e, xhi, it, 2)
                e.reduce_sum(m_ma[:, :], bank(0).rearrange("p (b t) -> p b t", b=GB), AX.X).then_inc(m_mean.sem, 1)
                e.reduce_sum(m_mr[:, :], bank(1, CR).rearrange("p (b t) -> p b t", b=GB), AX.X).then_inc(m_mean.sem, 1)
                wait(e, m_mean, it, 2)
                for o, a, wg, r in ((m_pa, m_ma, wg_a, P), (m_pr, m_mr, wg_r, CR)):
                    tt(o[:, :, :], a[:, :].unsqueeze(2).to_broadcast([r, GB, E]), wg[:, :].unsqueeze(1).to_broadcast([r, GB, E]),
                       ALU.mult).then_inc(m_prod.sem, 1)
                tt(xa_l[:, :], bank(0), xa_h[:, :], ALU.subtract).then_inc(xlo.sem, 1)
                tt(xe_l[:, :], bank(1, CR), xd_h[0:CR, :], ALU.subtract).then_inc(xlo.sem, 1)
                wait(e, m_log, it, 1)
                ts(m_l[:, :, :], bank(2, P, 0, GB * E).rearrange("p (b x) -> p b x", b=GB), 1.0 / T, None, ALU.mult).then_inc(m_st.sem, 1)
                wait(e, m_st, it, 1)
                e.reduce_max(m_mx[:, :], m_l[:, :, :], AX.X).then_inc(m_st.sem, 1)
                wait(e, m_st, it, 2)
                tt(m_ls[:, :, :], m_l[:, :, :], m_mx[:, :].unsqueeze(2).to_broadcast([P, GB, E]), ALU.subtract).then_inc(m_st.sem, 1)
                wait(e, m_st, it, 3)
                ts(m_eq[:, :, :], m_ls[:, :, :], 0.0, None, ALU.is_equal).then_inc(m_st.sem, 1)
                wait(e, m_st, it, 4)
                ts(m_t[:, 0, :], m_eq[:, :, 0], -1.0, 1.0, ALU.mult, ALU.add).then_inc(m_st.sem, 1)
                ts(m_t[:, 1, :], m_eq[:, :, 1], -1.0, 2.0, ALU.mult, ALU.add).then_inc(m_st.sem, 1)
                wait(e, m_st, it, 6)
                tt(m_idx[:, :], m_t[:, 0, :], m_t[:, 1, :], ALU.mult).then_inc(m_st.sem, 1)
                wait(e, m_ex, it, 1)
                e.reduce_sum(m_sum[:, :], m_e[:, :, :], AX.X).then_inc(m_st.sem, 1)
                wait(e, m_st, it, 8)
                e.reciprocal(m_w[:, :], m_sum[:, :]).then_inc(m_st.sem, 1)
                wait(e, m_st, it, 9)
                for b in range(GB):
                    wait(e, m_dn, it, b + 1)
                    stt(out=h[:, b, :], in0=bank(6 + b % 2, P, 0, C), scalar=m_w[:, b:b + 1], in1=h[:, b, :],
                        op0=ALU.mult, op1=ALU.add).then_inc(m_res.sem, 1)
                layernorm(it, 3, h, lambda b: wait(e, m_res, it, b + 1))
                wait(e, xhi, it, 4)
                e.tensor_copy(s_x[:, 0, :], bank(0)).then_inc(s_xc.sem, 1)
                e.tensor_copy(s_x[:, 1, :], bank(1)).then_inc(s_xc.sem, 1)
                tt(xa_l[:, :], bank(0), xa_h[:, :], ALU.subtract).then_inc(xlo.sem, 1)
                tt(xe_l[:, :], bank(1, CR), xd_h[0:CR, :], ALU.subtract).then_inc(xlo.sem, 1)
                for s in range(2):
                    wait(e, s_dps, it, s + 1)
                    ts(s_z[:, s, :], bank(4 + s), 1.0 / WS, dbias[:, s:s + 1], ALU.mult, ALU.add).then_inc(s_zs.sem, 1)
                wait(e, s_ln, it, 1)
                wait(e, s_zs, it, 2)
                stt(out=s_dt[:, :, :], in0=s_z[:, :, :], scalar=0.0, in1=s_u[:, :, :], op0=ALU.max, op1=ALU.add).then_inc(s_dlt.sem, 1)
                for i in range(NT + 1):
                    if i < NT:
                        wait(e, s_bps, it, i + 1)
                        wait(e, s_wxs, it, i + 1)
                        b_ps = bank(2 + i % 2)
                        stt(out=b_ps, in0=b_ps, scalar=ra_all[:, i:i + 1], in1=s_wx[:, i % AB, :], op0=ALU.mult,
                            op1=ALU.mult).then_inc(s_bx.sem, 1)
                    if i >= 1:
                        k = i - 1
                        wait(e, s_hs, it, k + 1)
                        wait(e, s_cps, it, k + 1)
                        if k >= AB:
                            wait(e, s_acc, it, k - AB + 1)
                        stt(out=s_p[:, k % AB, :], in0=bank(4 + k % 2), scalar=1.0 / WS, in1=s_h[:, k % AB, :], op0=ALU.mult,
                            op1=ALU.mult).then_inc(s_pr.sem, 1)
                    if i < NT:
                        wait(e, s_bx, it, i + 1)
                        wait(e, s_a0, it, i + 1)
                        e.tensor_tensor_scan(s_h[:, i % AB, :], s_a[:, i % AB, :], b_ps, 0.0, ALU.mult, ALU.add).then_inc(s_hs.sem, 1)
                for j in range(2):
                    wait(e, s_yT, it, j + 1)
                    tt(h[:, 2 * j:2 * j + 2, :], h[:, 2 * j:2 * j + 2, :],
                       bank(j, P, 0, 2 * C).rearrange("p (b c) -> p b c", b=2), ALU.add).then_inc(s_res.sem, 1)
                layernorm(it, 4, h, lambda b: wait(e, s_res, it, b // 2 + 1))
                wait(e, gxT, it, 4)
                e.tensor_copy(gx_r[:, :], bank(1, CR)).then_inc(gxTr.sem, 1)
                for j in range(2):
                    wait(e, f_dn, it, j + 1)
                    tt(yres[:, 2 * j:2 * j + 2, :], bank(3 + j, P, 0, 2 * C).rearrange("p (b c) -> p b c", b=2),
                       bcast(R_FBO, 2), ALU.add).then_inc(f_b.sem, 1)
                layernorm(it, 5, yres, lambda b: wait(e, f_b, it, b // 2 + 1))
                wait(e, ln_norm, it, LNS * GB)
                tt(yres[:, :, :], xn[:, :, 0:C], bcast(R_FG, GB), ALU.mult).then_inc(f_g.sem, 1)
                wait(e, f_g, it, 1)
                tt(yres[:, :, :], yres[:, :, :], bcast(R_FBETA, GB), ALU.add).then_inc(f_be.sem, 1)
                wait(e, f_be, it, 1)
                again(e, o_out, it, 16)
                tt(outb[:, :, :], h[:, :, :], yres[:, :, :], ALU.add).then_inc(f_out.sem, 1)


_INS = ['x', 'L0_tok_Wqkv', 'L0_tok_bqkv', 'L0_tok_Wproj', 'L0_tok_bproj', 'L0_attn_W_qkv', 'L0_attn_W_proj',
        'L0_attn_b_proj', 'L0_attn_gamma', 'L0_attn_beta', 'L0_attn_random_features', 'L0_ffn_Wg', 'L0_ffn_W1',
        'L0_ffn_b1', 'L0_ffn_W2', 'L0_ffn_b2', 'L1_attn_A', 'L1_attn_W_delta', 'L1_attn_delta_bias', 'L1_attn_W_B',
        'L1_attn_W_C', 'L1_ffn_W1', 'L1_ffn_b1', 'L1_ffn_W2', 'L1_ffn_b2', 'L1_ffn_Wo', 'L1_ffn_bo', 'L1_ffn_gamma',
        'L1_ffn_beta']


def kernel(**inputs):
    import numpy as _np
    import concourse.bacc as _bacc
    from concourse import mybir as _mybir
    from concourse.bass_utils import run_bass_kernel_spmd as _run

    nc = _bacc.Bacc("TRN2", target_bir_lowering=False, num_devices=1)
    arrays, args = {}, []
    for name in _INS:
        a = _np.ascontiguousarray(inputs[name])
        arrays[f"in_{name}_dram"] = a
        args.append(nc.dram_tensor(f"in_{name}_dram", a.shape, _mybir.dt.from_np(a.dtype), kind="ExternalInput").ap())
    args.append(nc.dram_tensor("out_0_dram", (NB, T, C), _mybir.dt.float32, kind="ExternalOutput").ap())
    tower(nc, *args)
    r = _run(nc, [arrays], core_ids=[0])
    return r.results[0]["out_0_dram"]
```

```python
from contextlib import ExitStack

import concourse.bass as bass
from concourse import mybir

fp32 = mybir.dt.float32
fp16 = mybir.dt.float16
i32 = mybir.dt.int32
ALU = mybir.AluOpType
ACT = mybir.ActivationFunctionType
AX = mybir.AxisListType

NB, NRAW, C = 16, 256, 192
P = 128
CR = C - P
W, NQ = 2, 64
T = W * NQ
H, D = 12, 16
HP = H // 2
VC = 2 * D + 1
M = 64
E, F = 3, 768
FT = F // P
N = 16
I = 128
GB = 4
G = NB // GB
GT = GB * T
N1, N2 = N, N // 2
NT = N1 + N2
NS = 2 * NT + 2
EPS = 1e-5
WS = 32.0
ES = 64.0
AW = 3 * C + 6 * P + C + C
A_Q, A_V, A_P = 3 * C, 3 * C + 6 * P, 3 * C + 6 * P + C
STG = 1280
SC = STG // P
NCH = 2 + E + NS // SC

ROWS = 7
R_TPROJ, R_AB, R_AG, R_ABETA, R_FBO, R_FG, R_FBETA = range(ROWS)


class Signal:

    def __init__(self, sem, per):
        self.sem, self.per = sem, per


def wait(e, signal, g, k):
    assert 1 <= k <= signal.per, k
    e.wait_ge(signal.sem, g * signal.per + k)


def again(e, signal, g, k, back=1):
    assert 1 <= k <= signal.per, k
    if g >= back:
        e.wait_ge(signal.sem, (g - back) * signal.per + k)


def tower(nc, x_t, w_att0, w_att1, w_exp, b_exp, w_scan, tproj_in, tbq_in, tbv_in, rows_in, rf_in, wg_in, w2_in, b2_in,
          a_in, dbias_in, fw1_in, fw2_in, fwo_in, fb_in, out):
    ctx = ExitStack()
    with ctx:
        def sb(name, shape, dt=fp32):
            return ctx.enter_context(nc.sbuf_tensor(name, shape, dt))

        def once(name):
            return ctx.enter_context(nc.semaphore(name))

        def signal(name, per):
            return Signal(ctx.enter_context(nc.semaphore(name)), per)

        ident = sb("ident", [P, P])
        ones = sb("ones", [P, P])
        fold = sb("fold", [P, CR])
        headmask = sb("headmask", [P, 8])
        halfmask = sb("halfmask", [P, 4])
        pairmask = sb("pairmask", [P, 2, D + 1])
        feat = sb("feat", [P, 4, M])
        featrow = sb("featrow", [P, M])
        tbq_a, tbq_r = sb("tbq_a", [P, 2]), sb("tbq_r", [CR, 2])
        tbv = sb("tbv", [HP * D, 2])
        tproj = sb("tproj", [HP * D, 2, C])
        bc = sb("bc", [P, ROWS, C])
        aw_h, aw_l = sb("aw_h", [P, AW], fp16), sb("aw_l", [P, AW], fp16)
        aw_d = sb("aw_d", [P, AW], fp16)
        wg_a, wg_r = sb("wg_a", [P, E]), sb("wg_r", [CR, E])
        w1_h, w1_l = sb("w1_h", [P, E * F], fp16), sb("w1_l", [P, E * F], fp16)
        w1_d = sb("w1_d", [P, E * F], fp16)
        w1_e = sb("w1_e", [P, E * F], fp16)
        b2_row = sb("b2_row", [1, E * C])
        w2 = sb("w2", [P, E * FT * C])
        sw_h, sw_l = sb("sw_h", [P, NS, P], fp16), sb("sw_l", [P, NS, P], fp16)
        sw_d = sb("sw_d", [P, NS, P], fp16)
        a_all, ra_all = sb("a_all", [P, NT]), sb("ra_all", [P, NT])
        dbias = sb("dbias", [P, 2])
        fw1_a, fw1_r = sb("fw1_a", [P, I]), sb("fw1_r", [CR, I])
        fw21 = sb("fw21", [I, C])
        fb1_c = sb("fb1_c", [I, 1])
        minus_half = sb("minus_half", [P, GB])

        h = sb("h", [P, 2, GB, C])
        x_h, x_l = sb("x_h", [P, 2, GT], fp16), sb("x_l", [P, 2, GT], fp16)
        x_d = sb("x_d", [P, 2, GT], fp16)
        x_e = sb("x_e", [P, 2, GT], fp16)
        s_x, s_dt = sb("s_x", [P, 2, 2, GT]), sb("s_dt", [P, 2, 2, GT])

        xn = sb("xn", [P, GB, C + CR])
        ln_st, ln_mv = sb("ln_st", [P, GB, 6]), sb("ln_mv", [P, GB, 2])
        ln_ve, ln_rs = sb("ln_ve", [P, GB]), sb("ln_rs", [P, GB])
        x_raw = sb("x_raw", [P, 2, NRAW])
        tx_h = sb("tx_h", [P, 2, 2, NRAW], fp16)
        tx_l, tx_e = sb("tx_l", [P, 2, NRAW], fp16), sb("tx_e", [CR, 2, NRAW], fp16)
        t_v = sb("t_v", [P, 2, W * HP, VC])
        p_v = sb("p_v", [P, GB, H, D + 1])

        def carve(arena, layout):
            at, views = 0, []
            for rows_, *dims in layout:
                n = 1
                for d in dims:
                    n *= d
                v = arena[0:rows_, at:at + n]
                if len(dims) == 2:
                    v = v.rearrange("p (a b) -> p a b", b=dims[1])
                elif len(dims) == 3:
                    v = v.rearrange("p (a b c) -> p a b c", b=dims[1], c=dims[2])
                views.append(v)
                at += n
            return views

        arena = sb("arena", [P, 9216])
        (t_qa, t_qr, t_ka, t_kr, t_qx, t_qxr, t_qm, t_qmr, t_mx, t_p, t_pt, t_rd, t_o, t_ot) = carve(arena, [
            (P, W, P), (CR, W, P), (P, W, P), (CR, W, P), (P, W, NQ), (CR, W, NQ), (P, W, 8, NQ), (CR, W, 4, NQ),
            (P, W * HP), (P, W * HP, P), (P, W * HP, P), (P, W * HP), (P, W * HP, D), (HP * D, 2, W, NQ)])
        (p_f, p_qp, p_kp, p_kv, p_n, p_r, p_xa) = carve(arena, [
            (P, 6, GT), (P, HP, GT), (P, 2, H * M), (P, 2, HP, 2 * (D + 1)), (P, 2, H), (P, 2, H), (P, GB, C + CR)])
        p_y, p_xb = carve(arena, [(P, GB, C), (P, GB, C)])
        m_h, s_z, s_u = carve(arena, [(P, 2, F), (P, 2, GT), (P, 2, GT)])
        m_ma, m_mr = sb("m_ma", [P, GB]), sb("m_mr", [CR, GB])
        m_pa, m_pr = sb("m_pa", [P, GB, E]), sb("m_pr", [CR, GB, E])
        m_l, m_ls, m_e, m_eq = (sb(f"m_{n}", [P, GB, E]) for n in ("l", "ls", "e", "eq"))
        m_mx, m_sum, m_w = sb("m_mx", [P, GB]), sb("m_sum", [P, GB]), sb("m_w", [P, GB])
        m_t = sb("m_t", [P, 2, GB])
        m_idx = sb("m_idx", [P, GB], i32)

        NA_, NW, NH, NP = 3, 2, 2, 3
        scan_arena = sb("scan_arena", [P, (NA_ + 2 * NW + NH + NP) * GT + 2 * GT])
        s_a, s_w, s_wx, s_h, s_p, s_acc = carve(scan_arena, [
            (P, NA_, GT), (P, NW, GT), (P, NW, GT), (P, NH, GT), (P, NP, GT), (P, 2, GT)])
        stage, b_stage = carve(scan_arena, [(P, 2, 2, STG), (P, 2, F)])
        rows, fwoT_a, fwoT_r, fw2_a, fw2_r, tbv_b, fb2_a, fb2_r, fb2_ab, fb2_rb = carve(arena, [
            (1, ROWS, C), (P, C), (CR, C), (P, I), (CR, I), (HP * D, 2, P), (P, 1), (CR, 1), (P, P), (CR, P)])
        k_xa, k_xr, f_h, k_xn = carve(scan_arena, [(P, GT), (CR, GT), (I, GT), (P, GB, C)])
        k_y = s_acc[:, :, :].rearrange("p a b -> p (a b)")[:, 0:GB * C].rearrange("p (b c) -> p b c", b=GB)
        kn_st, kn_mv = sb("kn_st", [P, GB, 6]), sb("kn_mv", [P, GB, 2])
        kn_ve, kn_rs = sb("kn_ve", [P, GB]), sb("kn_rs", [P, GB])

        ps = ctx.enter_context(nc.psum_tensor("ps", [P, 8, 512], fp32))

        def bank(n, rows_=P, a=0, b=512):
            return ps[0:rows_, n, a:b]

        d_small, d_tok, d_ffn, d_moe = once("d_small"), once("d_tok"), once("d_ffn"), once("d_moe")
        d_stage = [once("d_stage0"), once("d_stage1")]
        c_ident, c_ones, c_mask, c_mem = once("c_ident"), once("c_ones"), once("c_mask"), once("c_mem")
        c_hi, c_lo = [once(f"c_hi{n}") for n in range(NCH)], [once(f"c_lo{n}") for n in range(NCH)]
        c_cols, c_ra, c_feat = once("c_cols"), once("c_ra"), once("c_feat")
        c_bcast, c_bcs = once("c_bcast"), once("c_bcs")

        ln_stats, ln_aggr, ln_norm = signal("ln_stats", 4 * GB), signal("ln_aggr", 4 * GB), signal("ln_norm", 4 * GB)
        ln_eps, ln_rstd, ln_dup = signal("ln_eps", 4), signal("ln_rstd", 4), signal("ln_dup", 3)
        x_in = signal("x_in", 16 * GB)
        x_hi, x_lo = signal("x_hi", GB), signal("x_lo", 2 * GB)
        t_qka, t_qkr, t_vps = signal("t_qka", GB), signal("t_qkr", GB), signal("t_vps", GB)
        t_ea, t_er, t_vs = signal("t_ea", 2 * GB), signal("t_er", 2 * GB), signal("t_vs", GB)
        t_qmax, t_qmask = signal("t_qmax", 2 * GB), signal("t_qmask", 2 * GB)
        t_s, t_max, t_sub, t_exp = signal("t_s", GB), signal("t_max", GB), signal("t_sub", GB), signal("t_exp", GB)
        t_pT, t_pTa, t_pTd = signal("t_pT", 3 * GB), signal("t_pTa", 2 * GB), signal("t_pTd", GB)
        t_ops, t_rden, t_on = signal("t_ops", GB), signal("t_rden", GB), signal("t_on", 2 * GB)
        t_oT, t_oTs, t_y, t_h = signal("t_oT", GB), signal("t_oTs", GB), signal("t_y", GB), signal("t_h", GB)
        gT = signal("gT", 4)
        g_hi, g_lo = signal("g_hi", 8), signal("g_lo", 8)
        p_qk, p_sq, p_cp = signal("p_qk", 6), signal("p_sq", 6), signal("p_cp", 6)
        p_vps, p_vs, p_xbs = signal("p_vps", 2), signal("p_vs", 2), signal("p_xbs", 1)
        p_fq, p_eq, p_fk, p_ek = signal("p_fq", HP), signal("p_eq", HP), signal("p_fk", GB), signal("p_ek", GB)
        p_kvp, p_kvs, p_num = signal("p_kvp", GB), signal("p_kvs", GB), signal("p_num", GB)
        p_den, p_rec, p_att, p_dup = signal("p_den", GB), signal("p_rec", GB), signal("p_att", GB), signal("p_dup", 1)
        p_pr, p_ys, p_g, p_be, p_h = (signal("p_pr", 2), signal("p_ys", 2), signal("p_g", 1), signal("p_be", 1),
                                      signal("p_h", 1))
        m_mean, m_prod, m_log, m_st, m_ex = (signal("m_mean", 2), signal("m_prod", 2), signal("m_log", 1),
                                             signal("m_st", 9), signal("m_ex", 1))
        m_up, m_act, m_dn, m_res = signal("m_up", GB), signal("m_act", 2 * GB), signal("m_dn", GB), signal("m_res", GB)
        s_xc, s_dps, s_zs = signal("s_xc", 2), signal("s_dps", 2), signal("s_zs", 2)
        s_abs, s_exp, s_ln, s_dlt = signal("s_abs", 1), signal("s_exp", 1), signal("s_ln", 1), signal("s_dlt", 1)

        s_as, s_ws, s_wxs, s_a0 = signal("s_as", NT), signal("s_ws", NT), signal("s_wxs", NT), signal("s_a0", NT)
        s_bps, s_cps = signal("s_bps", NT), signal("s_cps", NT)
        s_bx, s_hs, s_pr, s_sum = signal("s_bx", NT), signal("s_hs", NT), signal("s_pr", NT), signal("s_sum", NT)
        s_yT, s_res = signal("s_yT", 2), signal("s_res", 2)
        kn_stats, kn_aggr, kn_norm = signal("kn_stats", 2 * GB), signal("kn_aggr", 2 * GB), signal("kn_norm", 2 * GB)
        kn_eps, kn_rstd = signal("kn_eps", 2), signal("kn_rstd", 2)
        kT, kTa, kTr = signal("kT", 1), signal("kTa", 1), signal("kTr", 1)
        f_up, f_rl, f_dn, f_b = signal("f_up", 1), signal("f_rl", 1), signal("f_dn", 2), signal("f_b", 2)
        f_g, f_be, f_out, o_out = signal("f_g", 1), signal("f_be", 1), signal("f_out", 1), signal("o_out", 16)

        TAIL = 9
        SLOTS = 2 * NT + TAIL
        FRONT = 58

        def interleave(front, scan_slot):
            done = 0
            for slot in range(SLOTS):
                if scan_slot:
                    scan_slot(slot)
                while front and done * SLOTS < FRONT * (slot + 1) and done < FRONT:
                    next(front)
                    done += 1
            if front:
                assert done == FRONT and next(front, "end") == "end"

        def program(front, scan_slot, setup_slot):
            for s in range(G + 1):
                interleave(front(s) if s < G else None,
                           (lambda slot: scan_slot(s - 1, slot)) if s else setup_slot)

        D_STAGE, landed = [], [0, 0]
        for c in range(NCH):
            landed[c % 2] += 16 * (3 if 2 <= c < 2 + E else 1)
            D_STAGE.append(landed[c % 2])

        def chunk_tiles(c):
            if c < 2:
                r = slice(0, A_Q) if c == 0 else slice(A_Q, AW)
                return aw_h[:, r], aw_l[:, r], aw_d[:, r], WS
            if c < 2 + E:
                r = slice(F * (c - 2), F * (c - 1))
                return w1_h[:, r], w1_l[:, r], w1_d[:, r], ES
            r = slice(SC * (c - 2 - E), SC * (c - 1 - E))
            return tuple(t[:, r, :].rearrange("p a b -> p (a b)") for t in (sw_h, sw_l, sw_d)) + (WS,)

        ctx.enter_context(nc.allow_non_contiguous_dma(reason="a few small weight vectors"))
        block = ctx.enter_context(nc.Block())

        @block.sync
        def _(e):
            def load_chunk(c):
                if c >= 2:
                    e.wait_ge(c_hi[c - 2], 2 if c - 2 not in range(2, 2 + E) else 5)
                    e.wait_ge(c_lo[c - 2], 2 if c - 2 not in range(2, 2 + E) else 3)
                if c < 2:
                    src = (w_att0, w_att1)[c]
                elif c < 2 + E:
                    src = w_exp[c - 2, :, :, :]
                else:
                    src = w_scan[c - 2 - E, :, :, :]
                n = src.shape[-1]
                e.dma_start(stage[:, c % 2, :, 0:n], src if c >= 2 else src[:, :, :]).then_inc(d_stage[c % 2], 16)
                if 2 <= c < 2 + E:
                    for r in (64, 96):
                        e.dma_start(b_stage[r:r + 1, c % 2, :], b_exp[c - 2:c - 1, :]).then_inc(d_stage[c % 2], 16)

            def load_x(g, b):
                if b:
                    wait(e, x_lo, g, 2 * b)
                else:
                    again(e, x_lo, g, 2 * GB)
                e.dma_start(x_raw[:, :, :], x_t[g * GB + b, :, :, :]).then_inc(x_in.sem, 16)

            load_chunk(0)
            load_x(0, 0)
            for dst, src in ((tbq_a, tbq_in[0:P, :]), (tbq_r, tbq_in[P:C, :])):
                e.dma_start(dst[:, :], src).then_inc(d_tok, 16)
            e.dma_start(tproj[:, :, :], tproj_in[:, :, :]).then_inc(d_tok, 16)
            e.dma_start(tbv[:, :], tbv_in[:, :]).then_inc(d_tok, 16)
            e.dma_start(rows[:, :, :], rows_in[:, :, :]).then_inc(d_ffn, 16)
            e.dma_start(fwoT_a[:, :], fwo_in[0:P, :]).then_inc(d_ffn, 16)
            e.dma_start(fwoT_r[:, :], fwo_in[P:C, :]).then_inc(d_ffn, 16)
            e.dma_start(fw2_a[:, :], fw2_in[0:P, :]).then_inc(d_ffn, 16)
            e.dma_start(fw2_r[:, :], fw2_in[P:C, :]).then_inc(d_ffn, 16)
            e.dma_start(fb2_a[:, :], fb_in[0:P, 1:2]).then_inc(d_ffn, 16)
            e.dma_start(fb2_r[:, :], fb_in[P:C, 1:2]).then_inc(d_ffn, 16)
            load_chunk(1)
            e.dma_start(featrow[0:64, :], rf_in[:, :]).then_inc(d_small, 16)
            e.dma_start(a_all[:, :], a_in[:, :]).then_inc(d_small, 16)
            e.dma_start(dbias[:, :], dbias_in[:, :]).then_inc(d_small, 16)
            e.dma_start(fw1_a[:, :], fw1_in[0:P, :]).then_inc(d_small, 16)
            e.dma_start(fw1_r[:, :], fw1_in[P:C, :]).then_inc(d_small, 16)
            e.dma_start(fb1_c[:, :], fb_in[0:P, 0:1]).then_inc(d_small, 16)
            load_x(0, 1)
            load_chunk(2)
            load_chunk(3)
            load_x(0, 2)
            load_chunk(4)
            e.dma_start(w2[:, :], w2_in[:, :]).then_inc(d_moe, 16)
            e.dma_start(b2_row[:, :], b2_in[:, :]).then_inc(d_moe, 16)
            e.dma_start(wg_a[:, :], wg_in[0:P, :]).then_inc(d_moe, 16)
            e.dma_start(wg_r[:, :], wg_in[P:C, :]).then_inc(d_moe, 16)
            load_x(0, 3)
            for c in range(5, NCH):
                load_chunk(c)
            for g in range(G):
                if g:
                    for b in range(GB):
                        load_x(g, b)
                    wait(e, f_out, g - 1, 1)
                    e.dma_start(out[GB * (g - 1):GB * g, :, :].rearrange("b p c -> p b c"), k_y[:, :, :]).then_inc(o_out.sem, 16)
            wait(e, f_out, G - 1, 1)
            e.dma_start(out[GB * (G - 1):GB * G, :, :].rearrange("b p c -> p b c"), k_y[:, :, :]).then_inc(o_out.sem, 16)
            e.wait_ge(o_out.sem, 16 * G)

        CHUNK_SLOT = {(0, 1, 5, 9, 12, 17, 22, 28, 33, 38)[c]: c for c in range(NCH)}

        @block.gpsimd
        def _(e):
            tt = e.tensor_tensor
            e.memset(ones[:, :], 1.0).then_inc(c_ones, 1)
            e.memset(ident[:, :], 0.0).then_inc(c_ident, 1)
            e.memset(headmask[:, :], 1.0).then_inc(c_mask, 1)
            e.memset(halfmask[:, :], 1.0).then_inc(c_mask, 1)
            e.memset(pairmask[:, :, :], 1.0).then_inc(c_mask, 1)
            e.wait_ge(c_ident, 1)
            e.affine_select(out=ident[:, :], in_=ident[:, :], compare_op=ALU.not_equal, fill=1.0, base=0,
                            pattern=[[-1, P]], channel_multiplier=1).then_inc(c_ident, 1)
            e.wait_ge(c_mask, 3)
            e.affine_select(out=headmask[:, :], in_=headmask[:, :], compare_op=ALU.is_ge, fill=0.0, base=0,
                            pattern=[[-D, 8]], channel_multiplier=1).then_inc(c_mask, 1)
            e.affine_select(out=pairmask[:, :, :], in_=pairmask[:, :, :], compare_op=ALU.is_ge, fill=0.0, base=0,
                            pattern=[[-M, 2], [0, D + 1]], channel_multiplier=1).then_inc(c_mask, 1)
            e.wait_ge(c_mask, 5)
            e.affine_select(out=headmask[:, :], in_=headmask[:, :], compare_op=ALU.is_ge, fill=0.0, base=D - 1,
                            pattern=[[D, 8]], channel_multiplier=-1).then_inc(c_mask, 1)
            e.affine_select(out=pairmask[:, :, :], in_=pairmask[:, :, :], compare_op=ALU.is_ge, fill=0.0, base=M - 1,
                            pattern=[[M, 2], [0, D + 1]], channel_multiplier=-1).then_inc(c_mask, 1)
            e.wait_ge(c_mask, 7)
            tt(halfmask[:, :], headmask[:, 0:4], headmask[:, 4:8], ALU.add).then_inc(c_mask, 1)
            e.memset(minus_half[:, :], -0.5).then_inc(c_mem, 1)
            e.memset(t_v[:, :, :, 2 * D:VC], 1.0).then_inc(c_mem, 1)
            e.memset(p_v[:, :, :, D:D + 1], 1.0).then_inc(c_mem, 1)
            e.wait_ge(c_mem, 6)

            def split_x(g, b):
                n = b % 2
                wait(e, x_in, g, 16 * (b + 1))
                if b >= 2:
                    wait(e, t_vps, g, b - 1)
                else:
                    again(e, t_vps, g, GB - 1 + b)
                e.tensor_copy(tx_h[:, n, :, :], x_raw[:, :, :]).then_inc(x_hi.sem, 1)
                wait(e, x_hi, g, b + 1)
                tt(tx_l[:, n, :], x_raw[:, 0, :], tx_h[:, n, 0, :], ALU.subtract).then_inc(x_lo.sem, 1)
                tt(tx_e[:, n, :], x_raw[0:CR, 1, :], tx_h[0:CR, n, 1, :], ALU.subtract).then_inc(x_lo.sem, 1)

            def queries(g, b):
                if b:
                    wait(e, t_s, g, b)
                wait(e, t_qmax, g, 2 * b + 1)
                tt(t_qm[:, :, :, :], t_qx[:, :, :].unsqueeze(2).to_broadcast([P, W, 8, NQ]),
                   headmask[:, :].unsqueeze(1).unsqueeze(3).to_broadcast([P, W, 8, NQ]), ALU.mult).then_inc(t_qmask.sem, 1)
                wait(e, t_qmax, g, 2 * b + 2)
                tt(t_qmr[:, :, :, :], t_qxr[:, :, :].unsqueeze(2).to_broadcast([CR, W, 4, NQ]),
                   headmask[0:CR, 0:4].unsqueeze(1).unsqueeze(3).to_broadcast([CR, W, 4, NQ]), ALU.mult).then_inc(t_qmask.sem, 1)

            def rstd(g, k):
                wait(e, ln_aggr, g, GB * (k + 1))
                e.tensor_scalar(ln_ve[:, :], ln_mv[:, :, 1], EPS, None, ALU.add).then_inc(ln_eps.sem, 1)
                wait(e, ln_eps, g, k + 1)
                tt(ln_rs[:, :], ln_ve[:, :], minus_half[:, :], ALU.pow).then_inc(ln_rstd.sem, 1)

            def duplicate(g, k, n):
                wait(e, ln_norm, g, GB * (k + 1))
                e.tensor_copy(xn[:, :, C:C + CR], xn[:, :, P:C]).then_inc(ln_dup.sem, 1)

            def bcast(row):
                return bc[:, row, :].unsqueeze(1).to_broadcast([P, GB, C])

            def front(g):
                split_x(g, 0)
                yield
                split_x(g, 1)
                yield
                queries(g, 0)
                yield
                for b in range(GB):
                    if 1 <= b < GB - 1:
                        split_x(g, b + 1)
                    yield
                    yield
                    if b + 1 < GB:
                        queries(g, b + 1)
                    yield
                    yield
                yield
                yield
                rstd(g, 0)
                yield
                duplicate(g, 0, 0)
                yield
                for _ in range(15):
                    yield
                wait(e, p_att, g, GB)
                e.tensor_copy(p_xa[:, :, C:C + CR], p_xa[:, :, P:C]).then_inc(p_dup.sem, 1)
                wait(e, p_fk, g, GB)
                wait(e, p_fq, g, HP)
                if g == 0:
                    e.wait_ge(c_bcs, 5)
                tt(p_xb[:, :, :], xn[:, :, 0:C], bcast(R_AB), ALU.add).then_inc(p_xbs.sem, 1)
                yield
                yield
                yield
                rstd(g, 1)
                yield
                yield
                wait(e, ln_norm, g, 2 * GB)
                tt(p_y[:, :, :], xn[:, :, 0:C], bcast(R_AG), ALU.mult).then_inc(p_g.sem, 1)
                wait(e, p_g, g, 1)
                tt(p_y[:, :, :], p_y[:, :, :], bcast(R_ABETA), ALU.add).then_inc(p_be.sem, 1)
                wait(e, p_be, g, 1)
                wait(e, t_h, g, GB)
                tt(h[:, g % 2, :, :], h[:, g % 2, :, :], p_y[:, :, :], ALU.add).then_inc(p_h.sem, 1)
                yield
                rstd(g, 2)
                yield
                duplicate(g, 2, 1)
                yield
                for _ in range(7):
                    yield
                rstd(g, 3)
                yield
                duplicate(g, 3, 2)
                yield
                for _ in range(3):
                    yield

            def add_product(g, k):
                half = k // N1
                wait(e, s_pr, g, k + 1)
                if k:
                    wait(e, s_sum, g, k)
                if k in (0, N1):
                    if k == 0:
                        again(e, o_out, g, 16)
                    e.tensor_copy(s_acc[:, half, :], s_p[:, k % NP, :]).then_inc(s_sum.sem, 1)
                else:
                    tt(s_acc[:, half, :], s_acc[:, half, :], s_p[:, k % NP, :], ALU.add).then_inc(s_sum.sem, 1)

            def weigh(g, i):
                wait(e, s_ws, g, i + 1)
                if i == 0:
                    wait(e, s_xc, g, 2)
                if i >= NW:
                    wait(e, s_bx, g, i - NW + 1)
                else:
                    again(e, s_bx, g, NT - NW + 1 + i)
                tt(s_wx[:, i % NW, :], s_w[:, i % NW, :], s_x[:, g % 2, i // N1, :], ALU.mult).then_inc(s_wxs.sem, 1)
                e.memset(s_a[:, i % NA_, :].rearrange("p (b t) -> p b t", t=T)[:, :, 0:1], 0.0).then_inc(s_a0.sem, 1)

            def scan_slot(g, slot):
                i, second = divmod(slot, 2)
                if i < NT:
                    if slot == 0:
                        weigh(g, 0)
                    elif second and i + 1 < NT:
                        weigh(g, i + 1)
                    elif not second:
                        add_product(g, i - 1)
                    return
                tail = slot - 2 * NT
                if tail == 0:
                    add_product(g, NT - 1)
                elif tail in (1, 6):
                    k = int(tail == 6)
                    wait(e, kn_aggr, g, GB * (k + 1))
                    e.tensor_scalar(kn_ve[:, :], kn_mv[:, :, 1], EPS, None, ALU.add).then_inc(kn_eps.sem, 1)
                    wait(e, kn_eps, g, k + 1)
                    tt(kn_rs[:, :], kn_ve[:, :], minus_half[:, :], ALU.pow).then_inc(kn_rstd.sem, 1)
                elif tail == 8:
                    wait(e, kn_norm, g, 2 * GB)
                    tt(k_y[:, :, :], k_xn[:, :, :], bcast(R_FG), ALU.mult).then_inc(f_g.sem, 1)
                    wait(e, f_g, g, 1)
                    tt(k_y[:, :, :], k_y[:, :, :], bcast(R_FBETA), ALU.add).then_inc(f_be.sem, 1)
                    wait(e, f_be, g, 1)
                    wait(e, s_res, g, 2)
                    tt(k_y[:, :, :], h[:, g % 2, :, :], k_y[:, :, :], ALU.add).then_inc(f_out.sem, 1)

            program(front, scan_slot, None)

        @block.scalar
        def _(e):
            act = e.activation

            def setup_slot(slot):
                if slot not in CHUNK_SLOT:
                    return
                c = CHUNK_SLOT[slot]
                w_hi, _, w_d, scale = chunk_tiles(c)
                n = w_hi.shape[-1]
                e.wait_ge(d_stage[c % 2], D_STAGE[c])
                act(w_hi, stage[:, c % 2, 0, 0:n], ACT.Copy, scale=scale).then_inc(c_hi[c], 1)
                act(w_d, stage[:, c % 2, 1, 0:n], ACT.Copy, scale=scale).then_inc(c_hi[c], 1)
                if 2 <= c < 2 + E:
                    r = slice(F * (c - 2), F * (c - 1))
                    e.wait_ge(c_mem, 6)
                    act(w1_e[0:CR, r], stage[0:CR, c % 2, 1, 0:n], ACT.Copy, scale=scale).then_inc(c_hi[c], 1)
                    for p in (64, 96):
                        act(w1_e[p:p + 1, r], b_stage[p:p + 1, c % 2, :], ACT.Copy, scale=scale).then_inc(c_hi[c], 1)

            def evac_qk(g, b, dst_q, dst_k, ps_bank, r, bias, done, made):
                wait(e, made, g, b + 1)
                if b:
                    wait(e, t_qmax, g, 2 * b)
                    wait(e, t_s, g, b)
                for j, dst in enumerate((dst_q, dst_k)):
                    act(dst[:, :, :].rearrange("p w t -> p (w t)"), bank(ps_bank, r, 256 * j, 256 * j + 256), ACT.Identity,
                        bias=bias[:, j:j + 1], scale=1 / WS).then_inc(done.sem, 1)

            def evac_v(g, b):
                wait(e, t_vps, g, b + 1)
                if b >= 2:
                    wait(e, t_ops, g, b - 1)
                else:
                    again(e, t_ops, g, GB - 1 + b)
                act(t_v[:, b % 2, :, 0:2 * D], bank(0, P, 0, W * C).rearrange("p (n d) -> p n d", d=2 * D), ACT.Copy,
                    scale=1 / WS).then_inc(t_vs.sem, 1)

            def hi_parts(g, n, banks):
                q = g % 2
                wait(e, gT, g, n + 1)
                act(x_h[:, q, :], bank(banks[0]), ACT.Copy).then_inc(g_hi.sem, 1)
                act(x_d[:, q, :], bank(banks[1]), ACT.Copy).then_inc(g_hi.sem, 1)

            def front(g):
                q = g % 2
                yield
                if g == 0:
                    e.wait_ge(d_tok, 16 * 4)
                    e.wait_ge(c_mem, 6)
                evac_qk(g, 0, t_qa, t_ka, 0, P, tbq_a, t_ea, t_qka)
                evac_qk(g, 0, t_qr, t_kr, 1, CR, tbq_r, t_er, t_qkr)
                yield
                evac_v(g, 0)
                yield
                for b in range(GB):
                    yield
                    wait(e, t_sub, g, b + 1)
                    act(t_p[:, :, :], t_p[:, :, :], ACT.Exp, scale=D ** -0.5).then_inc(t_exp.sem, 1)
                    if b + 1 < GB:
                        evac_qk(g, b + 1, t_qa, t_ka, 0, P, tbq_a, t_ea, t_qka)
                    yield
                    if b + 1 < GB:
                        evac_qk(g, b + 1, t_qr, t_kr, 1, CR, tbq_r, t_er, t_qkr)
                    for j in range(2):
                        wait(e, t_pT, g, 3 * b + j + 1)
                        if b and j == 0:
                            wait(e, t_ops, g, b)
                        act(t_pt[:, 4 * j:4 * j + 4, :].rearrange("p a b -> p (a b)"), bank(2 + j), ACT.Copy).then_inc(t_pTa.sem, 1)
                    if b + 1 < GB:
                        evac_v(g, b + 1)
                    yield
                    yield
                for _ in range(4):
                    yield
                hi_parts(g, 0, (0, 1))
                yield
                for half in range(2):
                    for j in range(3 * half, 3 * half + 3):
                        wait(e, p_qk, g, j + 1)
                        act(p_f[64:P, j, :], ps[64:P, 2 + j % 3, :], ACT.Square, scale=1 / WS).then_inc(p_sq.sem, 1)
                    yield
                    if half == 0:
                        for j in range(2):
                            wait(e, p_vps, g, j + 1)
                            act(p_v[:, 2 * j:2 * j + 2, :, 0:D],
                                bank(j, P, 0, 2 * C).rearrange("p (b n d) -> p b n d", b=2, n=H), ACT.Copy,
                                scale=1 / WS).then_inc(p_vs.sem, 1)
                        yield
                for j in range(HP):
                    wait(e, p_fq, g, j + 1)
                    act(p_qp[:, j, :], bank(j % 5), ACT.Exp).then_inc(p_eq.sem, 1)
                    if j % 2:
                        yield
                for k in range(9):
                    if k % 2 == 0 and k < 8 or k == 0:
                        b = k // 2
                        wait(e, p_fk, g, b + 1)
                        if b >= 2:
                            wait(e, p_kvp, g, b - 1)
                        n = 1 + 2 * (b % 2)
                        act(p_kp[:, b % 2, :], ps[:, n:n + 2, :].rearrange("p a b -> p (a b)")[:, 0:H * M], ACT.Exp).then_inc(p_ek.sem, 1)
                    yield
                hi_parts(g, 1, (1, 2))
                yield
                for _ in range(6):
                    yield
                hi_parts(g, 2, (0, 1))
                yield
                wait(e, m_st, g, 3)
                act(m_e[:, :, :], m_ls[:, :, :], ACT.Exp).then_inc(m_ex.sem, 1)
                yield
                for b in range(GB):
                    wait(e, m_up, g, b + 1)
                    if b >= 2:
                        wait(e, m_dn, g, b - 1)
                    n = 2 * (b % 2)
                    act(m_h[:, b % 2, 0:512], bank(n), ACT.Gelu, scale=1 / ES).then_inc(m_act.sem, 1)
                    act(m_h[:, b % 2, 512:F], bank(n + 1, P, 0, F - 512), ACT.Gelu, scale=1 / ES).then_inc(m_act.sem, 1)
                    yield
                yield
                yield
                yield
                hi_parts(g, 3, (0, 1))
                yield
                yield
                wait(e, s_zs, g, 2)
                act(s_u[:, :, :], s_z[:, :, :], ACT.Abs).then_inc(s_abs.sem, 1)
                wait(e, s_abs, g, 1)
                act(s_u[:, :, :], s_u[:, :, :], ACT.Exp, scale=-1.0).then_inc(s_exp.sem, 1)
                wait(e, s_exp, g, 1)
                act(s_u[:, :, :], s_u[:, :, :], ACT.Ln, bias=1.0).then_inc(s_ln.sem, 1)
                yield

            def scan_exp(g, i):
                if i >= NA_:
                    wait(e, s_hs, g, i - NA_ + 1)
                elif i == 0:
                    again(e, f_dn, g, 2)
                act(s_a[:, i % NA_, :], s_dt[:, g % 2, i // N1, :], ACT.Exp, scale=a_all[:, i:i + 1]).then_inc(s_as.sem, 1)

            def scan_less(g, i):
                wait(e, s_as, g, i + 1)
                if i >= NW:
                    wait(e, s_wxs, g, i - NW + 1)
                else:
                    again(e, f_g, g, 1)
                act(s_w[:, i % NW, :], s_a[:, i % NA_, :], ACT.Copy, bias=-1.0).then_inc(s_ws.sem, 1)

            def scan_slot(g, slot):
                i, second = divmod(slot, 2)
                tail = slot - 2 * NT
                if slot == 0:
                    wait(e, s_dlt, g, 1)
                    if g == 0:
                        for c in (NCH - 2, NCH - 1):
                            e.wait_ge(c_lo[c], 2)
                    scan_exp(g, 0)
                    scan_exp(g, 1)
                    scan_less(g, 0)
                if i + 1 < NT and not second:
                    scan_less(g, i + 1)
                    if i + 2 < NT:
                        scan_exp(g, i + 2)
                elif tail == 3:
                    wait(e, kT, g, 1)
                    act(k_xa[:, :], bank(7), ACT.Copy).then_inc(kTa.sem, 1)
                elif tail == 4:
                    wait(e, f_up, g, 1)
                    act(f_h[:, :], bank(6), ACT.Relu, bias=fb1_c[:, 0:1]).then_inc(f_rl.sem, 1)

            program(front, scan_slot, setup_slot)

        @block.tensor
        def _(e):
            mm, tr = nc.tensor.matmul, nc.tensor.transpose
            e.wait_ge(d_tok, 16 * 4)
            e.wait_ge(d_ffn, 16 * 7)
            e.wait_ge(c_ones, 1)
            e.wait_ge(c_ident, 2)
            e.wait_ge(c_cols, 3)
            one = ones[0:1, :]
            mm(bank(5, P, 0, C), one, rows[0:1, R_TPROJ, :], start=True, stop=False)
            for s in range(2):
                mm(bank(5, P, 0, C), tbv_b[:, s, :], tproj[:, s, :], start=False, stop=s == 1)
            mm(bank(5, P, C, 2 * C), one, rows[0:1, R_AB, :], start=True, stop=True)
            for n in (0, 1):
                mm(bank(6, P, C * n, C * n + C), one, rows[0:1, 2 + n, :], start=True, stop=True)
                mm(bank(7, P, C * n, C * n + C), one, rows[0:1, 5 + n, :], start=True, stop=True)
            mm(bank(4, P, 0, C), one, rows[0:1, R_FBO, :], start=True, stop=False)
            mm(bank(4, P, 0, C), fb2_ab[:, :], fwoT_a[:, :], start=False, stop=False)
            mm(bank(4, P, 0, C), fb2_rb[:, :], fwoT_r[:, :], start=False, stop=True)
            mm(bank(4, P, C, 2 * C), fw2_a[:, :], fwoT_a[:, :], start=True, stop=False)
            mm(bank(4, P, C, 2 * C), fw2_r[:, :], fwoT_r[:, :], start=False, stop=True).then_inc(c_bcast, 1)

            def split_mm(o, a, b):
                mm(o, a[0], b[0], start=True, stop=False)
                mm(o, a[0], b[1], start=False, stop=False)
                mm(o, a[1], b[0], start=False, stop=False)
                mm(o, a[2], b[2], start=False, stop=False)
                return mm(o, a[3], b[3], start=False, stop=True)

            def weights(c0, n):
                return (aw_h[:, c0:c0 + n], aw_l[:, c0:c0 + n], aw_d[:, c0:c0 + n], aw_d[0:CR, c0:c0 + n])

            def raw_x(b, c0, n):
                k = b % 2
                return (tx_h[:, k, 0, c0:c0 + n], tx_l[:, k, c0:c0 + n], tx_h[:, k, 1, c0:c0 + n], tx_e[:, k, c0:c0 + n])

            def group_x(q, c0, n, rows_=CR):
                return (x_h[:, q, c0:c0 + n], x_l[:, q, c0:c0 + n], x_d[:, q, c0:c0 + n], x_e[0:rows_, q, c0:c0 + n])

            def queries_keys_a(g, b):
                wait(e, x_lo, g, 2 * b + 2)
                if b:
                    wait(e, t_oTs, g, b - 1) if b >= 2 else None
                    wait(e, t_vs, g, b)
                else:
                    again(e, s_xc, g, 1)
                    again(e, g_lo, g, 7)
                split_mm(bank(0, P, 0, 256), weights(0, P), raw_x(b, 0, 256))
                split_mm(bank(0, P, 256, 512), weights(C, P), raw_x(b, 0, 256)).then_inc(t_qka.sem, 1)

            def queries_keys_r(g, b):
                if b >= 2:
                    wait(e, t_h, g, b - 1)
                elif b == 1:
                    wait(e, t_er, g, 2)
                else:
                    again(e, g_lo, g, 8)
                split_mm(bank(1, CR, 0, 256), weights(P, CR), raw_x(b, 0, 256))
                split_mm(bank(1, CR, 256, 512), weights(C + P, CR), raw_x(b, 0, 256)).then_inc(t_qkr.sem, 1)

            def values(g, b):
                wait(e, t_ea, g, 2 * b + 2)
                for w in range(W):
                    last = split_mm(bank(0, P, C * w, C * w + C), raw_x(b, P * w, P), weights(2 * C, C))
                last.then_inc(t_vps.sem, 1)

            def out_transposed(g, b):
                wait(e, t_on, g, 2 * b + 2)
                wait(e, t_vs, g, min(b + 2, GB))
                for w in range(W):
                    last = tr(bank(0, HP * D, P * w, P * w + P), t_o[:, HP * w:HP * w + HP, :].rearrange("p a b -> p (a b)"), ident[:, :])
                last.then_inc(t_oT.sem, 1)

            def out_projected(g, b):
                wait(e, t_oTs, g, b + 1)
                for s in range(2):
                    last = mm(bank(1, P, 0, C), t_ot[:, s, :, :], tproj[:, s, :], start=s == 0, stop=s == 1)
                last.then_inc(t_y.sem, 1)

            def to_channels(src, banks):
                for b in range(GB):
                    tr(bank(banks[0], P, T * b, T * b + T), src[:, b, 0:P], ident[:, :])
                for b in range(GB):
                    last = tr(bank(banks[1], P, T * b, T * b + T), src[:, b, P:C + CR], ident[:, :])
                return last

            def front(g):
                q = g % 2
                h_ = []
                yield
                if g == 0:
                    e.wait_ge(c_lo[0], 2)
                    e.wait_ge(c_hi[0], 2)
                    e.wait_ge(c_bcs, 5)
                queries_keys_a(g, 0)
                queries_keys_r(g, 0)
                yield
                values(g, 0)
                yield
                for b in range(GB):
                    wait(e, t_qmask, g, 2 * b + 2)
                    wait(e, t_er, g, 2 * b + 2)
                    if b:
                        wait(e, t_pTa, g, 2 * b)
                        wait(e, t_pTd, g, b)
                    elif g:
                        again(e, s_zs, g, 2)
                        again(e, m_res, g, GB)
                    for n in range(W * HP):
                        w, j = n // HP, n % HP
                        o = ps[:, 2 + n // 4, P * (n % 4):P * (n % 4) + P]
                        if j < 4:
                            last = mm(o, t_qm[:, w, 2 * j:2 * j + 2, :], t_ka[:, w, :], start=True, stop=True)
                        else:
                            last = mm(o, t_qmr[:, w, 2 * j - 8:2 * j - 6, :], t_kr[:, w, :], start=True, stop=True)
                    last.then_inc(t_s.sem, 1)
                    if b:
                        out_transposed(g, b - 1)
                    yield
                    if b + 1 < GB:
                        if b:
                            wait(e, t_oTs, g, b)
                        queries_keys_a(g, b + 1)
                    if b:
                        out_projected(g, b - 1)
                    yield
                    if b + 1 < GB:
                        if b:
                            wait(e, t_h, g, b)
                        queries_keys_r(g, b + 1)
                    wait(e, t_exp, g, b + 1)
                    for n in range(W * HP):
                        last = tr(ps[:, 2 + n // 4, P * (n % 4):P * (n % 4) + P], t_p[:, n, :], ident[:, :])
                        if n % 4 == 3:
                            last.then_inc(t_pT.sem, 1)
                    if b + 1 < GB:
                        values(g, b + 1)
                    yield
                    wait(e, t_vs, g, b + 1)
                    if b + 1 < GB:
                        wait(e, t_er, g, 2 * b + 4)
                    else:
                        wait(e, t_h, g, b)
                    for n in range(W * HP):
                        if n in (0, 4):
                            wait(e, t_pTa, g, 2 * b + 1 + n // 4)
                        if n == 8:
                            wait(e, t_pTd, g, b + 1)
                        last = mm(bank(1, P, VC * n, VC * n + VC), t_pt[:, n, :], t_v[:, b % 2, n, :], start=True, stop=True)
                    last.then_inc(t_ops.sem, 1)
                    yield
                out_transposed(g, GB - 1)
                yield
                out_projected(g, GB - 1)
                yield
                yield
                yield
                wait(e, ln_dup, g, 1)
                wait(e, t_h, g, GB)
                to_channels(xn, (0, 1)).then_inc(gT.sem, 1)
                yield
                wait(e, g_hi, g, 2)
                wait(e, g_lo, g, 2)
                if g == 0:
                    e.wait_ge(c_lo[1], 2)
                    e.wait_ge(c_hi[1], 2)
                    e.wait_ge(c_feat, 1)
                    e.wait_ge(c_mem, 6)

                def qk_tile(j):
                    if j >= 3:
                        wait(e, p_cp, g, j - 2)
                        wait(e, p_sq, g, j - 2)
                    else:
                        wait(e, t_pTa, g, 2 * GB)
                    split_mm(bank(2 + j % 3), weights(A_Q + P * j, P), group_x(q, 0, GT)).then_inc(p_qk.sem, 1)

                for j in range(3):
                    qk_tile(j)
                yield
                for b in range(GB):
                    last = split_mm(bank(b // 2, P, C * (b % 2), C * (b % 2) + C), group_x(q, T * b, T), weights(A_V, C))
                    if b % 2:
                        last.then_inc(p_vps.sem, 1)
                yield
                for j in range(3, 6):
                    qk_tile(j)
                yield
                for j in range(HP):
                    wait(e, p_cp, g, j // 2 + 1)
                    wait(e, p_sq, g, j // 2 + 1)
                    if j < 2:
                        wait(e, p_vs, g, j + 1)
                    elif j < 5:
                        wait(e, p_cp, g, j + 2)
                        wait(e, p_sq, g, j + 2)
                    else:
                        wait(e, p_eq, g, 1)
                    mm(bank(j % 5), feat[:, 2 * (j % 2):2 * (j % 2) + 2, :], p_f[:, j // 2, :], start=True, stop=True).then_inc(p_fq.sem, 1)
                    if j % 2:
                        yield

                def features_k(b):
                    if b < 2:
                        wait(e, p_eq, g, 3 if b == 0 else 5)
                        wait(e, p_cp, g, 6)
                        wait(e, p_sq, g, 6)
                    else:
                        wait(e, p_ek, g, b - 1)
                    n = 1 + 2 * (b % 2)
                    for j in range(3):
                        last = mm(bank(n + j // 2, P, 256 * (j % 2), 256 * (j % 2) + 256), p_f[:, 3 + j, T * b:T * b + T],
                                  feat[:, :, :], start=True, stop=True)
                    last.then_inc(p_fk.sem, 1)

                features_k(0)
                yield
                for b in range(GB):
                    wait(e, p_ek, g, b + 1)
                    wait(e, p_vs, g, 2)
                    if b:
                        wait(e, p_att, g, b)
                    else:
                        wait(e, p_eq, g, HP)
                    for j in range(HP):
                        last = mm(bank(0, P, 34 * j, 34 * j + 34), p_kp[:, b % 2, P * j:P * j + P],
                                  p_v[:, b, 2 * j:2 * j + 2, :], start=True, stop=True)
                    last.then_inc(p_kvp.sem, 1)
                    if b + 1 < GB:
                        features_k(b + 1)
                    yield
                    wait(e, p_kvs, g, b + 1)
                    for j in range(HP):
                        last = mm(bank(0, P, 256 + 34 * j - 0, 256 + 34 * j + 34), p_qp[:, j, T * b:T * b + T],
                                  p_kv[:, b % 2, j, :], start=True, stop=True)
                    last.then_inc(p_num.sem, 1)
                    yield
                wait(e, p_dup, g, 1)
                wait(e, p_ek, g, GB)
                to_channels(p_xa, (1, 2)).then_inc(gT.sem, 1)
                yield
                wait(e, g_hi, g, 4)
                wait(e, g_lo, g, 4)
                for b in range(GB):
                    last = split_mm(bank(3 + b // 2, P, C * (b % 2), C * (b % 2) + C), group_x(q, T * b, T), weights(A_P, C))
                    if b % 2:
                        last.then_inc(p_pr.sem, 1)
                for _ in range(6):
                    yield
                wait(e, ln_dup, g, 2)
                to_channels(xn, (0, 1)).then_inc(gT.sem, 1)
                yield
                wait(e, m_prod, g, 2)
                wait(e, g_hi, g, 6)
                wait(e, g_lo, g, 6)
                mm(bank(2, P, 0, GB * E), ones[:, :], m_pa[:, :, :], start=True, stop=False)
                mm(bank(2, P, 0, GB * E), ones[0:CR, :], m_pr[:, :, :], start=False, stop=True).then_inc(m_log.sem, 1)
                yield
                wait(e, m_st, g, 7)
                if g == 0:
                    for c in range(2, 2 + E):
                        e.wait_ge(c_lo[c], 3)
                        e.wait_ge(c_hi[c], 5)
                    e.wait_ge(d_moe, 16 * 4)
                    e.wait_ge(c_mem, 6)
                chosen = [e.value_load(m_idx[0:1, b:b + 1], min_val=0, max_val=E - 1) for b in range(GB)]

                def up(b):
                    if b >= 2:
                        wait(e, m_act, g, 2 * (b - 1))
                    for f in range(FT):
                        at = bass.ds(chosen[b] * F + P * f, P)
                        last = split_mm(bank(2 * (b % 2) + f // 4, P, P * (f % 4), P * (f % 4) + P),
                                        (w1_h[:, at], w1_l[:, at], w1_d[:, at], w1_e[:, at]), group_x(q, T * b, T, P))
                    last.then_inc(m_up.sem, 1)

                def down(b):
                    wait(e, m_act, g, 2 * (b + 1))
                    if b:
                        wait(e, m_res, g, b)
                    o = bank(4, P, 0, C)
                    for f in range(FT):
                        mm(o, m_h[:, b % 2, P * f:P * f + P], w2[:, bass.ds(chosen[b] * (FT * C) + C * f, C)],
                           start=f == 0, stop=False)
                    mm(o, one, b2_row[0:1, bass.ds(chosen[b] * C, C)], start=False, stop=True).then_inc(m_dn.sem, 1)

                up(0)
                yield
                for b in range(GB):
                    if b + 1 < GB:
                        up(b + 1)
                    down(b)
                    yield
                yield
                yield
                wait(e, ln_dup, g, 3)
                wait(e, m_act, g, 2 * GB)
                to_channels(xn, (0, 1)).then_inc(gT.sem, 1)
                yield
                wait(e, g_hi, g, 8)
                wait(e, g_lo, g, 8)
                if g == 0:
                    e.wait_ge(c_lo[NCH - 1], 2)
                    e.wait_ge(c_hi[NCH - 1], 2)
                for s in range(2):
                    scan_product(bank(2 + s), 2 * NT + s, q).then_inc(s_dps.sem, 1)
                yield
                yield

            def scan_product(o, n, q):
                return split_mm(o, (sw_h[:, n, :], sw_l[:, n, :], sw_d[:, n, :], sw_d[0:CR, n, :]), group_x(q, 0, GT))

            def scan_b(g, i):
                if i >= 2:
                    wait(e, s_pr, g, i - 1)
                elif i == 0:
                    again(e, f_b, g, 2)
                    again(e, f_rl, g, 1)
                    if g == 0:
                        e.wait_ge(c_bcs, 5)
                        for c in range(2 + E, NCH):
                            e.wait_ge(c_lo[c], 2)
                            e.wait_ge(c_hi[c], 2)
                scan_product(bank(5 + 2 * i % 3), i, g % 2).then_inc(s_bps.sem, 1)

            def scan_c(g, i):
                if i >= 1:
                    wait(e, s_hs, g, i)
                scan_product(bank(5 + (2 * i + 1) % 3), NT + i, g % 2).then_inc(s_cps.sem, 1)

            def scan_slot(g, slot):
                i, second = divmod(slot, 2)
                tail = slot - 2 * NT
                if i < NT and not second:
                    if i == 0:
                        scan_b(g, 0)
                    scan_c(g, i)
                elif i < NT:
                    if i + 1 < NT:
                        scan_b(g, i + 1)
                elif tail == 0:
                    wait(e, s_sum, g, NT)
                    wait(e, s_pr, g, NT)
                    for b in range(GB):
                        o, c = C * (b % 2), slice(T * b, T * b + T)
                        tr(bank(5 + b // 2, P, o, o + P), s_acc[:, 0, c], ident[:, :])
                        last = mm(bank(5 + b // 2, P, o + P, o + C), s_acc[:, 1, c], fold[:, :], start=True, stop=True)
                        if b % 2:
                            last.then_inc(s_yT.sem, 1)
                elif tail == 3:
                    wait(e, kn_norm, g, GB)
                    for b in range(GB):
                        tr(bank(7, P, T * b, T * b + T), k_xn[:, b, 0:P], ident[:, :])
                    for b in range(GB):
                        last = tr(bank(5, CR, T * b, T * b + T), k_xn[:, b, P:C], ident[:, :])
                    last.then_inc(kT.sem, 1)
                elif tail == 4:
                    wait(e, kTa, g, 1)
                    wait(e, kTr, g, 1)
                    mm(bank(6), fw1_a[:, :], k_xa[:, :], start=True, stop=False)
                    mm(bank(6), fw1_r[:, :], k_xr[:, :], start=False, stop=True).then_inc(f_up.sem, 1)
                elif tail == 5:
                    wait(e, f_rl, g, 1)
                    for b in range(GB):
                        last = mm(bank((7, 5)[b // 2], P, C * (b % 2), C * (b % 2) + C), f_h[:, T * b:T * b + T], fw21[:, :],
                                  start=True, stop=True)
                        if b % 2:
                            last.then_inc(f_dn.sem, 1)

            program(front, scan_slot, None)

        @block.vector
        def _(e):
            tt, ts, stt = e.tensor_tensor, e.tensor_scalar, e.scalar_tensor_tensor
            e.memset(featrow[64:P, :], -0.5).then_inc(c_mem, 1)
            e.memset(w1_e[64:P, :], 0.0).then_inc(c_mem, 1)
            e.memset(x_e[64:P, :, :], 1.0).then_inc(c_mem, 1)
            e.wait_ge(d_tok, 16 * 4)
            e.wait_ge(d_ffn, 16 * 7)
            e.wait_ge(c_ones, 1)
            tt(tbv_b[:, :, :], tbv[:, :].unsqueeze(2).to_broadcast([HP * D, 2, P]),
               ones[0:HP * D, :].unsqueeze(1).to_broadcast([HP * D, 2, P]), ALU.mult).then_inc(c_cols, 1)
            ts(fb2_ab[:, :], ones[:, :], fb2_a[:, 0:1], None, ALU.mult).then_inc(c_cols, 1)
            ts(fb2_rb[:, :], ones[0:CR, :], fb2_r[:, 0:1], None, ALU.mult).then_inc(c_cols, 1)
            e.wait_ge(c_ident, 2)
            tt(fold[:, :], ident[:, 0:CR], ident[:, CR:P], ALU.add).then_inc(c_ra, 1)
            e.wait_ge(d_small, 16 * 6)
            e.wait_ge(c_mask, 8)
            e.wait_ge(c_mem, 6)
            ts(ra_all[:, :], a_all[:, :], WS, None, ALU.mult).then_inc(c_ra, 1)
            tt(feat[:, :, :], featrow[:, :].unsqueeze(1).to_broadcast([P, 4, M]),
               halfmask[:, :].unsqueeze(2).to_broadcast([P, 4, M]), ALU.mult).then_inc(c_feat, 1)
            e.wait_ge(c_ra, 2)
            e.reciprocal(ra_all[:, :], ra_all[:, :]).then_inc(c_ra, 1)
            e.wait_ge(c_bcast, 1)
            e.tensor_copy(bc[:, 0:2, :], bank(5, P, 0, 2 * C)).then_inc(c_bcs, 1)
            e.tensor_copy(bc[:, 2:4, :], bank(6, P, 0, 2 * C)).then_inc(c_bcs, 1)
            e.tensor_copy(bc[:, 5:7, :], bank(7, P, 0, 2 * C)).then_inc(c_bcs, 1)
            e.tensor_copy(bc[:, R_FBO, :], bank(4, P, 0, C)).then_inc(c_bcs, 1)
            e.tensor_copy(fw21[:, :], bank(4, P, C, 2 * C)).then_inc(c_bcs, 1)
            e.wait_ge(c_bcs, 5)
            e.wait_ge(c_ra, 3)

            def setup_slot(slot):
                if slot not in CHUNK_SLOT:
                    return
                c = CHUNK_SLOT[slot]
                w_hi, w_lo, w_d, scale = chunk_tiles(c)
                n = w_hi.shape[-1]
                e.wait_ge(d_stage[c % 2], D_STAGE[c])
                e.wait_ge(c_hi[c], 2 if not 2 <= c < 2 + E else 5)
                stt(out=w_lo, in0=stage[:, c % 2, 0, 0:n], scalar=scale, in1=w_hi, op0=ALU.mult, op1=ALU.subtract).then_inc(c_lo[c], 1)
                stt(out=w_d[64:P], in0=stage[64:P, c % 2, 1, 0:n], scalar=scale, in1=w_d[64:P], op0=ALU.mult,
                    op1=ALU.subtract).then_inc(c_lo[c], 1)
                if 2 <= c < 2 + E:
                    r = slice(F * (c - 2), F * (c - 1))
                    stt(out=w1_e[96:97, r], in0=b_stage[96:97, c % 2, :], scalar=scale, in1=w1_e[96:97, r],
                        op0=ALU.mult, op1=ALU.subtract).then_inc(c_lo[c], 1)

            def ln_moments(g, k, src, st, mv, stats, aggr, ready):
                for b in range(GB):
                    ready(b)
                    e.bn_stats(st[:, b, :], src[:, b, :]).then_inc(stats.sem, 1)
                for b in range(GB):
                    wait(e, stats, g, GB * k + b + 1)
                    e.bn_aggr(mv[:, b, :], st[:, b, :]).then_inc(aggr.sem, 1)

            def ln_apply(g, k, dst, src, mv, rs, aggr, rstd, norm):
                wait(e, aggr, g, GB * (k + 1))
                wait(e, rstd, g, k + 1)
                for b in range(GB):
                    ts(dst[:, b, 0:C], src[:, b, :], mv[:, b, 0:1], rs[:, b:b + 1], ALU.subtract, ALU.mult).then_inc(norm.sem, 1)

            def moments(g, k, src, ready):
                ln_moments(g, k, src, ln_st, ln_mv, ln_stats, ln_aggr, ready)

            def apply(g, k, src):
                ln_apply(g, k, xn, src, ln_mv, ln_rs, ln_aggr, ln_rstd, ln_norm)

            def lo_parts(g, n, banks):
                q = g % 2
                wait(e, g_hi, g, 2 * n + 2)
                tt(x_l[:, q, :], bank(banks[0]), x_h[:, q, :], ALU.subtract).then_inc(g_lo.sem, 1)
                tt(x_e[0:CR, q, :], bank(banks[1], CR), x_d[0:CR, q, :], ALU.subtract).then_inc(g_lo.sem, 1)

            def query_max(g, b):
                if b:
                    wait(e, t_qmask, g, 2 * b)
                wait(e, t_ea, g, 2 * b + 2)
                tt(t_qx[:, :, :], t_qa[:, :, 0:NQ], t_qa[:, :, NQ:P], ALU.max).then_inc(t_qmax.sem, 1)
                wait(e, t_er, g, 2 * b + 2)
                tt(t_qxr[:, :, :], t_qr[:, :, 0:NQ], t_qr[:, :, NQ:P], ALU.max).then_inc(t_qmax.sem, 1)

            def transposed_out(g, b):
                wait(e, t_oT, g, b + 1)
                e.tensor_copy(t_ot[:, :, :, :].rearrange("p s w q -> p w s q"),
                              bank(0, HP * D, 0, W * P).rearrange("p (w s q) -> p w s q", w=W, s=2)).then_inc(t_oTs.sem, 1)

            def pooled(g, b):
                wait(e, t_y, g, b + 1)
                if b == 0:
                    again(e, f_out, g, 1, back=2)
                tt(h[:, g % 2, b, :], bank(1, P, 0, C), bc[:, R_TPROJ, :], ALU.add).then_inc(t_h.sem, 1)

            def front(g):
                q = g % 2
                hg = h[:, q, :, :]
                yield
                query_max(g, 0)
                yield
                yield
                for b in range(GB):
                    wait(e, t_s, g, b + 1)
                    scores = ps[:, 2:5, :].rearrange("p a (b c) -> p (a b) c", c=P)
                    e.reduce_max(t_mx[:, :], scores, AX.X).then_inc(t_max.sem, 1)
                    wait(e, t_max, g, b + 1)
                    if b:
                        wait(e, t_pT, g, 3 * b)
                    tt(t_p[:, :, :], scores, t_mx[:, :].unsqueeze(2).to_broadcast([P, W * HP, P]), ALU.subtract).then_inc(t_sub.sem, 1)
                    if b:
                        transposed_out(g, b - 1)
                    yield
                    if b:
                        pooled(g, b - 1)
                    yield
                    if b + 1 < GB:
                        query_max(g, b + 1)
                    wait(e, t_pT, g, 3 * b + 3)
                    if b:
                        wait(e, t_ops, g, b)
                    e.tensor_copy(t_pt[:, 8:12, :].rearrange("p a b -> p (a b)"), bank(4)).then_inc(t_pTd.sem, 1)
                    yield
                    wait(e, t_ops, g, b + 1)
                    o = bank(1, P, 0, W * HP * VC).rearrange("p (n c) -> p n c", c=VC)
                    e.reciprocal(t_rd[:, :], o[:, :, 2 * D]).then_inc(t_rden.sem, 1)
                    wait(e, t_rden, g, b + 1)
                    if b:
                        wait(e, t_oT, g, b)
                    for s in range(2):
                        r = slice(64 * s, 64 * s + 64)
                        tt(t_o[r, :, :], o[r, :, D * s:D * s + D], t_rd[r, :].unsqueeze(2).to_broadcast([64, W * HP, D]),
                           ALU.mult).then_inc(t_on.sem, 1)
                    yield
                transposed_out(g, GB - 1)
                yield
                pooled(g, GB - 1)
                yield
                moments(g, 0, hg, lambda b: wait(e, t_h, g, b + 1))
                yield
                apply(g, 0, hg)
                yield
                lo_parts(g, 0, (0, 1))
                yield
                for half in range(2):
                    for j in range(3 * half, 3 * half + 3):
                        wait(e, p_qk, g, j + 1)
                        ts(p_f[0:64, j, :], ps[0:64, 2 + j % 3, :], 1 / WS, None, ALU.mult).then_inc(p_cp.sem, 1)
                    yield
                    if half == 0:
                        yield
                for _ in range(4):
                    yield
                for b in range(GB):
                    wait(e, p_kvp, g, b + 1)
                    if b >= 2:
                        wait(e, p_num, g, b - 1)
                    tt(p_kv[:, b % 2, :, :], bank(0, P, 0, 204).rearrange("p (j c) -> p j c", c=34),
                       pairmask[:, :, :].rearrange("p a b -> p (a b)").unsqueeze(1).to_broadcast([P, HP, 34]),
                       ALU.mult).then_inc(p_kvs.sem, 1)
                    yield
                    wait(e, p_num, g, b + 1)
                    num = bank(0, P, 256, 460).rearrange("p (n c) -> p n c", c=D + 1)
                    ts(p_n[:, b % 2, :], num[:, :, D], M * 1e-6, None, ALU.add).then_inc(p_den.sem, 1)
                    wait(e, p_den, g, b + 1)
                    e.reciprocal(p_r[:, b % 2, :], p_n[:, b % 2, :]).then_inc(p_rec.sem, 1)
                    wait(e, p_rec, g, b + 1)
                    tt(p_xa[:, b, 0:C].rearrange("p (n d) -> p n d", n=H), num[:, :, 0:D],
                       p_r[:, b % 2, :].unsqueeze(2).to_broadcast([P, H, D]), ALU.mult).then_inc(p_att.sem, 1)
                    yield
                lo_parts(g, 1, (1, 2))
                yield
                wait(e, p_xbs, g, 1)
                for j in range(2):
                    wait(e, p_pr, g, j + 1)
                    stt(out=p_y[:, 2 * j:2 * j + 2, :], in0=bank(3 + j, P, 0, 2 * C).rearrange("p (b c) -> p b c", b=2),
                        scalar=1 / WS, in1=p_xb[:, 2 * j:2 * j + 2, :], op0=ALU.mult, op1=ALU.add).then_inc(p_ys.sem, 1)
                yield
                moments(g, 1, p_y, lambda b: wait(e, p_ys, g, b // 2 + 1))
                yield
                apply(g, 1, p_y)
                yield
                yield
                moments(g, 2, hg, lambda b: wait(e, p_h, g, 1))
                yield
                apply(g, 2, hg)
                yield
                wait(e, g_hi, g, 6)
                if g == 0:
                    e.wait_ge(d_moe, 16 * 4)
                e.reduce_sum(m_ma[:, :], bank(0).rearrange("p (b t) -> p b t", b=GB), AX.X).then_inc(m_mean.sem, 1)
                e.reduce_sum(m_mr[:, :], bank(1, CR).rearrange("p (b t) -> p b t", b=GB), AX.X).then_inc(m_mean.sem, 1)
                wait(e, m_mean, g, 2)
                for o, a, wg, r in ((m_pa, m_ma, wg_a, P), (m_pr, m_mr, wg_r, CR)):
                    tt(o[:, :, :], a[:, :].unsqueeze(2).to_broadcast([r, GB, E]), wg[:, :].unsqueeze(1).to_broadcast([r, GB, E]),
                       ALU.mult).then_inc(m_prod.sem, 1)
                lo_parts(g, 2, (0, 1))
                yield
                wait(e, m_log, g, 1)
                ts(m_l[:, :, :], bank(2, P, 0, GB * E).rearrange("p (b x) -> p b x", b=GB), 1.0 / T, None, ALU.mult).then_inc(m_st.sem, 1)
                wait(e, m_st, g, 1)
                e.reduce_max(m_mx[:, :], m_l[:, :, :], AX.X).then_inc(m_st.sem, 1)
                wait(e, m_st, g, 2)
                tt(m_ls[:, :, :], m_l[:, :, :], m_mx[:, :].unsqueeze(2).to_broadcast([P, GB, E]), ALU.subtract).then_inc(m_st.sem, 1)
                wait(e, m_st, g, 3)
                ts(m_eq[:, :, :], m_ls[:, :, :], 0.0, None, ALU.is_equal).then_inc(m_st.sem, 1)
                wait(e, m_st, g, 4)
                ts(m_t[:, 0, :], m_eq[:, :, 0], -1.0, 1.0, ALU.mult, ALU.add).then_inc(m_st.sem, 1)
                ts(m_t[:, 1, :], m_eq[:, :, 1], -1.0, 2.0, ALU.mult, ALU.add).then_inc(m_st.sem, 1)
                wait(e, m_st, g, 6)
                tt(m_idx[:, :], m_t[:, 0, :], m_t[:, 1, :], ALU.mult).then_inc(m_st.sem, 1)
                yield
                wait(e, m_ex, g, 1)
                e.reduce_sum(m_sum[:, :], m_e[:, :, :], AX.X).then_inc(m_st.sem, 1)
                wait(e, m_st, g, 8)
                e.reciprocal(m_w[:, :], m_sum[:, :]).then_inc(m_st.sem, 1)
                yield
                for b in range(GB):
                    wait(e, m_st, g, 9)
                    wait(e, m_dn, g, b + 1)
                    stt(out=h[:, q, b, :], in0=bank(4, P, 0, C), scalar=m_w[:, b:b + 1], in1=h[:, q, b, :],
                        op0=ALU.mult, op1=ALU.add).then_inc(m_res.sem, 1)
                    yield
                moments(g, 3, hg, lambda b: wait(e, m_res, g, b + 1))
                yield
                apply(g, 3, hg)
                yield
                wait(e, g_hi, g, 8)
                e.tensor_copy(s_x[:, q, 0, :], bank(0)).then_inc(s_xc.sem, 1)
                e.tensor_copy(s_x[:, q, 1, :], bank(1)).then_inc(s_xc.sem, 1)
                lo_parts(g, 3, (0, 1))
                yield
                for s in range(2):
                    wait(e, s_dps, g, s + 1)
                    ts(s_z[:, s, :], bank(2 + s), 1.0 / WS, dbias[:, s:s + 1], ALU.mult, ALU.add).then_inc(s_zs.sem, 1)
                yield
                wait(e, s_ln, g, 1)
                wait(e, s_zs, g, 2)
                stt(out=s_dt[:, q, :, :], in0=s_z[:, :, :], scalar=0.0, in1=s_u[:, :, :], op0=ALU.max, op1=ALU.add).then_inc(s_dlt.sem, 1)
                yield

            def tile_bx(g, i):
                wait(e, s_bps, g, i + 1)
                wait(e, s_wxs, g, i + 1)
                b_ps = bank(5 + 2 * i % 3)
                stt(out=b_ps, in0=b_ps, scalar=ra_all[:, i:i + 1], in1=s_wx[:, i % NW, :], op0=ALU.mult,
                    op1=ALU.mult).then_inc(s_bx.sem, 1)

            def tile_product(g, k):
                wait(e, s_hs, g, k + 1)
                wait(e, s_cps, g, k + 1)
                if k >= NP:
                    wait(e, s_sum, g, k - NP + 1)
                stt(out=s_p[:, k % NP, :], in0=bank(5 + (2 * k + 1) % 3), scalar=1.0 / WS, in1=s_h[:, k % NH, :],
                    op0=ALU.mult, op1=ALU.mult).then_inc(s_pr.sem, 1)

            def tile_scan(g, i):
                wait(e, s_bx, g, i + 1)
                wait(e, s_a0, g, i + 1)
                e.tensor_tensor_scan(s_h[:, i % NH, :], s_a[:, i % NA_, :], bank(5 + 2 * i % 3), 0.0, ALU.mult, ALU.add).then_inc(s_hs.sem, 1)

            def scan_slot(g, slot):
                hg = h[:, g % 2, :, :]
                i, second = divmod(slot, 2)
                tail = slot - 2 * NT
                if i < NT and not second:
                    tile_bx(g, i)
                    if i == 0:
                        again(e, s_sum, g, NT)
                    tile_scan(g, i)
                elif i < NT:
                    tile_product(g, i)
                elif tail == 0:
                    for j in range(2):
                        wait(e, s_yT, g, j + 1)
                        tt(hg[:, 2 * j:2 * j + 2, :], hg[:, 2 * j:2 * j + 2, :],
                           bank(5 + j, P, 0, 2 * C).rearrange("p (b c) -> p b c", b=2), ALU.add).then_inc(s_res.sem, 1)
                elif tail == 1:
                    ln_moments(g, 0, hg, kn_st, kn_mv, kn_stats, kn_aggr, lambda b: wait(e, s_res, g, b // 2 + 1))
                elif tail == 2:
                    ln_apply(g, 0, k_xn, hg, kn_mv, kn_rs, kn_aggr, kn_rstd, kn_norm)
                elif tail == 3:
                    wait(e, kT, g, 1)
                    e.tensor_copy(k_xr[:, :], bank(5, CR)).then_inc(kTr.sem, 1)
                elif tail == 5:
                    for j in range(2):
                        wait(e, f_dn, g, j + 1)
                        tt(k_y[:, 2 * j:2 * j + 2, :], bank((7, 5)[j], P, 0, 2 * C).rearrange("p (b c) -> p b c", b=2),
                           bc[:, R_FBO, :].unsqueeze(1).to_broadcast([P, 2, C]), ALU.add).then_inc(f_b.sem, 1)
                elif tail == 6:
                    ln_moments(g, 1, k_y, kn_st, kn_mv, kn_stats, kn_aggr, lambda b: wait(e, f_b, g, b // 2 + 1))
                elif tail == 7:
                    ln_apply(g, 1, k_xn, k_y, kn_mv, kn_rs, kn_aggr, kn_rstd, kn_norm)

            program(front, scan_slot, setup_slot)


def kernel(**inputs):
    import numpy as np
    import concourse.bacc as _bacc
    from concourse import mybir as _mybir
    from concourse.bass_utils import run_bass_kernel_spmd as _run

    a = {n: np.asarray(v) for n, v in inputs.items()}

    def lay(w):
        return np.stack([w[..., :P, :], np.concatenate([w[..., P:, :], w[..., P:, :]], axis=-2)], axis=-2)

    x_t = a['x'].reshape(NB, P, W, C).transpose(0, 3, 2, 1).reshape(NB, C, NRAW)
    wq = a['L0_attn_W_qkv']
    att1 = [wq[:, C * s + 64 * t:C * s + 64 * t + 64] for s in range(2) for t in range(3) for _ in range(2)]

    def scan_tiles(w):
        w = w.reshape(C, N, C)
        return np.concatenate([w[:P].transpose(1, 0, 2),
                               w[P:].reshape(CR, N2, 2, C).transpose(1, 2, 0, 3).reshape(N2, P, C)], axis=0)

    wd = a['L1_attn_W_delta']
    tiles = np.concatenate([scan_tiles(a['L1_attn_W_B']), scan_tiles(a['L1_attn_W_C']), wd[None, :P],
                            np.concatenate([wd[P:], wd[P:]])[None]])
    w_scan = tiles.reshape(NS // SC, SC, P, C).transpose(0, 3, 1, 2).reshape(NS // SC, C, SC * P)
    A = a['L1_attn_A']
    tb = a['L0_tok_bqkv'].reshape(3, C)
    ins = {
        'x_t': lay(x_t),
        'w_att0': lay(a['L0_tok_Wqkv']),
        'w_att1': lay(np.concatenate(att1 + [wq[:, 2 * C:], a['L0_attn_W_proj']], axis=1)),
        'w_exp': lay(a['L0_ffn_W1']),
        'b_exp': a['L0_ffn_b1'],
        'w_scan': lay(w_scan),
        'tproj': a['L0_tok_Wproj'].reshape(HP, 2, D, C).transpose(0, 2, 1, 3).reshape(HP * D, 2, C),
        'tbq': tb[0:2].T,
        'tbv': tb[2].reshape(HP, 2, D).transpose(0, 2, 1).reshape(HP * D, 2),
        'rows': np.stack([a[n] for n in ('L0_tok_bproj', 'L0_attn_b_proj', 'L0_attn_gamma', 'L0_attn_beta',
                                         'L1_ffn_bo', 'L1_ffn_gamma', 'L1_ffn_beta')])[None],
        'rf': np.concatenate([a['L0_attn_random_features'].T] * 4),
        'wg': a['L0_ffn_Wg'].T,
        'w2': a['L0_ffn_W2'].reshape(E, FT, P, C).transpose(2, 0, 1, 3).reshape(P, E * FT * C),
        'b2': a['L0_ffn_b2'].reshape(1, E * C),
        'a': np.concatenate([A[:P], A[P:].reshape(CR, N2, 2).transpose(2, 0, 1).reshape(P, N2)], axis=1),
        'dbias': np.stack([a['L1_attn_delta_bias'][:P], np.concatenate([a['L1_attn_delta_bias'][P:]] * 2)], axis=1),
        'fw1': a['L1_ffn_W1'].T,
        'fw2': a['L1_ffn_W2'],
        'fwo': a['L1_ffn_Wo'].T,
        'fb': np.stack([np.concatenate([a['L1_ffn_b1'], a['L1_ffn_b1'][:CR]]), a['L1_ffn_b2']], axis=1),
    }
    nc = _bacc.Bacc("TRN2", target_bir_lowering=False, num_devices=1)
    arrays, args = {}, []
    for name, v in ins.items():
        v = np.ascontiguousarray(v)
        arrays[f"in_{name}_dram"] = v
        args.append(nc.dram_tensor(f"in_{name}_dram", v.shape, _mybir.dt.from_np(v.dtype), kind="ExternalInput").ap())
    args.append(nc.dram_tensor("out_0_dram", (NB, T, C), _mybir.dt.float32, kind="ExternalOutput").ap())
    tower(nc, *args)
    r = _run(nc, [arrays], core_ids=[0])
    return r.results[0]["out_0_dram"]
```

```python
from contextlib import ExitStack

import concourse.bass as bass
from concourse import mybir

fp32 = mybir.dt.float32
fp16 = mybir.dt.float16
i32 = mybir.dt.int32
ALU = mybir.AluOpType
ACT = mybir.ActivationFunctionType
AX = mybir.AxisListType

NB, NRAW, C = 16, 256, 192
P = 128
CR = C - P
W, NQ = 2, 64
T = W * NQ
H, D = 12, 16
HP = H // 2
VC = 2 * D + 1
M = 64
E, F = 3, 768
FT = F // P
N = 16
I = 128
GB = 4
G = NB // GB
GT = GB * T
N1, N2 = N, N // 2
NT = N1 + N2
NS = 2 * NT + 2
EPS = 1e-5
WS = 32.0
ES = 64.0
AW = 3 * C + 6 * P + C + C
A_Q, A_V, A_P = 3 * C, 3 * C + 6 * P, 3 * C + 6 * P + C
STG = 1280
SC = STG // P
NCH = 2 + E + NS // SC

ROWS = 7
R_TPROJ, R_AB, R_AG, R_ABETA, R_FBO, R_FG, R_FBETA = range(ROWS)


class Signal:

    def __init__(self, sem, per):
        self.sem, self.per = sem, per


def wait(e, signal, g, k):
    assert 1 <= k <= signal.per, k
    e.wait_ge(signal.sem, g * signal.per + k)


def again(e, signal, g, k, back=1):
    assert 1 <= k <= signal.per, k
    if g >= back:
        e.wait_ge(signal.sem, (g - back) * signal.per + k)


def tower(nc, x_t, w_att0, w_att1, w_exp, b_exp, w_scan, tproj_in, tbq_in, tbv_in, rows_in, rf_in, wg_in, w2_in, b2_in,
          a_in, dbias_in, fw1_in, fw2_in, fwo_in, fb_in, out):
    ctx = ExitStack()
    with ctx:
        def sb(name, shape, dt=fp32):
            return ctx.enter_context(nc.sbuf_tensor(name, shape, dt))

        def once(name):
            return ctx.enter_context(nc.semaphore(name))

        def signal(name, per):
            return Signal(ctx.enter_context(nc.semaphore(name)), per)

        ident = sb("ident", [P, P])
        ones = sb("ones", [P, P])
        fold = sb("fold", [P, CR])
        headmask = sb("headmask", [P, 8])
        halfmask = sb("halfmask", [P, 4])
        pairmask = sb("pairmask", [P, 2, D + 1])
        feat = sb("feat", [P, 4, M])
        featrow = sb("featrow", [P, M])
        tbq_a, tbq_r = sb("tbq_a", [P, 2]), sb("tbq_r", [P, 1])
        tbv = sb("tbv", [HP * D, 2])
        tproj = sb("tproj", [HP * D, 2, C])
        bc = sb("bc", [P, ROWS, C])
        aw_h, aw_l = sb("aw_h", [P, AW], fp16), sb("aw_l", [P, AW], fp16)
        aw_d = sb("aw_d", [P, AW], fp16)
        wg_a, wg_r = sb("wg_a", [P, E]), sb("wg_r", [CR, E])
        w1_h, w1_l = sb("w1_h", [P, E * F], fp16), sb("w1_l", [P, E * F], fp16)
        w1_d = sb("w1_d", [P, E * F], fp16)
        w1_e = sb("w1_e", [P, E * F], fp16)
        b2_row = sb("b2_row", [1, E * C])
        w2 = sb("w2", [P, E * FT * C])
        sw_h, sw_l = sb("sw_h", [P, NS, P], fp16), sb("sw_l", [P, NS, P], fp16)
        sw_d = sb("sw_d", [P, NS, P], fp16)
        a_all, ra_all = sb("a_all", [P, NT]), sb("ra_all", [P, NT])
        dbias = sb("dbias", [P, 2])
        fw1_a, fw1_r = sb("fw1_a", [P, I]), sb("fw1_r", [CR, I])
        fw21 = sb("fw21", [I, C])
        fb1_c = sb("fb1_c", [I, 1])
        minus_half = sb("minus_half", [P, GB])

        h = sb("h", [P, 3, GB, C])
        x_h, x_l = sb("x_h", [P, 2, GT], fp16), sb("x_l", [P, 2, GT], fp16)
        x_d = sb("x_d", [P, 2, GT], fp16)
        x_e = sb("x_e", [P, 2, GT], fp16)
        s_x, s_dt = sb("s_x", [P, 2, GT]), sb("s_dt", [P, 2, GT])

        xn = sb("xn", [P, GB, C + CR])
        ln_st, ln_mv = sb("ln_st", [P, GB, 6]), sb("ln_mv", [P, GB, 2])
        ln_ve, ln_rs = sb("ln_ve", [P, GB]), sb("ln_rs", [P, GB])
        x_raw = sb("x_raw", [P, 2, NRAW])
        tx_h = sb("tx_h", [P, 2, 2, NRAW], fp16)
        tx_l, tx_e = sb("tx_l", [P, 2, NRAW], fp16), sb("tx_e", [CR, 2, NRAW], fp16)
        t_vh, t_vl = sb("t_vh", [P, 2, W * HP, VC], fp16), sb("t_vl", [P, 2, W * HP, VC], fp16)
        p_v = sb("p_v", [P, GB, H, D + 1])

        def carve(arena, layout):
            at, views = 0, []
            for rows_, *dims in layout:
                n = 1
                for d in dims:
                    n *= d
                v = arena[0:rows_, at:at + n]
                if len(dims) == 2:
                    v = v.rearrange("p (a b) -> p a b", b=dims[1])
                elif len(dims) == 3:
                    v = v.rearrange("p (a b c) -> p a b c", b=dims[1], c=dims[2])
                views.append(v)
                at += n
            return views

        t_qa, t_ka = sb("t_qa", [P, W, P]), sb("t_ka", [P, W, P])
        t_qr, t_kr = sb("t_qr", [CR, W, P]), sb("t_kr", [CR, W, P])
        t_qx, t_qxr = t_qa[:, :, 0:NQ], t_qr[:, :, 0:NQ]
        t_qm, t_qmr = sb("t_qm", [P, W, 8, NQ]), sb("t_qmr", [CR, W, 4, NQ])
        t_mx, t_rd = sb("t_mx", [P, W * HP]), sb("t_rd", [P, W * HP])
        t_p = sb("t_p", [P, W * HP, P])
        t_pt = [t_p[:, 4 * c:4 * c + 4, :].rearrange("p a b -> p (a b)").bitcast(fp16) for c in range(3)]
        t_o, t_ot = sb("t_o", [P, W * HP, D]), sb("t_ot", [HP * D, 2, W, NQ])
        KV = HP * 2 * (D + 1)
        arena = sb("arena", [P, (6 + HP) * GT + 2 * H * M + 2 * KV + 2 * GB * H])
        p_f, p_qp, p_kp, p_kv1, p_n, p_r = carve(arena, [
            (P, 6, GT), (P, HP, GT), (P, 2, H * M), (P, 2, HP, 2 * (D + 1)), (P, GB, H), (P, GB, H)])
        p_kv0, = carve(arena, [(P, 2, HP, 2 * (D + 1))])
        p_y, p_xb = carve(arena, [(P, GB, C), (P, GB, C)])
        p_kv = [p_kv0[:, 0, :, :], p_kv0[:, 1, :, :], p_kv1[:, 0, :, :], p_kv1[:, 1, :, :]]
        m_h, s_z, s_u = carve(arena, [(P, 2, F), (P, 2, GT), (P, 2, GT)])
        m_ma, m_mr = sb("m_ma", [P, GB]), sb("m_mr", [CR, GB])
        m_pa, m_pr = sb("m_pa", [P, GB, E]), sb("m_pr", [CR, GB, E])
        m_l, m_ls, m_e, m_eq = (sb(f"m_{n}", [P, GB, E]) for n in ("l", "ls", "e", "eq"))
        m_mx, m_sum, m_w = sb("m_mx", [P, GB]), sb("m_sum", [P, GB]), sb("m_w", [P, GB])
        m_t = sb("m_t", [P, 2, GB])
        m_idx = sb("m_idx", [P, GB], i32)

        NA_, NW, NH = 3, 3, 3
        scan_arena = sb("scan_arena", [P, (NA_ + NW + NH + 2) * GT])
        s_a, s_w, s_h, s_acc = carve(scan_arena, [(P, NA_, GT), (P, NW, GT), (P, NH, GT), (P, 2, GT)])
        stage, = carve(scan_arena, [(P, 2, 2, STG)])
        rows, fwoT_a, fwoT_r, fw2_a, fw2_r, tbv_b, fb2_a, fb2_r, fb2_ab, fb2_rb, b_stage = carve(arena, [
            (1, ROWS, C), (P, C), (CR, C), (P, I), (CR, I), (HP * D, 2, P), (P, 1), (CR, 1), (P, P), (CR, P), (P, 2, F)])
        k_xa, k_xr, f_h, k_xn = carve(scan_arena, [(P, GT), (CR, GT), (I, GT), (P, GB, C)])
        k_y = s_acc[:, :, :].rearrange("p a b -> p (a b)")[:, 0:GB * C].rearrange("p (b c) -> p b c", b=GB)
        kn_st, kn_mv = sb("kn_st", [P, GB, 6]), sb("kn_mv", [P, GB, 2])
        kn_ve, kn_rs = sb("kn_ve", [P, GB]), sb("kn_rs", [P, GB])

        ps = ctx.enter_context(nc.psum_tensor("ps", [P, 8, 512], fp32))

        def bank(n, rows_=P, a=0, b=512):
            return ps[0:rows_, n, a:b]

        d_small, d_tok, d_ffn, d_moe = once("d_small"), once("d_tok"), once("d_ffn"), once("d_moe")
        d_stage = [once("d_stage0"), once("d_stage1")]
        c_ident, c_ones, c_mask, c_mem = once("c_ident"), once("c_ones"), once("c_mask"), once("c_mem")
        c_hi, c_lo = [once(f"c_hi{n}") for n in range(NCH)], [once(f"c_lo{n}") for n in range(NCH)]
        c_cols, c_ra, c_feat = once("c_cols"), once("c_ra"), once("c_feat")
        c_bcast, c_bcs = once("c_bcast"), once("c_bcs")

        ln_stats, ln_aggr, ln_norm = signal("ln_stats", 4 * GB), signal("ln_aggr", 4 * GB), signal("ln_norm", 4 * GB)
        ln_eps, ln_rstd, ln_dup = signal("ln_eps", 4), signal("ln_rstd", 4), signal("ln_dup", 3)
        x_in = signal("x_in", 16 * GB)
        x_hi, x_lo = signal("x_hi", GB), signal("x_lo", 2 * GB)
        t_qka, t_qkr, t_vps = signal("t_qka", GB), signal("t_qkr", GB), signal("t_vps", GB)
        t_ea, t_er, t_vhi, t_vlo = signal("t_ea", 2 * GB), signal("t_er", 2 * GB), signal("t_vhi", GB), signal("t_vlo", GB)
        t_qmax, t_qmask = signal("t_qmax", 2 * GB), signal("t_qmask", 2 * GB)
        t_s, t_max, t_sub, t_exp = (signal("t_s", 3 * GB), signal("t_max", 3 * GB), signal("t_sub", 3 * GB),
                                    signal("t_exp", 3 * GB))
        t_pT, t_pth, t_ptl = signal("t_pT", 3 * GB), signal("t_pth", 3 * GB), signal("t_ptl", 3 * GB)
        t_ops, t_rden, t_on = signal("t_ops", GB), signal("t_rden", GB), signal("t_on", 2 * GB)
        t_oT, t_oTs, t_y, t_h = signal("t_oT", GB), signal("t_oTs", GB), signal("t_y", GB), signal("t_h", GB)
        gT = signal("gT", 4)
        g_hi, g_lo = signal("g_hi", 8), signal("g_lo", 8)
        p_qk, p_sq, p_cp = signal("p_qk", 6), signal("p_sq", 6), signal("p_cp", 6)
        p_vps, p_vs, p_xbs = signal("p_vps", 2), signal("p_vs", 2), signal("p_xbs", 1)
        p_fq, p_eq, p_fk, p_ek = signal("p_fq", HP), signal("p_eq", HP), signal("p_fk", GB), signal("p_ek", GB)
        p_kvp, p_kvs, p_num = signal("p_kvp", GB), signal("p_kvs", GB), signal("p_num", 2)
        p_den, p_rec, p_att, p_dup = signal("p_den", 1), signal("p_rec", 1), signal("p_att", GB), signal("p_dup", 1)
        p_pr, p_ys, p_g, p_be, p_h = (signal("p_pr", 2), signal("p_ys", 2), signal("p_g", 1), signal("p_be", 1),
                                      signal("p_h", 1))
        m_mean, m_prod, m_log, m_st, m_ex = (signal("m_mean", 2), signal("m_prod", 2), signal("m_log", 1),
                                             signal("m_st", 9), signal("m_ex", 1))
        m_up, m_act, m_dn, m_res = signal("m_up", GB), signal("m_act", 2 * GB), signal("m_dn", GB), signal("m_res", GB)
        s_xc, s_dps, s_zs = signal("s_xc", 2), signal("s_dps", 2), signal("s_zs", 2)
        s_abs, s_exp, s_ln, s_dlt = signal("s_abs", 1), signal("s_exp", 1), signal("s_ln", 1), signal("s_dlt", 1)

        s_as, s_ws, s_wxs, s_a0 = signal("s_as", NT), signal("s_ws", NT), signal("s_wxs", NT), signal("s_a0", NT)
        s_bps, s_cps = signal("s_bps", NT), signal("s_cps", NT)
        s_bx, s_hs, s_pr, s_sum = signal("s_bx", NT), signal("s_hs", NT), signal("s_pr", NT), signal("s_sum", NT)
        s_yT, s_res = signal("s_yT", 2), signal("s_res", 2)
        kn_stats, kn_aggr, kn_norm = signal("kn_stats", 2 * GB), signal("kn_aggr", 2 * GB), signal("kn_norm", 2 * GB)
        kn_eps, kn_rstd = signal("kn_eps", 2), signal("kn_rstd", 2)
        kT, kTa, kTr = signal("kT", 1), signal("kTa", 1), signal("kTr", 1)
        f_up, f_rl, f_dn, f_b = signal("f_up", 1), signal("f_rl", 1), signal("f_dn", 2), signal("f_b", 2)
        f_g, f_be, f_out, o_out = signal("f_g", 1), signal("f_be", 1), signal("f_out", 1), signal("o_out", 16)

        CHUNKS = [[(0, j) for j in range(4)], [(1, j) for j in range(4)], [(0, 4), (0, 5), (1, 4), (1, 5)]]
        S_BANK = (1, 2, 1)
        T_BANK = (2, 1, 2)
        ROT = (5, 3, 4)

        TAIL = 9
        S_SEGS = 2 * NT + TAIL
        T_TIMES = [3, 2, 2] + GB * [3, 3, 3, 3, 3, 3, 3] + [2, 2]
        M_TIMES = ([3.9, 5.2, 6.5, 4, 5, 3.5, 2, 2, 2, 2, 4, 4, 4, 4, 5]
                   + [5, 4, 3.9, 2.6, 3.9, 3.9, 3.9, 6, 3, 6, 5, 5, 5, 5, 4.8, 3.6, 7.2, 3.6, 7.2])
        SETUP_SPAN = (0.12, 1)
        T_SPAN, M_SPAN, S_SPAN = (0, 0.97), (0, 1), (0, 0.99)
        S_TIMES = 2 * NT * [1.3] + [3, 4, 2, 3, 4, 4, 3, 2, 3]
        SETUP = (range(1, 7), range(7, NCH))

        def scan_bank(g, i, c):
            return ((0, 1) if g >= G - 2 and i % 2 else (6, 7))[c]

        def program(attention, middle, scan, setup=None):
            for s in range(G + 2):
                threads = []
                if s < G:
                    threads.append((attention(s), T_TIMES, T_SPAN))
                if 0 <= s - 1 < G:
                    threads.append((middle(s - 1), M_TIMES, M_SPAN))
                if s >= 2:
                    threads.append((scan(s - 2), S_TIMES, S_SPAN))
                if setup and s < 2:
                    threads.append((setup(s), len(SETUP[s]) * [1], SETUP_SPAN))
                order = sorted((a + (z - a) * sum(times[:k]) / sum(times), t, k) for t, (_, times, (a, z)) in enumerate(threads)
                               for k in range(len(times)))
                for _, t, _ in order:
                    next(threads[t][0])
                for thread, _, _ in threads:
                    assert next(thread, "end") == "end"

        D_STAGE, landed = [], [0, 0]
        for c in range(NCH):
            landed[c % 2] += 16 * (3 if 2 <= c < 2 + E else 1)
            D_STAGE.append(landed[c % 2])

        def chunk_tiles(c):
            if c < 2:
                r = slice(0, A_Q) if c == 0 else slice(A_Q, AW)
                return aw_h[:, r], aw_l[:, r], aw_d[:, r], WS
            if c < 2 + E:
                r = slice(F * (c - 2), F * (c - 1))
                return w1_h[:, r], w1_l[:, r], w1_d[:, r], ES
            r = slice(SC * (c - 2 - E), SC * (c - 1 - E))
            return tuple(t[:, r, :].rearrange("p a b -> p (a b)") for t in (sw_h, sw_l, sw_d)) + (WS,)

        ctx.enter_context(nc.allow_non_contiguous_dma(reason="a few small weight vectors"))
        block = ctx.enter_context(nc.Block())

        @block.sync
        def _(e):
            def load_chunk(c):
                if c >= 2:
                    e.wait_ge(c_hi[c - 2], 2 if c - 2 not in range(2, 2 + E) else 5)
                    e.wait_ge(c_lo[c - 2], 2 if c - 2 not in range(2, 2 + E) else 3)
                if c < 2:
                    src = (w_att0, w_att1)[c]
                elif c < 2 + E:
                    src = w_exp[c - 2, :, :, :]
                else:
                    src = w_scan[c - 2 - E, :, :, :]
                n = src.shape[-1]
                e.dma_start(stage[:, c % 2, :, 0:n], src if c >= 2 else src[:, :, :]).then_inc(d_stage[c % 2], 16)
                if 2 <= c < 2 + E:
                    for r in (64, 96):
                        e.dma_start(b_stage[r:r + 1, c % 2, :], b_exp[c - 2:c - 1, :]).then_inc(d_stage[c % 2], 16)

            def load_x(g, b):
                if b:
                    wait(e, x_lo, g, 2 * b)
                else:
                    again(e, x_lo, g, 2 * GB)
                e.dma_start(x_raw[:, :, :], x_t[g * GB + b, :, :, :]).then_inc(x_in.sem, 16)

            load_chunk(0)
            load_x(0, 0)
            for dst, src in ((tbq_a[:, :], tbq_in[0:P, :]), (tbq_r[0:CR, :], tbq_in[P:C, 0:1]), (tbq_r[CR:P, :], tbq_in[P:C, 1:2])):
                e.dma_start(dst, src).then_inc(d_tok, 16)
            e.dma_start(tproj[:, :, :], tproj_in[:, :, :]).then_inc(d_tok, 16)
            e.dma_start(tbv[:, :], tbv_in[:, :]).then_inc(d_tok, 16)
            e.dma_start(rows[:, :, :], rows_in[:, :, :]).then_inc(d_ffn, 16)
            e.dma_start(fwoT_a[:, :], fwo_in[0:P, :]).then_inc(d_ffn, 16)
            e.dma_start(fwoT_r[:, :], fwo_in[P:C, :]).then_inc(d_ffn, 16)
            e.dma_start(fw2_a[:, :], fw2_in[0:P, :]).then_inc(d_ffn, 16)
            e.dma_start(fw2_r[:, :], fw2_in[P:C, :]).then_inc(d_ffn, 16)
            e.dma_start(fb2_a[:, :], fb_in[0:P, 1:2]).then_inc(d_ffn, 16)
            e.dma_start(fb2_r[:, :], fb_in[P:C, 1:2]).then_inc(d_ffn, 16)
            load_chunk(1)
            e.dma_start(featrow[0:64, :], rf_in[:, :]).then_inc(d_small, 16)
            e.dma_start(a_all[:, :], a_in[:, :]).then_inc(d_small, 16)
            e.dma_start(dbias[:, :], dbias_in[:, :]).then_inc(d_small, 16)
            e.dma_start(fw1_a[:, :], fw1_in[0:P, :]).then_inc(d_small, 16)
            e.dma_start(fw1_r[:, :], fw1_in[P:C, :]).then_inc(d_small, 16)
            e.dma_start(fb1_c[:, :], fb_in[0:P, 0:1]).then_inc(d_small, 16)
            load_x(0, 1)
            load_chunk(2)
            load_chunk(3)
            load_x(0, 2)
            load_chunk(4)
            e.dma_start(w2[:, :], w2_in[:, :]).then_inc(d_moe, 16)
            e.dma_start(b2_row[:, :], b2_in[:, :]).then_inc(d_moe, 16)
            e.dma_start(wg_a[:, :], wg_in[0:P, :]).then_inc(d_moe, 16)
            e.dma_start(wg_r[:, :], wg_in[P:C, :]).then_inc(d_moe, 16)
            load_x(0, 3)
            load_chunk(5)
            load_chunk(6)
            for b, c in enumerate(range(7, NCH)):
                load_x(1, b)
                load_chunk(c)
            load_x(1, 3)

            def store(g):
                wait(e, f_out, g, 1)
                e.dma_start(out[GB * g:GB * g + GB, :, :].rearrange("b p c -> p b c"), k_y[:, :, :]).then_inc(o_out.sem, 16)

            for s in range(1, G):
                for b in range(2, GB):
                    if s > 1:
                        load_x(s, b)
                for b in range(2):
                    if s + 1 < G:
                        load_x(s + 1, b)
                if s >= 2:
                    store(s - 2)
            store(G - 2)
            store(G - 1)
            e.wait_ge(o_out.sem, 16 * G)

        @block.gpsimd
        def _(e):
            tt = e.tensor_tensor
            e.memset(ones[:, :], 1.0).then_inc(c_ones, 1)
            e.memset(ident[:, :], 0.0).then_inc(c_ident, 1)
            e.memset(headmask[:, :], 1.0).then_inc(c_mask, 1)
            e.memset(halfmask[:, :], 1.0).then_inc(c_mask, 1)
            e.memset(pairmask[:, :, :], 1.0).then_inc(c_mask, 1)
            e.wait_ge(c_ident, 1)
            e.affine_select(out=ident[:, :], in_=ident[:, :], compare_op=ALU.not_equal, fill=1.0, base=0,
                            pattern=[[-1, P]], channel_multiplier=1).then_inc(c_ident, 1)
            e.wait_ge(c_mask, 3)
            e.affine_select(out=headmask[:, :], in_=headmask[:, :], compare_op=ALU.is_ge, fill=0.0, base=0,
                            pattern=[[-D, 8]], channel_multiplier=1).then_inc(c_mask, 1)
            e.affine_select(out=pairmask[:, :, :], in_=pairmask[:, :, :], compare_op=ALU.is_ge, fill=0.0, base=0,
                            pattern=[[-M, 2], [0, D + 1]], channel_multiplier=1).then_inc(c_mask, 1)
            e.wait_ge(c_mask, 5)
            e.affine_select(out=headmask[:, :], in_=headmask[:, :], compare_op=ALU.is_ge, fill=0.0, base=D - 1,
                            pattern=[[D, 8]], channel_multiplier=-1).then_inc(c_mask, 1)
            e.affine_select(out=pairmask[:, :, :], in_=pairmask[:, :, :], compare_op=ALU.is_ge, fill=0.0, base=M - 1,
                            pattern=[[M, 2], [0, D + 1]], channel_multiplier=-1).then_inc(c_mask, 1)
            e.wait_ge(c_mask, 7)
            tt(halfmask[:, :], headmask[:, 0:4], headmask[:, 4:8], ALU.add).then_inc(c_mask, 1)
            e.memset(minus_half[:, :], -0.5).then_inc(c_mem, 1)
            e.memset(t_vh[:, :, :, 2 * D:VC], 1.0).then_inc(c_mem, 1)
            e.memset(t_vl[:, :, :, 2 * D:VC], 0.0).then_inc(c_mem, 1)
            e.memset(p_v[:, :, :, D:D + 1], 1.0).then_inc(c_mem, 1)
            e.wait_ge(c_mem, 7)

            def split_x(g, b):
                n = b % 2
                wait(e, x_in, g, 16 * (b + 1))
                if b >= 2:
                    wait(e, t_vps, g, b - 1)
                else:
                    again(e, t_vps, g, GB - 1 + b)
                e.tensor_copy(tx_h[:, n, :, :], x_raw[:, :, :]).then_inc(x_hi.sem, 1)
                wait(e, x_hi, g, b + 1)
                tt(tx_l[:, n, :], x_raw[:, 0, :], tx_h[:, n, 0, :], ALU.subtract).then_inc(x_lo.sem, 1)
                tt(tx_e[:, n, :], x_raw[0:CR, 1, :], tx_h[0:CR, n, 1, :], ALU.subtract).then_inc(x_lo.sem, 1)

            def queries(g, b):
                if b:
                    wait(e, t_s, g, b)
                wait(e, t_qmax, g, 2 * b + 1)
                tt(t_qm[:, :, :, :], t_qx[:, :, :].unsqueeze(2).to_broadcast([P, W, 8, NQ]),
                   headmask[:, :].unsqueeze(1).unsqueeze(3).to_broadcast([P, W, 8, NQ]), ALU.mult).then_inc(t_qmask.sem, 1)
                wait(e, t_qmax, g, 2 * b + 2)
                tt(t_qmr[:, :, :, :], t_qxr[:, :, :].unsqueeze(2).to_broadcast([CR, W, 4, NQ]),
                   headmask[0:CR, 0:4].unsqueeze(1).unsqueeze(3).to_broadcast([CR, W, 4, NQ]), ALU.mult).then_inc(t_qmask.sem, 1)

            def rstd(g, k):
                wait(e, ln_aggr, g, GB * (k + 1))
                e.tensor_scalar(ln_ve[:, :], ln_mv[:, :, 1], EPS, None, ALU.add).then_inc(ln_eps.sem, 1)
                wait(e, ln_eps, g, k + 1)
                tt(ln_rs[:, :], ln_ve[:, :], minus_half[:, :], ALU.pow).then_inc(ln_rstd.sem, 1)

            def bcast(row):
                return bc[:, row, :].unsqueeze(1).to_broadcast([P, GB, C])

            def attention(g):
                if g == 0:
                    split_x(g, 0)
                split_x(g, 1)
                yield
                yield
                queries(g, 0)
                yield
                for b in range(GB):
                    if b + 2 < GB:
                        split_x(g, b + 2)
                    yield
                    yield
                    yield
                    yield
                    if b + 1 < GB:
                        queries(g, b + 1)
                    yield
                    yield
                    yield
                if g + 1 < G:
                    split_x(g + 1, 0)
                yield
                yield

            def middle(g):
                rstd(g, 0)
                yield
                yield
                for _ in range(7):
                    yield
                wait(e, p_fq, g, HP)
                if g == 0:
                    e.wait_ge(c_bcs, 5)
                tt(p_xb[:, :, :], xn[:, :, 0:C], bcast(R_AB), ALU.add).then_inc(p_xbs.sem, 1)
                wait(e, t_h, g, GB)
                hg = h[:, g % 3, :, :]
                tt(hg, hg, bcast(R_ABETA), ALU.add).then_inc(p_be.sem, 1)
                for _ in range(5):
                    yield
                yield
                yield
                yield
                rstd(g, 1)
                yield
                yield
                yield
                rstd(g, 2)
                yield
                yield
                for _ in range(7):
                    yield
                rstd(g, 3)
                yield
                yield
                for _ in range(3):
                    yield

            def add_product(g, k):
                half = k // N1
                wait(e, s_pr, g, k + 1)
                if k:
                    wait(e, s_sum, g, k)
                if k in (0, N1):
                    if k == 0:
                        again(e, o_out, g, 16)
                    e.tensor_copy(s_acc[:, half, :], s_h[:, k % NH, :]).then_inc(s_sum.sem, 1)
                else:
                    tt(s_acc[:, half, :], s_acc[:, half, :], s_h[:, k % NH, :], ALU.add).then_inc(s_sum.sem, 1)

            def weigh(g, i):
                wait(e, s_ws, g, i + 1)
                if i == 0:
                    wait(e, s_xc, g, 2)
                tt(s_w[:, i % NW, :], s_w[:, i % NW, :], s_x[:, i // N1, :], ALU.mult).then_inc(s_wxs.sem, 1)
                e.memset(s_a[:, i % NA_, :].rearrange("p (b t) -> p b t", t=T)[:, :, 0:1], 0.0).then_inc(s_a0.sem, 1)

            def scan_step(g, slot):
                i, second = divmod(slot, 2)
                tail = slot - 2 * NT
                if slot == 0:
                    weigh(g, 0)
                    weigh(g, 1)
                elif i < NT and not second:
                    if i + 1 < NT:
                        weigh(g, i + 1)
                    add_product(g, i - 1)
                elif tail == 0:
                    add_product(g, NT - 1)
                elif tail in (1, 6):
                    k = int(tail == 6)
                    wait(e, kn_aggr, g, GB * (k + 1))
                    e.tensor_scalar(kn_ve[:, :], kn_mv[:, :, 1], EPS, None, ALU.add).then_inc(kn_eps.sem, 1)
                    wait(e, kn_eps, g, k + 1)
                    tt(kn_rs[:, :], kn_ve[:, :], minus_half[:, :], ALU.pow).then_inc(kn_rstd.sem, 1)
                elif tail == 4:
                    wait(e, kn_norm, g, GB)
                    tt(h[:, g % 3, :, :], h[:, g % 3, :, :], bcast(R_FBETA), ALU.add).then_inc(f_be.sem, 1)

            def scan(g):
                for slot in range(S_SEGS):
                    scan_step(g, slot)
                    yield

            program(attention, middle, scan)

        @block.scalar
        def _(e):
            act = e.activation

            def split_chunk(c):
                w_hi, _, w_d, scale = chunk_tiles(c)
                n = w_hi.shape[-1]
                e.wait_ge(d_stage[c % 2], D_STAGE[c])
                act(w_hi, stage[:, c % 2, 0, 0:n], ACT.Copy, scale=scale).then_inc(c_hi[c], 1)
                act(w_d, stage[:, c % 2, 1, 0:n], ACT.Copy, scale=scale).then_inc(c_hi[c], 1)
                if 2 <= c < 2 + E:
                    r = slice(F * (c - 2), F * (c - 1))
                    e.wait_ge(c_mem, 7)
                    act(w1_e[0:CR, r], stage[0:CR, c % 2, 1, 0:n], ACT.Copy, scale=scale).then_inc(c_hi[c], 1)
                    for p in (64, 96):
                        act(w1_e[p:p + 1, r], b_stage[p:p + 1, c % 2, :], ACT.Copy, scale=scale).then_inc(c_hi[c], 1)

            def evac_qk(g, b, rest):
                wait(e, t_qkr if rest else t_qka, g, b + 1)
                if b:
                    wait(e, t_qmax, g, 2 * b)
                    wait(e, t_s, g, 3 * b)
                for j in range(2):
                    if rest:
                        dst, r, src = (t_qr, t_kr)[j], slice(CR * j, CR * j + CR), ps[CR * j:CR * j + CR, 0, 0:256]
                        act(dst[:, :, :].rearrange("p w t -> p (w t)"), src, ACT.Identity, bias=tbq_r[r, 0:1],
                            scale=1 / WS).then_inc(t_er.sem, 1)
                    else:
                        act((t_qa, t_ka)[j][:, :, :].rearrange("p w t -> p (w t)"), bank(0, P, 256 * j, 256 * j + 256), ACT.Identity,
                            bias=tbq_a[:, j:j + 1], scale=1 / WS).then_inc(t_ea.sem, 1)

            def evac_v(g, b):
                wait(e, t_vps, g, b + 1)
                if b >= 2:
                    wait(e, t_ops, g, b - 1)
                else:
                    again(e, t_ops, g, GB - 1 + b)
                act(t_vh[:, b % 2, :, 0:2 * D], bank(0, P, 0, W * C).rearrange("p (n d) -> p n d", d=2 * D), ACT.Copy,
                    scale=1 / WS).then_inc(t_vhi.sem, 1)

            def hi_parts(g, n):
                q = g % 2
                wait(e, gT, g, n + 1)
                act(x_h[:, q, :], bank(3), ACT.Copy).then_inc(g_hi.sem, 1)
                act(x_d[:, q, :], bank(4), ACT.Copy).then_inc(g_hi.sem, 1)

            def attention(g):
                def exp_chunk(b, c):
                    wait(e, t_sub, g, 3 * b + c + 1)
                    act(t_p[:, 4 * c:4 * c + 4, :], t_p[:, 4 * c:4 * c + 4, :], ACT.Exp, scale=D ** -0.5).then_inc(t_exp.sem, 1)

                def keep_transposed(b, c):
                    wait(e, t_pT, g, 3 * b + c + 1)
                    act(t_pt[c][:, 0:GT], bank(T_BANK[c]), ACT.Copy).then_inc(t_pth.sem, 1)

                if g == 0:
                    e.wait_ge(d_tok, 16 * 5)
                    e.wait_ge(c_mem, 7)
                evac_qk(g, 0, False)
                yield
                evac_qk(g, 0, True)
                yield
                evac_v(g, 0)
                yield
                for b in range(GB):
                    yield
                    exp_chunk(b, 0)
                    yield
                    exp_chunk(b, 1)
                    yield
                    exp_chunk(b, 2)
                    keep_transposed(b, 0)
                    if b + 1 < GB:
                        evac_qk(g, b + 1, False)
                    yield
                    if b + 1 < GB:
                        evac_qk(g, b + 1, True)
                    keep_transposed(b, 1)
                    yield
                    keep_transposed(b, 2)
                    if b + 1 < GB:
                        evac_v(g, b + 1)
                    yield
                    yield
                yield
                yield

            def middle(g):
                yield
                yield
                hi_parts(g, 0)
                yield
                for half in range(2):
                    for j in range(3 * half, 3 * half + 3):
                        wait(e, p_qk, g, j + 1)
                        act(p_f[64:P, j, :], ps[64:P, ROT[j % 3], :], ACT.Square, scale=1 / WS).then_inc(p_sq.sem, 1)
                    yield
                for j in range(2):
                    wait(e, p_vps, g, j + 1)
                    act(p_v[:, 2 * j:2 * j + 2, :, 0:D],
                        bank(ROT[j], P, 0, 2 * C).rearrange("p (b n d) -> p b n d", b=2, n=H), ACT.Copy,
                        scale=1 / WS).then_inc(p_vs.sem, 1)
                yield
                for j in range(HP):
                    wait(e, p_fq, g, j + 1)
                    act(p_qp[:, j, :], bank(ROT[(j + 2) % 3]), ACT.Exp).then_inc(p_eq.sem, 1)
                    if j % 2:
                        yield
                for b in range(GB):
                    wait(e, p_fk, g, b + 1)
                    if b >= 2:
                        wait(e, p_kvp, g, b - 1)
                    act(p_kp[:, b % 2, :], ps[:, 3:5, :].rearrange("p a b -> p (a b)")[:, 0:H * M], ACT.Exp).then_inc(p_ek.sem, 1)
                    yield
                yield
                yield
                hi_parts(g, 1)
                yield
                for _ in range(6):
                    yield
                hi_parts(g, 2)
                yield
                wait(e, m_st, g, 3)
                act(m_e[:, :, :], m_ls[:, :, :], ACT.Exp).then_inc(m_ex.sem, 1)
                yield
                for b in range(GB):
                    wait(e, m_up, g, b + 1)
                    if b >= 2:
                        wait(e, m_dn, g, b - 1)
                    act(m_h[:, b % 2, 0:512], bank(3), ACT.Gelu, scale=1 / ES).then_inc(m_act.sem, 1)
                    act(m_h[:, b % 2, 512:F], bank(4, P, 0, F - 512), ACT.Gelu, scale=1 / ES).then_inc(m_act.sem, 1)
                    yield
                yield
                yield
                yield
                hi_parts(g, 3)
                yield
                yield
                wait(e, s_zs, g, 2)
                act(s_u[:, :, :], s_z[:, :, :], ACT.Abs).then_inc(s_abs.sem, 1)
                wait(e, s_abs, g, 1)
                act(s_u[:, :, :], s_u[:, :, :], ACT.Exp, scale=-1.0).then_inc(s_exp.sem, 1)
                wait(e, s_exp, g, 1)
                act(s_u[:, :, :], s_u[:, :, :], ACT.Ln, bias=1.0).then_inc(s_ln.sem, 1)
                yield

            def scan_exp(g, i):
                if i >= NA_:
                    wait(e, s_hs, g, i - NA_ + 1)
                elif i == 0:
                    again(e, f_dn, g, 2)
                act(s_a[:, i % NA_, :], s_dt[:, i // N1, :], ACT.Exp, scale=a_all[:, i:i + 1]).then_inc(s_as.sem, 1)

            def scan_less(g, i):
                wait(e, s_as, g, i + 1)
                if i >= NW:
                    wait(e, s_hs, g, i - NW + 1)
                else:
                    again(e, f_g, g, 1)
                act(s_w[:, i % NW, :], s_a[:, i % NA_, :], ACT.Copy, bias=-1.0).then_inc(s_ws.sem, 1)

            def scan_step(g, slot):
                i, second = divmod(slot, 2)
                tail = slot - 2 * NT
                if slot == 0:
                    wait(e, s_dlt, g, 1)
                    if g == 0:
                        for c in (NCH - 2, NCH - 1):
                            e.wait_ge(c_lo[c], 2)
                    scan_exp(g, 0)
                    scan_exp(g, 1)
                    scan_less(g, 0)
                if i + 1 < NT and not second:
                    scan_less(g, i + 1)
                    if i + 2 < NT:
                        scan_exp(g, i + 2)
                elif tail == 3:
                    wait(e, kT, g, 1)
                    act(k_xa[:, :], bank(6), ACT.Copy).then_inc(kTa.sem, 1)
                elif tail == 4:
                    wait(e, f_up, g, 1)
                    act(f_h[:, :], bank(6), ACT.Relu, bias=fb1_c[:, 0:1]).then_inc(f_rl.sem, 1)

            def scan(g):
                for slot in range(S_SEGS):
                    scan_step(g, slot)
                    yield

            def setup(s):
                for c in SETUP[s]:
                    split_chunk(c)
                    yield

            split_chunk(0)
            program(attention, middle, scan, setup)

        @block.tensor
        def _(e):
            mm, tr = nc.tensor.matmul, nc.tensor.transpose
            one = ones[0:1, :]

            def tables():
                e.wait_ge(d_tok, 16 * 5)
                e.wait_ge(d_ffn, 16 * 7)
                e.wait_ge(c_ones, 1)
                e.wait_ge(c_ident, 2)
                e.wait_ge(c_cols, 3)
                mm(bank(5, P, 0, C), one, rows[0:1, R_TPROJ, :], start=True, stop=False)
                for s in range(2):
                    mm(bank(5, P, 0, C), tbv_b[:, s, :], tproj[:, s, :], start=False, stop=s == 1)
                mm(bank(5, P, C, 2 * C), one, rows[0:1, R_AB, :], start=True, stop=True)
                for n in (0, 1):
                    mm(bank(6, P, C * n, C * n + C), one, rows[0:1, 2 + n, :], start=True, stop=True)
                    mm(bank(7, P, C * n, C * n + C), one, rows[0:1, 5 + n, :], start=True, stop=True)
                mm(bank(4, P, 0, C), one, rows[0:1, R_FBO, :], start=True, stop=False)
                mm(bank(4, P, 0, C), fb2_ab[:, :], fwoT_a[:, :], start=False, stop=False)
                mm(bank(4, P, 0, C), fb2_rb[:, :], fwoT_r[:, :], start=False, stop=True)
                mm(bank(4, P, C, 2 * C), fw2_a[:, :], fwoT_a[:, :], start=True, stop=False)
                mm(bank(4, P, C, 2 * C), fw2_r[:, :], fwoT_r[:, :], start=False, stop=True).then_inc(c_bcast, 1)

            def split_mm(o, a, b):
                mm(o, a[0], b[0], start=True, stop=False)
                mm(o, a[0], b[1], start=False, stop=False)
                mm(o, a[1], b[0], start=False, stop=False)
                mm(o, a[2], b[2], start=False, stop=False)
                return mm(o, a[3], b[3], start=False, stop=True)

            def weights(c0, n):
                return (aw_h[:, c0:c0 + n], aw_l[:, c0:c0 + n], aw_d[:, c0:c0 + n], aw_d[0:CR, c0:c0 + n])

            def raw_x(b, c0, n):
                k = b % 2
                return (tx_h[:, k, 0, c0:c0 + n], tx_l[:, k, c0:c0 + n], tx_h[:, k, 1, c0:c0 + n], tx_e[:, k, c0:c0 + n])

            def group_x(q, c0, n, rows_=CR):
                return (x_h[:, q, c0:c0 + n], x_l[:, q, c0:c0 + n], x_d[:, q, c0:c0 + n], x_e[0:rows_, q, c0:c0 + n])

            def queries_keys_a(g, b):
                wait(e, x_lo, g, 2 * b + 2)
                if b == 1:
                    wait(e, t_vlo, g, 1)
                elif b:
                    wait(e, t_h, g, b - 1)
                else:
                    again(e, t_h, g, GB)
                split_mm(bank(0, P, 0, 256), weights(0, P), raw_x(b, 0, 256))
                split_mm(bank(0, P, 256, 512), weights(P, P), raw_x(b, 0, 256)).then_inc(t_qka.sem, 1)

            def queries_keys_r(g, b):
                wait(e, t_ea, g, 2 * b + 2)
                split_mm(bank(0, P, 0, 256), weights(2 * P, P), raw_x(b, 0, 256)).then_inc(t_qkr.sem, 1)

            def values(g, b):
                wait(e, t_er, g, 2 * b + 2)
                for w in range(W):
                    last = split_mm(bank(0, P, C * w, C * w + C), raw_x(b, P * w, P), weights(2 * C, C))
                last.then_inc(t_vps.sem, 1)

            def out_transposed(g, b):
                wait(e, t_on, g, 2 * b + 2)
                for w in range(W):
                    last = tr(bank(0, HP * D, P * w, P * w + P), t_o[:, HP * w:HP * w + HP, :].rearrange("p a b -> p (a b)"), ident[:, :])
                last.then_inc(t_oT.sem, 1)

            def out_projected(g, b):
                wait(e, t_oTs, g, b + 1)
                for s in range(2):
                    last = mm(bank(0, P, 0, C), t_ot[:, s, :, :], tproj[:, s, :], start=s == 0, stop=s == 1)
                last.then_inc(t_y.sem, 1)

            def scores(g, b, c):
                wait(e, t_qmask, g, 2 * b + 2)
                wait(e, t_er, g, 2 * b + 2)
                if c == 2:
                    wait(e, t_sub, g, 3 * b + 1)
                elif b and c == 0:
                    wait(e, t_ptl, g, 3 * b - 1)
                elif b:
                    wait(e, t_ptl, g, 3 * b)
                else:
                    again(e, t_ptl, g, 3 * GB)
                for k, (w, j) in enumerate(CHUNKS[c]):
                    o = bank(S_BANK[c], P, P * k, P * k + P)
                    if j < 4:
                        last = mm(o, t_qm[:, w, 2 * j:2 * j + 2, :], t_ka[:, w, :], start=True, stop=True)
                    else:
                        last = mm(o, t_qmr[:, w, 2 * j - 8:2 * j - 6, :], t_kr[:, w, :], start=True, stop=True)
                last.then_inc(t_s.sem, 1)

            def weights_transposed(g, b, c):
                wait(e, t_exp, g, 3 * b + c + 1)
                if c < 2:
                    wait(e, t_sub, g, 3 * b + c + 2)
                else:
                    wait(e, t_ptl, g, 3 * b + 1)
                for k in range(4):
                    last = tr(bank(T_BANK[c], P, P * k, P * k + P), t_p[:, 4 * c + k, :], ident[:, :])
                last.then_inc(t_pT.sem, 1)

            def weighted_values(g, b):
                wait(e, t_vlo, g, min(b + 2, GB))
                if b == GB - 1:
                    wait(e, t_h, g, b)
                for c in range(3):
                    wait(e, t_ptl, g, 3 * b + c + 1)
                    for k, (w, j) in enumerate(CHUNKS[c]):
                        n = w * HP + j
                        o = bank(0, P, VC * n, VC * n + VC)
                        hi, lo = t_pt[c][:, P * k:P * k + P], t_pt[c][:, GT + P * k:GT + P * k + P]
                        mm(o, hi, t_vh[:, b % 2, n, :], start=True, stop=False)
                        mm(o, hi, t_vl[:, b % 2, n, :], start=False, stop=False)
                        last = mm(o, lo, t_vh[:, b % 2, n, :], start=False, stop=True)
                last.then_inc(t_ops.sem, 1)

            def to_channels(src):
                for b in range(GB):
                    tr(bank(3, P, T * b, T * b + T), src[:, b, 0:P], ident[:, :])
                for b in range(GB):
                    last = tr(bank(4, P, T * b, T * b + T), src[:, b, P:C + CR], ident[:, :])
                return last

            def attention(g):
                if g == 0:
                    e.wait_ge(c_lo[0], 2)
                    e.wait_ge(c_hi[0], 2)
                queries_keys_a(g, 0)
                yield
                queries_keys_r(g, 0)
                yield
                values(g, 0)
                if g == 0:
                    tables()
                yield
                for b in range(GB):
                    scores(g, b, 0)
                    scores(g, b, 1)
                    if b:
                        out_transposed(g, b - 1)
                    yield
                    scores(g, b, 2)
                    yield
                    if b:
                        out_projected(g, b - 1)
                    weights_transposed(g, b, 0)
                    yield
                    if b + 1 < GB:
                        queries_keys_a(g, b + 1)
                    weights_transposed(g, b, 1)
                    yield
                    if b + 1 < GB:
                        queries_keys_r(g, b + 1)
                    weights_transposed(g, b, 2)
                    yield
                    if b + 1 < GB:
                        values(g, b + 1)
                    yield
                    weighted_values(g, b)
                    yield
                out_transposed(g, GB - 1)
                yield
                out_projected(g, GB - 1)
                yield

            def middle(g):
                q = g % 2
                yield
                yield
                wait(e, ln_dup, g, 1)
                again(e, s_zs, g, 2)
                again(e, s_xc, g, 2)
                again(e, g_lo, g, 8)
                if g == 0:
                    e.wait_ge(c_bcs, 5)
                to_channels(xn).then_inc(gT.sem, 1)
                yield
                wait(e, g_hi, g, 2)
                wait(e, g_lo, g, 2)
                if g == 0:
                    for c in range(1, 2 + E):
                        e.wait_ge(c_lo[c], 3 if c > 1 else 2)
                        e.wait_ge(c_hi[c], 5 if c > 1 else 2)
                    e.wait_ge(c_feat, 1)
                    e.wait_ge(c_mem, 7)

                def qk_tile(j):
                    if j >= 3:
                        wait(e, p_cp, g, j - 2)
                        wait(e, p_sq, g, j - 2)
                    split_mm(bank(ROT[j % 3]), weights(A_Q + P * j, P), group_x(q, 0, GT)).then_inc(p_qk.sem, 1)

                for j in range(3):
                    qk_tile(j)
                yield
                for j in range(3, 6):
                    qk_tile(j)
                yield
                for b in range(GB):
                    if b % 2 == 0:
                        wait(e, p_cp, g, 4 + b // 2)
                        wait(e, p_sq, g, 4 + b // 2)
                    last = split_mm(bank(ROT[b // 2], P, C * (b % 2), C * (b % 2) + C), group_x(q, T * b, T), weights(A_V, C))
                    if b % 2:
                        last.then_inc(p_vps.sem, 1)
                yield
                for j in range(HP):
                    if j == 0:
                        wait(e, p_cp, g, 6)
                        wait(e, p_sq, g, 6)
                    elif j < 3:
                        wait(e, p_vs, g, j)
                    else:
                        wait(e, p_eq, g, j - 2)
                    mm(bank(ROT[(j + 2) % 3]), feat[:, 2 * (j % 2):2 * (j % 2) + 2, :], p_f[:, j // 2, :], start=True,
                       stop=True).then_inc(p_fq.sem, 1)
                    if j % 2:
                        yield

                def features_k(b):
                    if b:
                        wait(e, p_ek, g, b)
                    else:
                        wait(e, p_eq, g, HP)
                    for j in range(3):
                        last = mm(bank(3 + j // 2, P, 256 * (j % 2), 256 * (j % 2) + 256), p_f[:, 3 + j, T * b:T * b + T],
                                  feat[:, :, :], start=True, stop=True)
                    last.then_inc(p_fk.sem, 1)

                features_k(0)
                yield
                for b in range(GB):
                    wait(e, p_ek, g, b + 1)
                    wait(e, p_vs, g, 2)
                    if b:
                        wait(e, p_kvs, g, b)
                    for j in range(HP):
                        last = mm(bank(5, P, 34 * j, 34 * j + 34), p_kp[:, b % 2, P * j:P * j + P],
                                  p_v[:, b, 2 * j:2 * j + 2, :], start=True, stop=True)
                    last.then_inc(p_kvp.sem, 1)
                    if b + 1 < GB:
                        features_k(b + 1)
                    yield
                wait(e, p_kvs, g, GB)
                wait(e, p_ek, g, GB)
                for b in range(GB):
                    for j in range(HP):
                        o = 256 * (b % 2) + 34 * j
                        last = mm(bank(3 + b // 2, P, o, o + 34), p_qp[:, j, T * b:T * b + T], p_kv[b][:, j, :], start=True, stop=True)
                    if b % 2:
                        last.then_inc(p_num.sem, 1)
                yield
                wait(e, p_dup, g, 1)
                wait(e, p_ek, g, GB)
                to_channels(xn).then_inc(gT.sem, 1)
                yield
                wait(e, g_hi, g, 4)
                wait(e, g_lo, g, 4)
                for b in range(GB):
                    last = split_mm(bank(ROT[b // 2], P, C * (b % 2), C * (b % 2) + C), group_x(q, T * b, T), weights(A_P, C))
                    if b % 2:
                        last.then_inc(p_pr.sem, 1)
                for _ in range(6):
                    yield
                wait(e, ln_dup, g, 2)
                to_channels(xn).then_inc(gT.sem, 1)
                yield
                wait(e, m_prod, g, 2)
                wait(e, g_hi, g, 6)
                wait(e, g_lo, g, 6)
                mm(bank(5, P, 0, GB * E), ones[:, :], m_pa[:, :, :], start=True, stop=False)
                mm(bank(5, P, 0, GB * E), ones[0:CR, :], m_pr[:, :, :], start=False, stop=True).then_inc(m_log.sem, 1)
                yield
                wait(e, m_st, g, 7)
                if g == 0:
                    e.wait_ge(d_moe, 16 * 4)
                chosen = []

                def up(b):
                    chosen.append(e.value_load(m_idx[0:1, b:b + 1], min_val=0, max_val=E - 1))
                    if b:
                        wait(e, m_act, g, 2 * b)
                    for f in range(FT):
                        at = bass.ds(chosen[b] * F + P * f, P)
                        last = split_mm(bank(3 + f // 4, P, P * (f % 4), P * (f % 4) + P),
                                        (w1_h[:, at], w1_l[:, at], w1_d[:, at], w1_e[:, at]), group_x(q, T * b, T, P))
                    last.then_inc(m_up.sem, 1)

                def down(b):
                    wait(e, m_act, g, 2 * (b + 1))
                    if b:
                        wait(e, m_res, g, b)
                    o = bank(5, P, 0, C)
                    for f in range(FT):
                        mm(o, m_h[:, b % 2, P * f:P * f + P], w2[:, bass.ds(chosen[b] * (FT * C) + C * f, C)],
                           start=f == 0, stop=False)
                    mm(o, one, b2_row[0:1, bass.ds(chosen[b] * C, C)], start=False, stop=True).then_inc(m_dn.sem, 1)

                up(0)
                yield
                for b in range(GB):
                    if b + 1 < GB:
                        up(b + 1)
                    down(b)
                    yield
                yield
                yield
                wait(e, ln_dup, g, 3)
                wait(e, m_act, g, 2 * GB)
                to_channels(xn).then_inc(gT.sem, 1)
                yield
                wait(e, g_hi, g, 8)
                wait(e, g_lo, g, 8)
                if g == 0:
                    e.wait_ge(c_lo[NCH - 1], 2)
                    e.wait_ge(c_hi[NCH - 1], 2)
                wait(e, s_xc, g, 2)
                for s in range(2):
                    scan_product(bank((5, 3)[s]), 2 * NT + s, q).then_inc(s_dps.sem, 1)
                yield
                yield

            def scan_product(o, n, q):
                return split_mm(o, (sw_h[:, n, :], sw_l[:, n, :], sw_d[:, n, :], sw_d[0:CR, n, :]), group_x(q, 0, GT))

            def scan_b(g, i):
                ahead = 2 if g >= G - 2 else 1
                if i >= ahead:
                    wait(e, s_bx, g, i - ahead + 1)
                elif i:
                    wait(e, t_h, G - 1, GB)
                    again(e, s_bx, g, NT)
                elif i == 0:
                    again(e, f_b, g, 2)
                    again(e, f_rl, g, 1)
                    if g == 0:
                        e.wait_ge(c_bcs, 5)
                        for c in range(2 + E, NCH):
                            e.wait_ge(c_lo[c], 2)
                            e.wait_ge(c_hi[c], 2)
                scan_product(bank(scan_bank(g, i, 0)), i, g % 2).then_inc(s_bps.sem, 1)

            def scan_c(g, i):
                ahead = 2 if g >= G - 2 else 1
                if i >= ahead:
                    wait(e, s_pr, g, i - ahead + 1)
                elif i:
                    wait(e, t_ptl, G - 1, 3 * GB)
                    again(e, s_pr, g, NT)
                scan_product(bank(scan_bank(g, i, 1)), NT + i, g % 2).then_inc(s_cps.sem, 1)

            def scan_step(g, slot):
                i, second = divmod(slot, 2)
                tail = slot - 2 * NT
                if i < NT and not second:
                    if i == 0:
                        scan_b(g, 0)
                    scan_c(g, i)
                elif i < NT:
                    if i + 1 < NT:
                        scan_b(g, i + 1)
                elif tail == 0:
                    wait(e, s_sum, g, NT)
                    wait(e, s_pr, g, NT)
                    for b in range(GB):
                        o, c = C * (b % 2), slice(T * b, T * b + T)
                        tr(bank(6 + b // 2, P, o, o + P), s_acc[:, 0, c], ident[:, :])
                        last = mm(bank(6 + b // 2, P, o + P, o + C), s_acc[:, 1, c], fold[:, :], start=True, stop=True)
                        if b % 2:
                            last.then_inc(s_yT.sem, 1)
                elif tail == 3:
                    wait(e, kn_norm, g, GB)
                    for b in range(GB):
                        tr(bank(6, P, T * b, T * b + T), k_xn[:, b, 0:P], ident[:, :])
                    for b in range(GB):
                        last = tr(bank(7, CR, T * b, T * b + T), k_xn[:, b, P:C], ident[:, :])
                    last.then_inc(kT.sem, 1)
                elif tail == 4:
                    wait(e, kTa, g, 1)
                    wait(e, kTr, g, 1)
                    mm(bank(6), fw1_a[:, :], k_xa[:, :], start=True, stop=False)
                    mm(bank(6), fw1_r[:, :], k_xr[:, :], start=False, stop=True).then_inc(f_up.sem, 1)
                elif tail == 5:
                    wait(e, f_rl, g, 1)
                    for b in range(GB):
                        last = mm(bank((7, 6)[b // 2], P, C * (b % 2), C * (b % 2) + C), f_h[:, T * b:T * b + T], fw21[:, :],
                                  start=True, stop=True)
                        if b % 2:
                            last.then_inc(f_dn.sem, 1)

            def scan(g):
                for slot in range(S_SEGS):
                    scan_step(g, slot)
                    yield

            program(attention, middle, scan)

        @block.vector
        def _(e):
            tt, ts, stt = e.tensor_tensor, e.tensor_scalar, e.scalar_tensor_tensor
            e.memset(featrow[64:P, :], -0.5).then_inc(c_mem, 1)
            e.memset(w1_e[64:P, :], 0.0).then_inc(c_mem, 1)
            e.memset(x_e[64:P, :, :], 1.0).then_inc(c_mem, 1)

            def tables():
                e.wait_ge(d_tok, 16 * 5)
                e.wait_ge(d_ffn, 16 * 7)
                e.wait_ge(c_ones, 1)
                tt(tbv_b[:, :, :], tbv[:, :].unsqueeze(2).to_broadcast([HP * D, 2, P]),
                   ones[0:HP * D, :].unsqueeze(1).to_broadcast([HP * D, 2, P]), ALU.mult).then_inc(c_cols, 1)
                ts(fb2_ab[:, :], ones[:, :], fb2_a[:, 0:1], None, ALU.mult).then_inc(c_cols, 1)
                ts(fb2_rb[:, :], ones[0:CR, :], fb2_r[:, 0:1], None, ALU.mult).then_inc(c_cols, 1)
                e.wait_ge(c_ident, 2)
                tt(fold[:, :], ident[:, 0:CR], ident[:, CR:P], ALU.add).then_inc(c_ra, 1)
                e.wait_ge(d_small, 16 * 6)
                e.wait_ge(c_mask, 8)
                e.wait_ge(c_mem, 7)
                ts(ra_all[:, :], a_all[:, :], WS, None, ALU.mult).then_inc(c_ra, 1)
                tt(feat[:, :, :], featrow[:, :].unsqueeze(1).to_broadcast([P, 4, M]),
                   halfmask[:, :].unsqueeze(2).to_broadcast([P, 4, M]), ALU.mult).then_inc(c_feat, 1)
                e.wait_ge(c_ra, 2)
                e.reciprocal(ra_all[:, :], ra_all[:, :]).then_inc(c_ra, 1)

            def keep_vectors():
                e.wait_ge(c_bcast, 1)
                e.tensor_copy(bc[:, 0:2, :], bank(5, P, 0, 2 * C)).then_inc(c_bcs, 1)
                e.tensor_copy(bc[:, 2:4, :], bank(6, P, 0, 2 * C)).then_inc(c_bcs, 1)
                e.tensor_copy(bc[:, 5:7, :], bank(7, P, 0, 2 * C)).then_inc(c_bcs, 1)
                e.tensor_copy(bc[:, R_FBO, :], bank(4, P, 0, C)).then_inc(c_bcs, 1)
                e.tensor_copy(fw21[:, :], bank(4, P, C, 2 * C)).then_inc(c_bcs, 1)
                e.wait_ge(c_bcs, 5)
                e.wait_ge(c_ra, 3)

            def split_chunk(c):
                w_hi, w_lo, w_d, scale = chunk_tiles(c)
                n = w_hi.shape[-1]
                e.wait_ge(d_stage[c % 2], D_STAGE[c])
                e.wait_ge(c_hi[c], 2 if not 2 <= c < 2 + E else 5)
                stt(out=w_lo, in0=stage[:, c % 2, 0, 0:n], scalar=scale, in1=w_hi, op0=ALU.mult, op1=ALU.subtract).then_inc(c_lo[c], 1)
                stt(out=w_d[64:P], in0=stage[64:P, c % 2, 1, 0:n], scalar=scale, in1=w_d[64:P], op0=ALU.mult,
                    op1=ALU.subtract).then_inc(c_lo[c], 1)
                if 2 <= c < 2 + E:
                    r = slice(F * (c - 2), F * (c - 1))
                    stt(out=w1_e[96:97, r], in0=b_stage[96:97, c % 2, :], scalar=scale, in1=w1_e[96:97, r],
                        op0=ALU.mult, op1=ALU.subtract).then_inc(c_lo[c], 1)

            def ln_moments(g, k, src, st, mv, stats, aggr, ready):
                for b in range(GB):
                    ready(b)
                    e.bn_stats(st[:, b, :], src[:, b, :]).then_inc(stats.sem, 1)
                for b in range(GB):
                    wait(e, stats, g, GB * k + b + 1)
                    e.bn_aggr(mv[:, b, :], st[:, b, :]).then_inc(aggr.sem, 1)

            def ln_apply(g, k, dst, src, mv, rs, aggr, rstd, norm):
                wait(e, aggr, g, GB * (k + 1))
                wait(e, rstd, g, k + 1)
                for b in range(GB):
                    ts(dst[:, b, 0:C], src[:, b, :], mv[:, b, 0:1], rs[:, b:b + 1], ALU.subtract, ALU.mult).then_inc(norm.sem, 1)

            def duplicate(g, n):
                wait(e, ln_norm, g, GB * ((1, 3, 4)[n]))
                e.tensor_copy(xn[:, :, C:C + CR], xn[:, :, P:C]).then_inc(ln_dup.sem, 1)

            def moments(g, k, src, ready):
                ln_moments(g, k, src, ln_st, ln_mv, ln_stats, ln_aggr, ready)

            def apply(g, k, src):
                ln_apply(g, k, xn, src, ln_mv, ln_rs, ln_aggr, ln_rstd, ln_norm)

            def lo_parts(g, n):
                q = g % 2
                wait(e, g_hi, g, 2 * n + 2)
                tt(x_l[:, q, :], bank(3), x_h[:, q, :], ALU.subtract).then_inc(g_lo.sem, 1)
                tt(x_e[0:CR, q, :], bank(4, CR), x_d[0:CR, q, :], ALU.subtract).then_inc(g_lo.sem, 1)

            def query_max(g, b):
                wait(e, t_ea, g, 2 * b + 2)
                tt(t_qx[:, :, :], t_qa[:, :, 0:NQ], t_qa[:, :, NQ:P], ALU.max).then_inc(t_qmax.sem, 1)
                wait(e, t_er, g, 2 * b + 2)
                tt(t_qxr[:, :, :], t_qr[:, :, 0:NQ], t_qr[:, :, NQ:P], ALU.max).then_inc(t_qmax.sem, 1)

            def transposed_out(g, b):
                wait(e, t_oT, g, b + 1)
                e.tensor_copy(t_ot[:, :, :, :].rearrange("p s w q -> p w s q"),
                              bank(0, HP * D, 0, W * P).rearrange("p (w s q) -> p w s q", w=W, s=2)).then_inc(t_oTs.sem, 1)

            def values_lo(g, b):
                wait(e, t_vhi, g, b + 1)
                stt(out=t_vl[:, b % 2, :, 0:2 * D], in0=bank(0, P, 0, W * C).rearrange("p (n d) -> p n d", d=2 * D),
                    scalar=1 / WS, in1=t_vh[:, b % 2, :, 0:2 * D], op0=ALU.mult, op1=ALU.subtract).then_inc(t_vlo.sem, 1)

            def transposed_lo(g, b, c):
                wait(e, t_pth, g, 3 * b + c + 1)
                tt(t_pt[c][:, GT:2 * GT], bank(T_BANK[c]), t_pt[c][:, 0:GT], ALU.subtract).then_inc(t_ptl.sem, 1)

            def pooled(g, b):
                wait(e, t_y, g, b + 1)
                if b == 0:
                    again(e, f_out, g, 1, back=3)
                tt(h[:, g % 3, b, :], bank(0, P, 0, C), bc[:, R_TPROJ, :], ALU.add).then_inc(t_h.sem, 1)

            def attention(g):
                def less_max(b, c):
                    n = 3 * b + c + 1
                    wait(e, t_s, g, n)
                    chunk = bank(S_BANK[c]).rearrange("p (a b) -> p a b", b=P)
                    r = slice(4 * c, 4 * c + 4)
                    e.reduce_max(t_mx[:, r], chunk, AX.X).then_inc(t_max.sem, 1)
                    wait(e, t_max, g, n)
                    if b:
                        wait(e, t_ops, g, b)
                    tt(t_p[:, r, :], chunk, t_mx[:, r].unsqueeze(2).to_broadcast([P, 4, P]), ALU.subtract).then_inc(t_sub.sem, 1)

                yield
                query_max(g, 0)
                yield
                values_lo(g, 0)
                if g == 0:
                    tables()
                yield
                for b in range(GB):
                    less_max(b, 0)
                    if b:
                        transposed_out(g, b - 1)
                    yield
                    less_max(b, 1)
                    yield
                    less_max(b, 2)
                    if b:
                        pooled(g, b - 1)
                    yield
                    transposed_lo(g, b, 0)
                    if g == 0 and b == 0:
                        keep_vectors()
                    yield
                    if b + 1 < GB:
                        query_max(g, b + 1)
                    transposed_lo(g, b, 1)
                    yield
                    transposed_lo(g, b, 2)
                    if b + 1 < GB:
                        values_lo(g, b + 1)
                    yield
                    wait(e, t_ops, g, b + 1)
                    o = bank(0, P, 0, W * HP * VC).rearrange("p (n c) -> p n c", c=VC)
                    e.reciprocal(t_rd[:, :], o[:, :, 2 * D]).then_inc(t_rden.sem, 1)
                    wait(e, t_rden, g, b + 1)
                    if b:
                        wait(e, t_oT, g, b)
                    for s in range(2):
                        r = slice(64 * s, 64 * s + 64)
                        tt(t_o[r, :, :], o[r, :, D * s:D * s + D], t_rd[r, :].unsqueeze(2).to_broadcast([64, W * HP, D]),
                           ALU.mult).then_inc(t_on.sem, 1)
                    yield
                transposed_out(g, GB - 1)
                yield
                pooled(g, GB - 1)
                yield

            def middle(g):
                q = g % 2
                hg = h[:, g % 3, :, :]
                moments(g, 0, hg, lambda b: wait(e, t_h, g, b + 1))
                yield
                apply(g, 0, hg)
                duplicate(g, 0)
                yield
                lo_parts(g, 0)
                yield
                for half in range(2):
                    for j in range(3 * half, 3 * half + 3):
                        wait(e, p_qk, g, j + 1)
                        ts(p_f[0:64, j, :], ps[0:64, ROT[j % 3], :], 1 / WS, None, ALU.mult).then_inc(p_cp.sem, 1)
                    yield
                for _ in range(5):
                    yield
                for b in range(GB):
                    wait(e, p_kvp, g, b + 1)
                    if b == 0:
                        wait(e, p_fq, g, HP)
                    tt(p_kv[b], bank(5, P, 0, KV).rearrange("p (j c) -> p j c", c=34),
                       pairmask[:, :, :].rearrange("p a b -> p (a b)").unsqueeze(1).to_broadcast([P, HP, 34]),
                       ALU.mult).then_inc(p_kvs.sem, 1)
                    yield
                wait(e, p_num, g, 2)
                num = (ps[:, 3:5, :].rearrange("p a (b c) -> p (a b) c", c=256)[:, :, 0:KV]
                       .rearrange("p b (n c) -> p b n c", c=D + 1))
                ts(p_n[:, :, :], num[:, :, :, D], M * 1e-6, None, ALU.add).then_inc(p_den.sem, 1)
                wait(e, p_den, g, 1)
                e.reciprocal(p_r[:, :, :], p_n[:, :, :]).then_inc(p_rec.sem, 1)
                wait(e, p_rec, g, 1)
                wait(e, p_xbs, g, 1)
                wait(e, gT, g, 1)
                for b in range(GB):
                    tt(xn[:, b, 0:C].rearrange("p (n d) -> p n d", n=H), num[:, b, :, 0:D],
                       p_r[:, b, :].unsqueeze(2).to_broadcast([P, H, D]), ALU.mult).then_inc(p_att.sem, 1)
                wait(e, p_att, g, GB)
                e.tensor_copy(xn[:, :, C:C + CR], xn[:, :, P:C]).then_inc(p_dup.sem, 1)
                yield
                lo_parts(g, 1)
                yield
                wait(e, p_xbs, g, 1)
                for j in range(2):
                    wait(e, p_pr, g, j + 1)
                    stt(out=p_y[:, 2 * j:2 * j + 2, :], in0=bank(ROT[j], P, 0, 2 * C).rearrange("p (b c) -> p b c", b=2),
                        scalar=1 / WS, in1=p_xb[:, 2 * j:2 * j + 2, :], op0=ALU.mult, op1=ALU.add).then_inc(p_ys.sem, 1)
                yield
                moments(g, 1, p_y, lambda b: wait(e, p_ys, g, b // 2 + 1))
                yield
                apply(g, 1, p_y)
                yield
                wait(e, ln_norm, g, 2 * GB)
                tt(p_y[:, :, :], xn[:, :, 0:C], bc[:, R_AG, :].unsqueeze(1).to_broadcast([P, GB, C]), ALU.mult).then_inc(p_g.sem, 1)
                wait(e, p_g, g, 1)
                wait(e, p_be, g, 1)
                tt(hg, hg, p_y[:, :, :], ALU.add).then_inc(p_h.sem, 1)
                yield
                moments(g, 2, hg, lambda b: wait(e, p_h, g, 1))
                yield
                apply(g, 2, hg)
                duplicate(g, 1)
                yield
                wait(e, g_hi, g, 6)
                if g == 0:
                    e.wait_ge(d_moe, 16 * 4)
                e.reduce_sum(m_ma[:, :], bank(3).rearrange("p (b t) -> p b t", b=GB), AX.X).then_inc(m_mean.sem, 1)
                e.reduce_sum(m_mr[:, :], bank(4, CR).rearrange("p (b t) -> p b t", b=GB), AX.X).then_inc(m_mean.sem, 1)
                wait(e, m_mean, g, 2)
                for o, a, wg, r in ((m_pa, m_ma, wg_a, P), (m_pr, m_mr, wg_r, CR)):
                    tt(o[:, :, :], a[:, :].unsqueeze(2).to_broadcast([r, GB, E]), wg[:, :].unsqueeze(1).to_broadcast([r, GB, E]),
                       ALU.mult).then_inc(m_prod.sem, 1)
                lo_parts(g, 2)
                yield
                wait(e, m_log, g, 1)
                ts(m_l[:, :, :], bank(5, P, 0, GB * E).rearrange("p (b x) -> p b x", b=GB), 1.0 / T, None, ALU.mult).then_inc(m_st.sem, 1)
                wait(e, m_st, g, 1)
                e.reduce_max(m_mx[:, :], m_l[:, :, :], AX.X).then_inc(m_st.sem, 1)
                wait(e, m_st, g, 2)
                tt(m_ls[:, :, :], m_l[:, :, :], m_mx[:, :].unsqueeze(2).to_broadcast([P, GB, E]), ALU.subtract).then_inc(m_st.sem, 1)
                wait(e, m_st, g, 3)
                ts(m_eq[:, :, :], m_ls[:, :, :], 0.0, None, ALU.is_equal).then_inc(m_st.sem, 1)
                wait(e, m_st, g, 4)
                ts(m_t[:, 0, :], m_eq[:, :, 0], -1.0, 1.0, ALU.mult, ALU.add).then_inc(m_st.sem, 1)
                ts(m_t[:, 1, :], m_eq[:, :, 1], -1.0, 2.0, ALU.mult, ALU.add).then_inc(m_st.sem, 1)
                wait(e, m_st, g, 6)
                tt(m_idx[:, :], m_t[:, 0, :], m_t[:, 1, :], ALU.mult).then_inc(m_st.sem, 1)
                yield
                wait(e, m_ex, g, 1)
                e.reduce_sum(m_sum[:, :], m_e[:, :, :], AX.X).then_inc(m_st.sem, 1)
                wait(e, m_st, g, 8)
                e.reciprocal(m_w[:, :], m_sum[:, :]).then_inc(m_st.sem, 1)
                yield
                for b in range(GB):
                    wait(e, m_st, g, 9)
                    wait(e, m_dn, g, b + 1)
                    stt(out=h[:, g % 3, b, :], in0=bank(5, P, 0, C), scalar=m_w[:, b:b + 1], in1=h[:, g % 3, b, :],
                        op0=ALU.mult, op1=ALU.add).then_inc(m_res.sem, 1)
                    yield
                moments(g, 3, hg, lambda b: wait(e, m_res, g, b + 1))
                yield
                apply(g, 3, hg)
                duplicate(g, 2)
                yield
                wait(e, g_hi, g, 8)
                again(e, s_wxs, g, NT)
                e.tensor_copy(s_x[:, 0, :], bank(3)).then_inc(s_xc.sem, 1)
                e.tensor_copy(s_x[:, 1, :], bank(4)).then_inc(s_xc.sem, 1)
                lo_parts(g, 3)
                yield
                for s in range(2):
                    wait(e, s_dps, g, s + 1)
                    ts(s_z[:, s, :], bank((5, 3)[s]), 1.0 / WS, dbias[:, s:s + 1], ALU.mult, ALU.add).then_inc(s_zs.sem, 1)
                yield
                wait(e, s_ln, g, 1)
                wait(e, s_zs, g, 2)
                again(e, s_as, g, NT)
                stt(out=s_dt[:, :, :], in0=s_z[:, :, :], scalar=0.0, in1=s_u[:, :, :], op0=ALU.max, op1=ALU.add).then_inc(s_dlt.sem, 1)
                yield

            def tile_bx(g, i):
                wait(e, s_bps, g, i + 1)
                wait(e, s_wxs, g, i + 1)
                w = s_w[:, i % NW, :]
                stt(out=w, in0=bank(scan_bank(g, i, 0)), scalar=ra_all[:, i:i + 1], in1=w, op0=ALU.mult, op1=ALU.mult).then_inc(s_bx.sem, 1)

            def tile_scan(g, i):
                wait(e, s_bx, g, i + 1)
                wait(e, s_a0, g, i + 1)
                if i >= NH:
                    wait(e, s_sum, g, i - NH + 1)
                else:
                    again(e, s_sum, g, NT)
                e.tensor_tensor_scan(s_h[:, i % NH, :], s_a[:, i % NA_, :], s_w[:, i % NW, :], 0.0, ALU.mult, ALU.add).then_inc(s_hs.sem, 1)

            def tile_product(g, k):
                wait(e, s_hs, g, k + 1)
                wait(e, s_cps, g, k + 1)
                st = s_h[:, k % NH, :]
                stt(out=st, in0=bank(scan_bank(g, k, 1)), scalar=1.0 / WS, in1=st, op0=ALU.mult, op1=ALU.mult).then_inc(s_pr.sem, 1)

            def scan_step(g, slot):
                hg = h[:, g % 3, :, :]
                i, second = divmod(slot, 2)
                tail = slot - 2 * NT
                if i < NT and not second:
                    tile_bx(g, i)
                    tile_scan(g, i)
                elif i < NT:
                    tile_product(g, i)
                elif tail == 0:
                    for j in range(2):
                        wait(e, s_yT, g, j + 1)
                        tt(hg[:, 2 * j:2 * j + 2, :], hg[:, 2 * j:2 * j + 2, :],
                           bank(6 + j, P, 0, 2 * C).rearrange("p (b c) -> p b c", b=2), ALU.add).then_inc(s_res.sem, 1)
                elif tail == 1:
                    ln_moments(g, 0, hg, kn_st, kn_mv, kn_stats, kn_aggr, lambda b: wait(e, s_res, g, b // 2 + 1))
                elif tail == 2:
                    ln_apply(g, 0, k_xn, hg, kn_mv, kn_rs, kn_aggr, kn_rstd, kn_norm)
                elif tail == 3:
                    wait(e, kT, g, 1)
                    e.tensor_copy(k_xr[:, :], bank(7, CR)).then_inc(kTr.sem, 1)
                elif tail == 5:
                    for j in range(2):
                        wait(e, f_dn, g, j + 1)
                        tt(k_y[:, 2 * j:2 * j + 2, :], bank((7, 6)[j], P, 0, 2 * C).rearrange("p (b c) -> p b c", b=2),
                           bc[:, R_FBO, :].unsqueeze(1).to_broadcast([P, 2, C]), ALU.add).then_inc(f_b.sem, 1)
                elif tail == 6:
                    ln_moments(g, 1, k_y, kn_st, kn_mv, kn_stats, kn_aggr, lambda b: wait(e, f_b, g, b // 2 + 1))
                elif tail == 7:
                    ln_apply(g, 1, k_xn, k_y, kn_mv, kn_rs, kn_aggr, kn_rstd, kn_norm)
                elif tail == 8:
                    wait(e, kn_norm, g, 2 * GB)
                    tt(k_y[:, :, :], k_xn[:, :, :], bc[:, R_FG, :].unsqueeze(1).to_broadcast([P, GB, C]), ALU.mult).then_inc(f_g.sem, 1)
                    wait(e, f_g, g, 1)
                    wait(e, f_be, g, 1)
                    tt(k_y[:, :, :], hg, k_y[:, :, :], ALU.add).then_inc(f_out.sem, 1)

            def scan(g):
                for slot in range(S_SEGS):
                    scan_step(g, slot)
                    yield

            def setup(s):
                for c in SETUP[s]:
                    split_chunk(c)
                    yield

            split_chunk(0)
            program(attention, middle, scan, setup)


def kernel(**inputs):
    import numpy as np
    import concourse.bacc as _bacc
    from concourse import mybir as _mybir
    from concourse.bass_utils import run_bass_kernel_spmd as _run

    a = {n: np.asarray(v) for n, v in inputs.items()}

    def lay(w):
        return np.stack([w[..., :P, :], np.concatenate([w[..., P:, :], w[..., P:, :]], axis=-2)], axis=-2)

    x_t = a['x'].reshape(NB, P, W, C).transpose(0, 3, 2, 1).reshape(NB, C, NRAW)
    wq = a['L0_attn_W_qkv']
    att1 = [wq[:, C * s + 64 * t:C * s + 64 * t + 64] for s in range(2) for t in range(3) for _ in range(2)]

    def scan_tiles(w):
        w = w.reshape(C, N, C)
        return np.concatenate([w[:P].transpose(1, 0, 2),
                               w[P:].reshape(CR, N2, 2, C).transpose(1, 2, 0, 3).reshape(N2, P, C)], axis=0)

    wd = a['L1_attn_W_delta']
    tiles = np.concatenate([scan_tiles(a['L1_attn_W_B']), scan_tiles(a['L1_attn_W_C']), wd[None, :P],
                            np.concatenate([wd[P:], wd[P:]])[None]])
    w_scan = tiles.reshape(NS // SC, SC, P, C).transpose(0, 3, 1, 2).reshape(NS // SC, C, SC * P)
    A = a['L1_attn_A']
    tw = a['L0_tok_Wqkv']
    tb = a['L0_tok_bqkv'].reshape(3, C)
    ins = {
        'x_t': lay(x_t),
        'w_att0': lay(np.concatenate([tw[:, :P], tw[:, C:C + P], tw[:, P:C], tw[:, C + P:]], axis=1)),
        'w_att1': lay(np.concatenate(att1 + [wq[:, 2 * C:], a['L0_attn_W_proj']], axis=1)),
        'w_exp': lay(a['L0_ffn_W1']),
        'b_exp': a['L0_ffn_b1'],
        'w_scan': lay(w_scan),
        'tproj': a['L0_tok_Wproj'].reshape(HP, 2, D, C).transpose(0, 2, 1, 3).reshape(HP * D, 2, C),
        'tbq': tb[0:2].T,
        'tbv': tb[2].reshape(HP, 2, D).transpose(0, 2, 1).reshape(HP * D, 2),
        'rows': np.stack([a[n] for n in ('L0_tok_bproj', 'L0_attn_b_proj', 'L0_attn_gamma', 'L0_attn_beta',
                                         'L1_ffn_bo', 'L1_ffn_gamma', 'L1_ffn_beta')])[None],
        'rf': np.concatenate([a['L0_attn_random_features'].T] * 4),
        'wg': a['L0_ffn_Wg'].T,
        'w2': a['L0_ffn_W2'].reshape(E, FT, P, C).transpose(2, 0, 1, 3).reshape(P, E * FT * C),
        'b2': a['L0_ffn_b2'].reshape(1, E * C),
        'a': np.concatenate([A[:P], A[P:].reshape(CR, N2, 2).transpose(2, 0, 1).reshape(P, N2)], axis=1),
        'dbias': np.stack([a['L1_attn_delta_bias'][:P], np.concatenate([a['L1_attn_delta_bias'][P:]] * 2)], axis=1),
        'fw1': a['L1_ffn_W1'].T,
        'fw2': a['L1_ffn_W2'],
        'fwo': a['L1_ffn_Wo'].T,
        'fb': np.stack([np.concatenate([a['L1_ffn_b1'], a['L1_ffn_b1'][:CR]]), a['L1_ffn_b2']], axis=1),
    }
    nc = _bacc.Bacc("TRN2", target_bir_lowering=False, num_devices=1)
    arrays, args = {}, []
    for name, v in ins.items():
        v = np.ascontiguousarray(v)
        arrays[f"in_{name}_dram"] = v
        args.append(nc.dram_tensor(f"in_{name}_dram", v.shape, _mybir.dt.from_np(v.dtype), kind="ExternalInput").ap())
    args.append(nc.dram_tensor("out_0_dram", (NB, T, C), _mybir.dt.float32, kind="ExternalOutput").ap())
    tower(nc, *args)
    r = _run(nc, [arrays], core_ids=[0])
    return r.results[0]["out_0_dram"]
```
